# Optimizing a Trainium2 kernel written in Bass

```python
import numpy as np
import jax
import jax.numpy as jnp

def _softmax(x, axis=-1):
    return jax.nn.softmax(x, axis=axis)

def _gelu(x):
    return jax.nn.gelu(x, approximate=True)

def _silu(x):
    return jax.nn.silu(x)

def _sigmoid(x):
    return jax.nn.sigmoid(x)

def _layernorm(x, axis=-1, eps=1e-05):
    m = jnp.mean(x, axis=axis, keepdims=True)
    v = jnp.var(x, axis=axis, keepdims=True)
    return (x - m) / jnp.sqrt(v + eps)

def _scatter_add(tgt, idx, src, axis=0):
    return tgt.at[idx].add(src)

def _segment_sum(src, seg, n):
    return jax.ops.segment_sum(src, seg, n)
kernel_name = 'mk_flamingo_gated_d1_seqx_r4_1c551d'

def setup_inputs(seed: int=0):
    np.random.seed(seed)
    _w = jnp.asarray

    def _rec_inputs():
        import jax
        import jax.numpy as jnp
        _rk = jax.random.key(seed)
        x = -7.109e-05 + 0.9999 * jax.random.normal(jax.random.fold_in(_rk, 1), (32, 128, 256), jnp.float32)
        _lenS = 128 - jax.random.randint(jax.random.fold_in(_rk, 7), (32,), 0, max(1, 128 // 4) + 1, jnp.int32)
        _lenS2 = 128 - jax.random.randint(jax.random.fold_in(_rk, 8), (32,), 0, max(1, 128 // 4) + 1, jnp.int32)
        _ctx_768P = jax.random.normal(jax.random.fold_in(_rk, 11), (32, 16, 192), jnp.float32)
        _ctx_768c = jax.random.dirichlet(jax.random.fold_in(_rk, 511), 0.3 * jnp.ones((16,), jnp.float32), (32, 128))
        _ctx_768t = jnp.einsum('bsk,bkd->bsd', _ctx_768c, _ctx_768P)
        _ctx_768t = _ctx_768t * jax.lax.rsqrt(jnp.mean(jnp.square(_ctx_768t)) + 1e-12) * 0.953939
        ctx_768 = 0.000486113 + 1.00014 * (_ctx_768t + 0.3 * jax.random.normal(jax.random.fold_in(_rk, 611), (32, 128, 192), jnp.float32))
        _g = jax.random.normal(jax.random.fold_in(_rk, 9001), (2, 1), jnp.float32)
        _g = jnp.sign(_g) * jnp.maximum(jnp.abs(_g), 1.0) + (_g == 0) * 1.0
        g_xattn = _g[0]
        g_ffn = _g[1]
        return (x, ctx_768, g_xattn, g_ffn)
    x, ctx_768, g_xattn, g_ffn = _rec_inputs()

    def _L0_xattn_setup():
        import jax, jax.numpy as jnp
        import numpy as np
        HEADS = 16
        DIM_HEAD = 64
        key = jax.random.key(seed)
        ks = jax.random.split(key, 8)
        B, S, D = (16, 1024, 256)
        K, DE = (77, 192)
        inner = HEADS * DIM_HEAD
        hidden_states = jax.random.normal(ks[0], (B, S, D), dtype=jnp.float32)
        encoder_hidden_states = jax.random.normal(ks[1], (B, K, DE), dtype=jnp.float32)
        sc_q = 1.0 / np.sqrt(D)
        sc_kv = 1.0 / np.sqrt(DE)
        sc_o = 1.0 / np.sqrt(inner)
        Wq = jax.random.normal(ks[2], (D, inner), dtype=jnp.float32) * sc_q
        Wk = jax.random.normal(ks[3], (DE, inner), dtype=jnp.float32) * sc_kv
        Wv = jax.random.normal(ks[4], (DE, inner), dtype=jnp.float32) * sc_kv
        Wo = jax.random.normal(ks[5], (inner, D), dtype=jnp.float32) * sc_o
        bo = jax.random.normal(ks[6], (D,), dtype=jnp.float32) * 0.01
        return {'hidden_states': hidden_states, 'encoder_hidden_states': encoder_hidden_states, 'Wq': Wq, 'Wk': Wk, 'Wv': Wv, 'Wo': Wo, 'bo': bo}
    _L0_xattn_all = _L0_xattn_setup()
    _L0_xattn_in = {k: v for k, v in _L0_xattn_all.items() if k in ('Wq', 'Wk', 'Wv', 'Wo', 'bo')}
    del _L0_xattn_all

    def _L0_ffn_setup():
        import jax, jax.numpy as jnp
        import numpy as np
        E = 8
        K = 2
        D = 256
        H = 1024
        CAP_FACTOR = 1.0
        key = jax.random.key(seed)
        ks = jax.random.split(key, 5)
        x = jax.random.normal(ks[0], (4, 512, D), jnp.float32)
        gate_w = jax.random.normal(ks[1], (E, D), jnp.float32) * 0.02
        fc1_w = jax.random.normal(ks[2], (E, H, D), jnp.float32) * 0.02
        fc1_b = jnp.zeros((E, 1, H), jnp.float32)
        fc2_w = jax.random.normal(ks[3], (E, H, D), jnp.float32) * 0.02
        fc2_b = jnp.zeros((E, 1, D), jnp.float32)
        return {'x': x, 'gate_w': gate_w, 'fc1_w': fc1_w, 'fc1_b': fc1_b, 'fc2_w': fc2_w, 'fc2_b': fc2_b}
    _L0_ffn_all = _L0_ffn_setup()
    _L0_ffn_in = {k: v for k, v in _L0_ffn_all.items() if k in ('gate_w', 'fc1_w', 'fc1_b', 'fc2_w', 'fc2_b')}
    del _L0_ffn_all
    return {'x': x, 'ctx_768': ctx_768, 'g_xattn': g_xattn, 'g_ffn': g_ffn, 'L0_xattn_Wq': _L0_xattn_in['Wq'], 'L0_xattn_Wk': _L0_xattn_in['Wk'], 'L0_xattn_Wv': _L0_xattn_in['Wv'], 'L0_xattn_Wo': _L0_xattn_in['Wo'], 'L0_xattn_bo': _L0_xattn_in['bo'], 'L0_ffn_gate_w': _L0_ffn_in['gate_w'], 'L0_ffn_fc1_w': _L0_ffn_in['fc1_w'], 'L0_ffn_fc1_b': _L0_ffn_in['fc1_b'], 'L0_ffn_fc2_w': _L0_ffn_in['fc2_w'], 'L0_ffn_fc2_b': _L0_ffn_in['fc2_b']}

def reference(x, ctx_768, g_xattn, g_ffn, L0_xattn_Wq, L0_xattn_Wk, L0_xattn_Wv, L0_xattn_Wo, L0_xattn_bo, L0_ffn_gate_w, L0_ffn_fc1_w, L0_ffn_fc1_b, L0_ffn_fc2_w, L0_ffn_fc2_b):
    import jax
    import jax.numpy as jnp

    def _L0_xattn_ref(hidden_states, encoder_hidden_states, Wq, Wk, Wv, Wo, bo):
        import jax, jax.numpy as jnp
        import numpy as np
        HEADS = 16
        DIM_HEAD = 64
        B, S, D = hidden_states.shape
        K = encoder_hidden_states.shape[1]
        H, Dh = (HEADS, DIM_HEAD)
        scale = 1.0 / np.sqrt(Dh)
        q = hidden_states @ Wq
        k = encoder_hidden_states @ Wk
        v = encoder_hidden_states @ Wv
        q = q.reshape(B, S, H, Dh).transpose(0, 2, 1, 3)
        k = k.reshape(B, K, H, Dh).transpose(0, 2, 1, 3)
        v = v.reshape(B, K, H, Dh).transpose(0, 2, 1, 3)
        scores = jnp.einsum('bhsd,bhkd->bhsk', q, k) * scale
        probs = jax.nn.softmax(scores, axis=-1)
        out = jnp.einsum('bhsk,bhkd->bhsd', probs, v)
        out = out.transpose(0, 2, 1, 3).reshape(B, S, H * Dh)
        out = out @ Wo + bo
        return out

    def _L0_ffn_ref(x, gate_w, fc1_w, fc1_b, fc2_w, fc2_b):
        import jax, jax.numpy as jnp
        import numpy as np
        E = 8
        K = 2
        D = 256
        H = 1024
        CAP_FACTOR = 1.0
        B, S, Dm = x.shape
        xf = x.reshape(-1, Dm)
        N = xf.shape[0]
        cap = int(K * CAP_FACTOR * ((N + E - 1) // E))
        logits = xf @ gate_w.T
        scores = jax.nn.softmax(logits, axis=-1)
        topv, topi = jax.lax.top_k(scores, K)
        gates = topv / jnp.sum(topv, axis=-1, keepdims=True)
        offset = jnp.zeros((E,), jnp.int32)
        locs = []
        for j in range(K):
            mask = jax.nn.one_hot(topi[:, j], E, dtype=jnp.int32)
            loc_in = jnp.cumsum(mask, axis=0) - 1 + offset[None, :]
            locs.append(jnp.take_along_axis(loc_in, topi[:, j:j + 1], axis=1)[:, 0])
            offset = offset + mask.sum(axis=0)
        loc = jnp.stack(locs, axis=1)
        valid = loc < cap
        flat_idx = jnp.where(valid, topi * cap + loc, 0)
        w = valid.astype(xf.dtype)
        disp = jnp.zeros((E * cap, Dm), xf.dtype)
        disp = disp.at[flat_idx.reshape(-1)].add((xf[:, None, :] * w[:, :, None]).reshape(-1, Dm))
        de = disp.reshape(E, cap, Dm)
        h = jax.nn.relu(jnp.einsum('ecd,ehd->ech', de, fc1_w) + fc1_b)
        eo = jnp.einsum('ech,ehd->ecd', h, fc2_w) + fc2_b
        gathered = eo.reshape(E * cap, Dm)[flat_idx]
        out = jnp.sum(gathered * (gates * w)[:, :, None], axis=1)
        return out.reshape(B, S, Dm)
    x = x + jnp.tanh(g_xattn[0]) * _L0_xattn_ref(_layernorm(x, axis=-1), ctx_768, L0_xattn_Wq, L0_xattn_Wk, L0_xattn_Wv, L0_xattn_Wo, L0_xattn_bo)
    x = x + jnp.tanh(g_ffn[0]) * _L0_ffn_ref(_layernorm(x, axis=-1), L0_ffn_gate_w, L0_ffn_fc1_w, L0_ffn_fc1_b, L0_ffn_fc2_w, L0_ffn_fc2_b)
    return x

_drawn_inputs = setup_inputs


def setup_inputs(seed=0):
    import zlib

    import numpy as np

    out = dict(_drawn_inputs(seed))
    spreads = {'L0_ffn_fc1_b': (0.0, 0.301), 'L0_ffn_fc2_b': (0.0, 0.1)}
    factors = {'L0_xattn_bo': 4.798}
    for name, (base, spread) in spreads.items():
        noise = np.random.default_rng([zlib.crc32(name.encode()), seed]).standard_normal(out[name].shape)
        drawn = base * np.exp(spread * noise) if base else spread * noise
        out[name] = jnp.asarray(drawn.astype(out[name].dtype))
    for name, factor in factors.items():
        out[name] = (out[name] * factor).astype(out[name].dtype)
    return out
```

```python
import concourse.bass as bass
from concourse import mybir
from contextlib import ExitStack

P = 128
B, S, D, DE = 32, 128, 256, 192
HEADS, DH = 16, 64
INNER = HEADS * DH
E, H = 8, 1024
N = B * S
CAP = 2 * ((N + E - 1) // E)
EPS = 1e-5
SCALE = 1.0 / 8.0

GB = 4
NG = B // GB
TOK = GB * S
NP = HEADS // 2
DK = D // P
HALF = INNER // 2
R2 = DE - P
HK = H // P
NHI = E * CAP // P
EH = CAP // P
NSG = E * CAP // TOK
PAD = P
BIG = 65536.0


def pass_gate(eng, sem):
    eng.sem_inc(sem, 1)


class Steps:

    def __init__(self, eng, sem):
        self.eng, self.sem, self.base, self.n = eng, sem, 0, 0

    def mark(self, ins):
        ins.then_inc(self.sem, 1)
        self.n += 1
        return self.n

    def after(self, n=None):
        self.eng.wait_ge(self.sem, self.base + (self.n if n is None else n))

    def enter(self, base):
        self.base, self.n = base, 0


MISC_PREV = {1: ["O0", "O1"], 2: ["XA", "XB"], 3: ["LG"], 4: ["PR"], 7: ["T0", "T1"]}


def jobs_of(has_prev, has_cur):
    out = []
    for j in range(NP):
        if has_cur:
            out += [("Q", j), ("K", j)] + [("FA", 0), ("FB", 0)] * (j == NP - 1) + [("V", j)]
        if has_prev:
            out += [(m, 0) for m in MISC_PREV.get(j, [])]
    return out


def gated_block(nc, x, ctxT, g_x, g_f, wq, wk, wv, wo, bo, gateT, fc1T, fc1b, fc2, fc2b, out):
    f32 = mybir.dt.float32

    xn2_dram = nc.dram_tensor("xn2_rows", [N + PAD, D], f32, kind="Internal").ap()
    acc_dram = nc.dram_tensor("acc_rows", [N + PAD, D], f32, kind="Internal").ap()
    x_v = x.rearrange("b p d -> p b d")
    acc_v = acc_dram[0:N, :].rearrange("(b p) d -> p b d", p=P)
    xn2_v = xn2_dram[0:N, :].rearrange("(b p) d -> p b d", p=P)

    with ExitStack() as keep:
        def sem(name):
            return keep.enter_context(nc.semaphore(name))

        table = keep.enter_context(nc.sbuf_tensor("table", [P, 2, 2, NHI], f32))
        running = keep.enter_context(nc.sbuf_tensor("running", [P, 2, GB + 1, E], f32))
        tanh_g = keep.enter_context(nc.sbuf_tensor("tanh_g", [P, 2], f32))

        with ExitStack() as ctx:
            attention(nc, ctx, sem, x_v, acc_v, xn2_v, acc_dram, xn2_dram, ctxT, g_x, g_f, wq, wk, wv, wo, bo, gateT,
                      table, running, tanh_g)
        with ExitStack() as ctx:
            experts(nc, ctx, sem, acc_dram, xn2_dram, fc1T, fc1b, fc2, fc2b, out, table, running, tanh_g)


def attention(nc, ctx, sem, x_v, acc_v, xn2_v, acc_dram, xn2_dram, ctxT, g_x, g_f, wq, wk, wv, wo, bo, gateT,
              table, running, tanh_g):
    f32, f32r, i32, u32 = mybir.dt.float32, mybir.dt.float32r, mybir.dt.int32, mybir.dt.uint32
    ALU, ACT, AX = mybir.AluOpType, mybir.ActivationFunctionType, mybir.AxisListType.X

    def sb(name, shape, dt=f32):
        return ctx.enter_context(nc.sbuf_tensor(name, shape, dt))

    wq_h, wq_l = sb("wq_h", [P, DK, INNER], f32r), sb("wq_l", [P, DK, INNER], f32r)
    wo_h, wo_l = sb("wo_h", [P, NP, D], f32r), sb("wo_l", [P, NP, D], f32r)
    wk_h, wk_l, wk_d = (sb(n, [P, INNER], f32r) for n in ("wk_h", "wk_l", "wk_d"))
    wk_e = sb("wk_e", [R2, INNER], f32r)
    wv_h, wv_l, wv_d = (sb(n, [P, INNER], f32r) for n in ("wv_h", "wv_l", "wv_d"))
    wv_e = sb("wv_e", [R2, INNER], f32r)
    v_sb = sb("v_sb", [P, 2, GB, HALF])
    xT_h, xT_l = sb("xT_h", [P, DK, TOK], f32r), sb("xT_l", [P, DK, TOK], f32r)
    cv_h, cv_l, cv_d = (sb(n, [P, TOK], f32r) for n in ("cv_h", "cv_l", "cv_d"))
    ck_h, ck_l, ck_d = (sb(n, [P, TOK], f32r) for n in ("ck_h", "ck_l", "ck_d"))
    c_raw = sb("c_raw", [P, 2, TOK])
    c_tmp = sb("c_tmp", [P, TOK], f32r)
    work = sb("work", [P, 2 * 1024])
    probs = work[:, 0:1024].rearrange("p (s k) -> p s k", s=8)
    xn2T = work[:, 1024:2048].rearrange("p (k t) -> p k t", k=DK)
    onehot_lo = work[:, 1024:2048].rearrange("p (s k) -> p s k", s=8)
    rows = sb("rows", [P, 4, GB, D])
    xn, xr, x1, xn2 = (rows[:, n] for n in range(4))
    hi_vals = rows[:, 3].rearrange("p b (two c) -> p (b two) c", two=2)
    q_sb, k_sb = sb("q_sb", [P, TOK]), sb("k_sb", [P, TOK])
    pT = sb("pT", [P, 2, TOK])
    aT_h, aT_l = sb("aT_h", [P, NP, TOK], f32r), sb("aT_l", [P, NP, TOK], f32r)
    ident, tri, ones, iota = (sb(n, [P, P]) for n in ("ident", "tri", "ones", "iota"))
    bias_o = sb("bias_o", [P, D])
    gate_sb = sb("gate_sb", [P, DK, E])
    zrow = sb("zrow", [P, D])
    stats1, mv1, rstd1 = sb("stats1", [P, GB, 6]), sb("mv1", [P, GB, 2]), sb("rstd1", [P, GB])
    stats2, mv2, rstd2 = sb("stats2", [P, GB, 6]), sb("mv2", [P, GB, 2]), sb("rstd2", [P, GB])
    var1, var2, mhalf = sb("var1", [P, GB]), sb("var2", [P, GB]), sb("mhalf", [P, GB])
    negmax = sb("negmax", [P, 2, 8])
    sums = sb("sums", [P, 2, 8])
    rsum = sb("rsum", [P, 8])
    logits, top, topi = sb("logits", [P, GB, E]), sb("top", [P, GB, E]), sb("topi", [P, GB, E], u32)
    choice = sb("choice", [P, 2, GB])
    mask = sb("mask", [P, 2, GB, E])
    gates, gdiff, gexp, gden = sb("gates", [P, 2, GB]), sb("gdiff", [P, GB]), sb("gexp", [P, GB]), sb("gden", [P, GB])
    place, loc, late, slot = sb("place", [P, 2, GB, E]), sb("loc", [P, 2, GB]), sb("late", [P, 2, GB]), sb("slot", [P, 2, GB])
    ranks = sb("ranks", [P, 2 * 2 * GB * E])
    sloti, hl_i = sb("sloti", [P, 2, GB], i32), sb("hl_i", [P, 2, 2, GB], i32)
    hl = sb("hl", [P, 2, 2, GB])
    token = sb("token", [P, GB])
    lower_half = sb("lower_half", [P, 1])

    def ps(name):
        return ctx.enter_context(nc.psum_tensor(name, [P, TOK], f32))

    proj = [ps("proj0"), ps("proj1")]
    score = [ps("score0"), ps("score1")]
    probT = [ps("probT0"), ps("probT1")]
    av = [ps("av0"), ps("av1")]

    (
        s_consts, s_w_in, s_wq_in, s_wo_in, s_c_in, s_x_in, s_xr_in, s_small_in, s_zeros_out, s_w_hi,
        s_w_lo, s_tanh, s_bias_o, s_zrow, s_q_ready, s_k_ready, s_v_ready, s_s_ready, s_pt_ready,
        s_av_ready, s_o_ready, s_xt_ready, s_lg_ready, s_pr_ready, s_tb_ready, s_f_ready, s_at_hi,
        s_f_hi, s_q_done, s_k_done, s_v_done, s_pt_done0, s_pt_done1, s_at_split, s_f_split, s_negmax,
        s_exp, s_p_ready, s_o_done, s_xt_done, s_lg_done, s_pr_done, s_tb_done, s_stats1,
        s_rstd1, s_xn_ready, s_stats2, s_rstd2, s_xn2_ready, s_mask_ready, s_gdiff, s_gexp,
        s_slot_ready, s_onehot, s_cv_ready, s_ck_ready, s_xr_ready, s_x1_out, s_xn2_out, s_act_self,
        s_dve_self, s_pool_self, s_dve_gate, s_pool_gate,
    ) = (sem("a_" + name) for name in (
        "consts", "w_in", "wq_in", "wo_in", "c_in", "x_in", "xr_in", "small_in", "zeros_out", "w_hi",
        "w_lo", "tanh", "bias_o", "zrow", "q_ready", "k_ready", "v_ready", "s_ready", "pt_ready",
        "av_ready", "o_ready", "xt_ready", "lg_ready", "pr_ready", "tb_ready", "f_ready", "at_hi",
        "f_hi", "q_done", "k_done", "v_done", "pt_done0", "pt_done1", "at_split", "f_split", "negmax",
        "exp", "p_ready", "o_done", "xt_done", "lg_done", "pr_done", "tb_done", "stats1",
        "rstd1", "xn_ready", "stats2", "rstd2", "xn2_ready", "mask_ready", "gdiff", "gexp",
        "slot_ready", "onehot", "cv_ready", "ck_ready", "xr_ready", "x1_out", "xn2_out", "act_self",
        "dve_self", "pool_self", "dve_gate", "pool_gate",
    ))

    def done(job, g):
        kind, j = job
        return {
            "Q": (s_q_done, 8 * g + j + 1), "K": (s_k_done, 8 * g + j + 1), "V": (s_v_done, 8 * g + j + GB + 1),
            "O0": (s_o_done, 2 * g - 1), "O1": (s_o_done, 2 * g), "XA": (s_xt_done, 2 * g - 1), "XB": (s_xt_done, 2 * g),
            "LG": (s_lg_done, g), "PR": (s_pr_done, g), "T0": (s_tb_done, 2 * g + 1), "T1": (s_tb_done, 2 * g + 2),
            "FA": (s_f_split, 2 * g + 3), "FB": (s_f_split, 2 * g + 4),
        }[kind]

    def bank_of(job, jobs):
        return proj[jobs.index(job) % 2]

    block = ctx.enter_context(nc.Block())

    @block.sync
    def _(sp):
        def load_x(g, dst, done_sem):
            sp.dma_start(rows[:, dst], x_v[:, bass.ds(g * GB, GB), :]).then_inc(done_sem, 16)

        def load_ctx(g):
            cols = bass.ds(g * TOK, TOK)
            sp.dma_start(c_raw[:, 0, :], ctxT[0:P, cols]).then_inc(s_c_in, 16)
            sp.dma_start(c_raw[0:R2, 1, :], ctxT[P:DE, cols]).then_inc(s_c_in, 16)
            sp.dma_start(c_raw[R2:P, 1, :], ctxT[P:DE, cols]).then_inc(s_c_in, 16)

        load_x(0, 0, s_x_in)
        load_ctx(0)
        stage = [work[:, :], rows[:, 2:4].rearrange("p a b d -> p (a b d)")]

        def load_kv(w, dst):
            sp.dma_start(dst[:, 0:INNER], w[0:P, :]).then_inc(s_w_in, 16)
            sp.dma_start(dst[0:R2, INNER:2 * INNER], w[P:DE, :]).then_inc(s_w_in, 16)
            sp.dma_start(dst[R2:P, INNER:2 * INNER], w[P:DE, :]).then_inc(s_w_in, 16)

        load_kv(wv, stage[0])
        load_kv(wk, stage[1])
        for k, (src, n) in enumerate(((g_x, 0), (g_f, 1))):
            sp.dma_start(tanh_g[:, n:n + 1], src.rearrange("(o n) -> o n", o=1).to_broadcast([P, 1])).then_inc(s_small_in, 16)
        sp.dma_start(bias_o[:, :], bo.rearrange("(o n) -> o n", o=1).to_broadcast([P, D])).then_inc(s_small_in, 16)
        sp.dma_start(gate_sb[:, :, :], gateT.rearrange("(k p) e -> p k e", p=P)).then_inc(s_small_in, 16)
        sp.wait_ge(s_w_lo, 1)
        sp.dma_start(stage[0].rearrange("p (k n) -> p k n", k=DK), wq.rearrange("(k p) n -> p k n", p=P)).then_inc(s_wq_in, 16)
        sp.wait_ge(s_w_lo, 2)
        sp.dma_start(stage[1].rearrange("p (j n) -> p j n", j=NP), wo.rearrange("(j p) n -> p j n", p=P)).then_inc(s_wo_in, 16)
        sp.wait_ge(s_zrow, 1)
        for rows_dram in (xn2_dram, acc_dram):
            sp.dma_start(rows_dram[N:N + PAD, :], zrow[:, :]).then_inc(s_zeros_out, 16)

        def iteration(g, nxt, has_prev, has_cur):
            if has_cur:
                sp.wait_ge(s_f_ready, 2 * g + 2)
                load_x(nxt, 0, s_x_in)
                sp.wait_ge(s_cv_ready, g + 1)
                load_ctx(nxt)
            if has_prev:
                sp.wait_ge(s_w_lo, 4) if isinstance(g, int) else None
                if not isinstance(g, int) or g > 1:
                    sp.wait_ge(s_o_done, 2 * g - 2)
                load_x(g - 1, 1, s_xr_in)
                sp.wait_ge(s_stats2, g)
                sp.dma_start(acc_v[:, bass.ds((g - 1) * GB, GB), :], x1).then_inc(s_x1_out, 16)
                sp.wait_ge(s_xn2_ready, g)
                sp.dma_start(xn2_v[:, bass.ds((g - 1) * GB, GB), :], xn2).then_inc(s_xn2_out, 16)

        iteration(0, 1, False, True)
        iteration(1, 2, True, True)
        with sp.Fori(2, NG - 1) as g:
            iteration(g, g + 1, True, True)
        iteration(NG - 1, NG - 1, True, True)
        iteration(NG, None, True, False)
        sp.wait_ge(s_x1_out, 16 * NG)
        sp.wait_ge(s_xn2_out, 16 * NG)
        sp.wait_ge(s_zeros_out, 32)
        sp.wait_ge(s_x_in, 16 * (NG + 1))
        sp.wait_ge(s_c_in, 48 * (NG + 1))

    @block.gpsimd
    def _(pool):
        me = Steps(pool, s_pool_self)
        me.mark(nc.gpsimd.memset(ident[:, :], 0.0))
        me.mark(nc.gpsimd.memset(tri[:, :], 1.0))
        nc.gpsimd.memset(ones[:, :], 1.0)
        me.mark(nc.gpsimd.memset(lower_half[:, :], 0.0))
        nc.gpsimd.memset(mhalf[:, :], -0.5)
        nc.gpsimd.memset(running[:, :, :, :], 0.0)
        nc.gpsimd.memset(table[:, :, :, :], 0.0)
        nc.gpsimd.memset(zrow[:, :], 0.0).then_inc(s_zrow, 1)
        me.after()
        nc.gpsimd.affine_select(out=ident[:, :], in_=ident[:, :], compare_op=ALU.not_equal, fill=1.0, base=0,
                                pattern=[[-1, P]], channel_multiplier=1)
        nc.gpsimd.affine_select(out=tri[:, :], in_=tri[:, :], compare_op=ALU.is_gt, fill=0.0, base=0,
                                pattern=[[1, P]], channel_multiplier=-1)
        nc.gpsimd.affine_select(out=lower_half[:, :], in_=lower_half[:, :], compare_op=ALU.is_ge, fill=1.0, base=R2 - 1,
                                pattern=[[0, 1]], channel_multiplier=-1)
        nc.gpsimd.iota(iota[:, :], pattern=[[1, P]], base=0, channel_multiplier=0, allow_small_or_imprecise_dtypes=True)
        me.mark(nc.gpsimd.iota(token[:, :], pattern=[[P, GB]], base=1, channel_multiplier=1,
                               allow_small_or_imprecise_dtypes=True))
        me.after()
        nc.gpsimd.tensor_scalar(token[:, :], token[:, :], 0.0, None, ALU.add).then_inc(s_consts, 1)

        def copy(out_, in_):
            return nc.gpsimd.tensor_scalar(out_, in_, 1.0, 0.0, ALU.mult, ALU.add)

        def rstd(var_mv, var, r, ready, value, out_sem):
            pool.wait_ge(ready, value)
            pass_gate(pool, s_pool_gate)
            me.mark(nc.gpsimd.tensor_scalar(var[:, :], var_mv[:, :, 1], EPS, None, ALU.add))
            me.after()
            nc.gpsimd.tensor_tensor(r[:, :], var[:, :], mhalf[:, :], ALU.pow).then_inc(out_sem, 1)

        def split_cv(n):
            pool.wait_ge(s_c_in, 48 * (n + 1))
            pass_gate(pool, s_pool_gate)
            copy(cv_h[:, :], c_raw[:, 0, :])
            me.mark(copy(c_tmp[:, :], c_raw[:, 1, :]))
            me.after()
            nc.gpsimd.tensor_tensor(cv_l[:, :], c_raw[:, 0, :], cv_h[:, :].bitcast(f32), ALU.subtract)
            me.mark(nc.gpsimd.tensor_scalar(c_tmp[:, :], c_tmp[:, :].bitcast(f32), lower_half[:, 0:1], 0.0, ALU.mult, ALU.add))
            me.after()
            nc.gpsimd.tensor_tensor(cv_d[:, :], c_raw[:, 1, :], c_tmp[:, :].bitcast(f32),
                                    ALU.subtract).then_inc(s_cv_ready, 1)

        def copy_ck():
            pass_gate(pool, s_pool_gate)
            copy(ck_h[:, :], cv_h[:, :].bitcast(f32))
            copy(ck_l[:, :], cv_l[:, :].bitcast(f32))
            copy(ck_d[:, :], cv_d[:, :].bitcast(f32)).then_inc(s_ck_ready, 1)

        rstd(mv1, var1, rstd1, s_stats1, 1, s_rstd1)
        split_cv(0)
        pool.wait_ge(s_cv_ready, 1)
        copy_ck()

        def iteration(g, has_prev, has_cur):
            if has_prev:
                pool.wait_ge(s_xr_in, 16 * g)
                pool.wait_ge(s_bias_o, 1)
                for b in range(GB):
                    last = nc.gpsimd.tensor_tensor(xr[:, b, :], xr[:, b, :], bias_o[:, :], ALU.add)
                last.then_inc(s_xr_ready, 1)
                rstd(mv2, var2, rstd2, s_stats2, g, s_rstd2)
            if has_cur:
                rstd(mv1, var1, rstd1, s_stats1, g + 2, s_rstd1)
                pool.wait_ge(s_v_ready, 8 * g + 8)
                split_cv(g + 1)
            if has_prev:
                pool.wait_ge(s_slot_ready, g)
                pool.wait_ge(s_xn2_out, 16 * g)
                pass_gate(pool, s_pool_gate)
                for j in range(2):
                    for b in range(GB):
                        n = j * GB + b
                        nc.gpsimd.tensor_scalar(onehot_lo[:, n, :], iota[:, :], hl[:, 1, j, b:b + 1], None, ALU.is_equal)
                        nc.gpsimd.tensor_scalar(hi_vals[:, n, 0:NHI], iota[:, 0:NHI], hl[:, 0, j, b:b + 1],
                                                token[:, b:b + 1], ALU.is_equal, ALU.mult)
                        last = nc.gpsimd.tensor_scalar(hi_vals[:, n, NHI:2 * NHI], iota[:, 0:NHI], hl[:, 0, j, b:b + 1],
                                                       gates[:, j, b:b + 1], ALU.is_equal, ALU.mult)
                me.mark(last)
                me.after()
                pass_gate(pool, s_pool_gate)
                nc.gpsimd.tensor_scalar(token[:, :], token[:, :], float(TOK), None, ALU.add).then_inc(s_onehot, 1)
            if has_cur:
                pool.wait_ge(s_k_ready, 8 * g + 8)
                pool.wait_ge(s_cv_ready, g + 2)
                copy_ck()

        pool.wait_ge(s_consts, 1)
        iteration(0, False, True)
        start = me.n
        per = 5
        with pool.Fori(1, NG) as g:
            me.enter((g - 1) * per + start)
            iteration(g, True, True)
            assert me.n == per, me.n
        me.enter(start + (NG - 1) * per)
        iteration(NG, True, False)

    @block.tensor
    def _(pe):
        mm = nc.tensor.matmul
        pe.wait_ge(s_consts, 1)

        def take_bank(job, jobs, g):
            n = jobs.index(job)
            if n >= 2:
                pe.wait_ge(*done(jobs[n - 2], g))
            elif isinstance(g, int) and g == 0:
                pe.wait_ge(s_f_split, 1 + n)
            else:
                pe.wait_ge(s_tb_done, 2 * g - 1 + n)
            return proj[n % 2]

        def values(bank, b, half):
            cols, keys = slice(half * HALF, (half + 1) * HALF), slice(b * P, (b + 1) * P)
            mm(bank[:, :], cv_h[:, keys], wv_h[:, cols], start=True, stop=False)
            mm(bank[:, :], cv_h[:, keys], wv_l[:, cols], start=False, stop=False)
            mm(bank[:, :], cv_l[:, keys], wv_h[:, cols], start=False, stop=False)
            mm(bank[:, :], cv_d[:, keys], wv_d[:, cols], start=False, stop=False)
            mm(bank[:, :], cv_d[0:R2, keys], wv_e[:, cols], start=False, stop=True).then_inc(s_v_ready, 1)

        def front(bank, k):
            for b in range(GB):
                last = nc.tensor.transpose(bank[:, b * P:(b + 1) * P], xn[:, b, k * P:(k + 1) * P], ident[:, :])
            last.then_inc(s_f_ready, 1)

        def transpose_probs(u):
            for hh in range(2):
                pe.wait_ge(s_p_ready, 2 * u + hh + 1)
                if not isinstance(u, int) or u > 0:
                    pe.wait_ge((s_pt_done0, s_pt_done1)[hh], u)
                for b in range(GB):
                    last = nc.tensor.transpose(probT[hh][:, b * P:(b + 1) * P], probs[:, hh * GB + b, :], ident[:, :])
                last.then_inc(s_pt_ready, 1)

        def weigh_values(u, j, v_needed):
            pe.wait_ge(s_v_done, v_needed)
            if not isinstance(u, int) or u > 1:
                pe.wait_ge(s_at_split, u - 1)
            pe.wait_ge(s_pt_done0, u + 1)
            pe.wait_ge(s_pt_done1, u + 1)
            for b in range(GB):
                for hh in range(2):
                    cols = slice((j % 4) * P + hh * DH, (j % 4) * P + (hh + 1) * DH)
                    last = mm(av[j % 2][hh * DH:(hh + 1) * DH, b * P:(b + 1) * P], v_sb[:, j // 4, b, cols],
                              pT[:, hh, b * P:(b + 1) * P], start=True, stop=True)
            last.then_inc(s_av_ready, 1)

        def scores(u):
            pe.wait_ge(s_q_done, u + 1)
            pe.wait_ge(s_k_done, u + 1)
            if not isinstance(u, int) or u > 0:
                pe.wait_ge(s_exp, 2 * u)
            for b in range(GB):
                for hh in range(2):
                    r, t = slice(hh * DH, (hh + 1) * DH), slice(b * P, (b + 1) * P)
                    last = mm(score[hh][:, t], q_sb[r, t], k_sb[r, t], start=True, stop=True)
                    if b == GB - 1:
                        last.then_inc(s_s_ready, 1)

        def project_out(bank, g, b0):
            pe.wait_ge(s_at_split, 8 * g)
            for i in range(2):
                o, t = bank[:, i * D:(i + 1) * D], slice((b0 + i) * P, (b0 + i + 1) * P)
                for j in range(NP):
                    mm(o, aT_h[:, j, t], wo_h[:, j, :], start=(j == 0), stop=False)
                    mm(o, aT_h[:, j, t], wo_l[:, j, :], start=False, stop=False)
                    last = mm(o, aT_l[:, j, t], wo_h[:, j, :], start=False, stop=(j == NP - 1))
            last.then_inc(s_o_ready, 1)

        def misc(kind, bank, g):
            if kind in ("O0", "O1"):
                project_out(bank, g, 0 if kind == "O0" else 2)
            elif kind in ("XA", "XB"):
                pe.wait_ge(s_xn2_ready, g)
                k = 0 if kind == "XA" else 1
                for b in range(GB):
                    last = nc.tensor.transpose(bank[:, b * P:(b + 1) * P], xn2[:, b, k * P:(k + 1) * P], ident[:, :])
                last.then_inc(s_xt_ready, 1)
            elif kind == "LG":
                pe.wait_ge(s_xt_done, 2 * g)
                for b in range(GB):
                    for k in range(DK):
                        last = mm(bank[:, b * E:(b + 1) * E], xn2T[:, k, b * P:(b + 1) * P], gate_sb[:, k, :],
                                  start=(k == 0), stop=(k == DK - 1))
                last.then_inc(s_lg_ready, 1)
            elif kind == "PR":
                pe.wait_ge(s_mask_ready, g)
                flat = mask[:, :, :, :].rearrange("p j b e -> p (j b e)")
                mm(bank[:, 0:64], tri[:, :], flat, start=True, stop=True)
                mm(bank[:, 64:128], ones[:, :], flat, start=True, stop=True).then_inc(s_pr_ready, 1)
            elif kind in ("T0", "T1"):
                pe.wait_ge(s_onehot, g)
                j = int(kind[1])
                for b in range(GB):
                    last = mm(bank[:, 0:2 * NHI], onehot_lo[:, j * GB + b, :], hi_vals[:, j * GB + b, :],
                              start=(b == 0), stop=(b == GB - 1))
                last.then_inc(s_tb_ready, 1)
            else:
                if kind == "FA":
                    pe.wait_ge(s_xn_ready, g + 2)
                front(bank, 0 if kind == "FA" else 1)

        pe.wait_ge(s_w_lo, 1)
        pe.wait_ge(s_cv_ready, 1)
        for b in range(GB):
            if b >= 2:
                pe.wait_ge(s_v_done, b - 1)
            values(proj[b % 2], b, 0)
        pe.wait_ge(s_xn_ready, 1)
        for k in range(DK):
            pe.wait_ge(s_v_done, 3 + k)
            front(proj[k], k)

        def iteration(g, has_prev, has_cur):
            jobs = jobs_of(has_prev, has_cur)
            for j in range(NP):
                u = 8 * g + j
                if has_cur:
                    bank = take_bank(("Q", j), jobs, g)
                    if j == 0:
                        pe.wait_ge(s_f_split, 2 * g + 2)
                        pe.wait_ge(s_w_lo, 3)
                    c = slice(j * P, (j + 1) * P)
                    for k in range(DK):
                        mm(bank[:, :], wq_h[:, k, c], xT_h[:, k, :], start=(k == 0), stop=False)
                        mm(bank[:, :], wq_h[:, k, c], xT_l[:, k, :], start=False, stop=False)
                        last = mm(bank[:, :], wq_l[:, k, c], xT_h[:, k, :], start=False, stop=(k == DK - 1))
                    last.then_inc(s_q_ready, 1)
                if has_cur:
                    bank = take_bank(("K", j), jobs, g)
                    if j == 0:
                        pe.wait_ge(s_ck_ready, g + 1)
                    mm(bank[:, :], wk_h[:, c], ck_h[:, :], start=True, stop=False)
                    mm(bank[:, :], wk_h[:, c], ck_l[:, :], start=False, stop=False)
                    mm(bank[:, :], wk_l[:, c], ck_h[:, :], start=False, stop=False)
                    mm(bank[:, :], wk_d[:, c], ck_d[:, :], start=False, stop=False)
                    mm(bank[:, :], wk_e[:, c], ck_d[0:R2, :], start=False, stop=True).then_inc(s_k_ready, 1)
                    if j == NP - 1:
                        misc("FA", take_bank(("FA", 0), jobs, g), g)
                        misc("FB", take_bank(("FB", 0), jobs, g), g)
                        transpose_probs(u - 1)
                    bank = take_bank(("V", j), jobs, g)
                    if j == 4:
                        pe.wait_ge(s_cv_ready, g + 2)
                    values(bank, j % 4, 1 if j < 4 else 0)
                prev_unit = (has_cur and j > 0) or (has_prev and j == 0)
                if prev_unit and j < NP - 1:
                    transpose_probs(u - 1)
                if has_cur:
                    scores(u)
                if prev_unit:
                    jp = (j - 1) % NP
                    v_needed = 8 * g + (8 if 4 <= jp and j else 4) if j else 8 * g
                    weigh_values(u - 1, jp, v_needed)
                for kind in MISC_PREV.get(j, []) if has_prev else []:
                    misc(kind, take_bank((kind, 0), jobs, g), g)

        iteration(0, False, True)
        with pe.Fori(1, NG) as g:
            iteration(g, True, True)
        iteration(NG, True, False)

    @block.scalar
    def _(act):
        me = Steps(act, s_act_self)

        def high(out_, in_, scale=1.0):
            return nc.scalar.activation(out_, in_, ACT.Copy, scale=scale)

        stage = [work[:, :], rows[:, 2:4].rearrange("p a b d -> p (a b d)")]
        act.wait_ge(s_w_in, 96)
        high(wv_h[:, :], stage[0][:, 0:INNER])
        high(wv_d[:, :], stage[0][:, INNER:2 * INNER]).then_inc(s_w_hi, 1)
        high(wk_h[:, :], stage[1][:, 0:INNER])
        high(wk_d[:, :], stage[1][:, INNER:2 * INNER]).then_inc(s_w_hi, 1)
        act.wait_ge(s_small_in, 64)
        nc.scalar.activation(tanh_g[:, :], tanh_g[:, :], ACT.Tanh).then_inc(s_tanh, 1)

        act.wait_ge(s_wq_in, 16)
        high(wq_h[:, :, :], stage[0].rearrange("p (k n) -> p k n", k=DK), SCALE).then_inc(s_w_hi, 1)
        for k in range(DK):
            act.wait_ge(s_f_ready, k + 1)
            high(xT_h[:, k, :], proj[k][:, :]).then_inc(s_f_hi, 1)
        act.wait_ge(s_wo_in, 16)
        high(wo_h[:, :, :], stage[1].rearrange("p (j n) -> p j n", j=NP)).then_inc(s_w_hi, 1)

        def iteration(g, has_prev, has_cur):
            jobs = jobs_of(has_prev, has_cur)
            for j in range(NP):
                u = 8 * g + j
                if has_cur:
                    act.wait_ge(s_q_ready, u + 1)
                    high(q_sb[:, :], bank_of(("Q", j), jobs)[:, :]).then_inc(s_q_done, 1)
                if (has_prev and (has_cur or j < 2)) or (has_cur and j >= 2):
                    act.wait_ge(s_av_ready, u - 1)
                    high(aT_h[:, (j - 2) % NP, :], av[j % 2][:, :]).then_inc(s_at_hi, 1)
                if has_cur:
                    act.wait_ge(s_k_ready, u + 1)
                    high(k_sb[:, :], bank_of(("K", j), jobs)[:, :]).then_inc(s_k_done, 1)
                if has_cur and j == NP - 1:
                    for k in range(DK):
                        act.wait_ge(s_f_ready, 2 * g + 3 + k)
                        high(xT_h[:, k, :], bank_of(("FA" if k == 0 else "FB", 0), jobs)[:, :]).then_inc(s_f_hi, 1)
                if has_prev and j == 4:
                    act.wait_ge(s_gdiff, g)
                    nc.scalar.activation(gexp[:, :], gdiff[:, :], ACT.Exp).then_inc(s_gexp, 1)
                prev_unit = (has_cur and j > 0) or (has_prev and j == 0)
                if prev_unit:
                    act.wait_ge(s_pt_ready, 2 * u - 1)
                    high(pT[:, 0, :], probT[0][:, :]).then_inc(s_pt_done0, 1)
                if has_cur:
                    for hh in range(2):
                        act.wait_ge(s_negmax, 2 * u + 1 + hh)
                        for b in range(GB):
                            c = hh * GB + b
                            last = nc.scalar.activation(probs[:, c, :], score[hh][:, b * P:(b + 1) * P], ACT.Exp,
                                                        bias=negmax[:, j % 2, c:c + 1], accum_out=sums[:, j % 2, c:c + 1])
                        last.then_inc(s_exp, 1)

        iteration(0, False, True)
        with act.Fori(1, NG) as g:
            iteration(g, True, True)
        iteration(NG, True, False)

    @block.vector
    def _(dve):
        me = Steps(dve, s_dve_self)
        V = nc.vector

        def low(out_, full, high_):
            return V.tensor_tensor(out_, full, high_.bitcast(f32), ALU.subtract)

        def stats(src, st, mv, out_sem):
            for b in range(GB):
                n = me.mark(V.bn_stats(st[:, b, :], src[:, b, :]))
            me.after(n)
            pass_gate(dve, s_dve_gate)
            for b in range(GB):
                last = V.bn_aggr(mv[:, b, :], st[:, b, :])
            last.then_inc(out_sem, 1)

        def normalise(dst, src, mv, r, out_sem):
            for b in range(GB):
                last = V.tensor_scalar(dst[:, b, :], src[:, b, :], mv[:, b, 0:1], r[:, b:b + 1], ALU.subtract, ALU.mult)
            last.then_inc(out_sem, 1)

        dve.wait_ge(s_x_in, 16)
        stats(xn, stats1, mv1, s_stats1)
        stage = [work[:, :], rows[:, 2:4].rearrange("p a b d -> p (a b d)")]
        for n, (l, h, d, e) in enumerate(((wv_l, wv_h, wv_d, wv_e), (wk_l, wk_h, wk_d, wk_e))):
            dve.wait_ge(s_w_hi, n + 1)
            low(l[:, :], stage[n][:, 0:INNER], h[:, :])
            low(e[:, :], stage[n][0:R2, INNER:2 * INNER], d[0:R2, :]).then_inc(s_w_lo, 1)
        dve.wait_ge(s_rstd1, 1)
        normalise(xn, xn, mv1, rstd1, s_xn_ready)
        dve.wait_ge(s_tanh, 1)
        V.tensor_scalar(bias_o[:, :], bias_o[:, :], tanh_g[:, 0:1], None, ALU.mult).then_inc(s_bias_o, 1)

        def low_v0(b):
            dve.wait_ge(s_v_ready, b + 1)
            V.tensor_copy(v_sb[:, 0, b, :], proj[b % 2][:, :]).then_inc(s_v_done, 1)

        low_v0(0)
        low_v0(1)
        dve.wait_ge(s_w_hi, 3)
        V.scalar_tensor_tensor(out=wq_l[:, :, :], in0=stage[0].rearrange("p (k n) -> p k n", k=DK), scalar=SCALE,
                               in1=wq_h[:, :, :].bitcast(f32), op0=ALU.mult, op1=ALU.subtract).then_inc(s_w_lo, 1)
        low_v0(2)
        low_v0(3)
        for k in range(DK):
            dve.wait_ge(s_f_hi, k + 1)
            low(xT_l[:, k, :], proj[k][:, :], xT_h[:, k, :]).then_inc(s_f_split, 1)
        dve.wait_ge(s_w_hi, 4)
        low(wo_l[:, :, :], stage[1].rearrange("p (j n) -> p j n", j=NP), wo_h[:, :, :]).then_inc(s_w_lo, 1)

        def route_masks(g):
            dve.wait_ge(s_lg_done, g)
            pass_gate(dve, s_dve_gate)
            for b in range(GB):
                n = me.mark(V.max(top[:, b, :], logits[:, b, :]))
            me.after(n)
            n = me.mark(V.tensor_tensor(gdiff[:, :], top[:, :, 1], top[:, :, 0], ALU.subtract))
            for b in range(GB):
                n = me.mark(V.max_index(topi[:, b, :], top[:, b, :], logits[:, b, :]))
            me.after(n)
            n = me.mark(V.tensor_copy(choice[:, :, :], topi[:, :, 0:2].rearrange("p b j -> p j b")))
            me.after(n)
            dve.sem_inc(s_gdiff, 1)
            V.tensor_tensor(mask[:, :, :, :].rearrange("p j b e -> p (j b) e"),
                            iota[:, 0:E].unsqueeze(1).to_broadcast([P, 2 * GB, E]),
                            choice[:, :, :].rearrange("p j b -> p (j b)").unsqueeze(2).to_broadcast([P, 2 * GB, E]),
                            ALU.is_equal).then_inc(s_mask_ready, 1)

        def route_slots(g):
            dve.wait_ge(s_gexp, g)
            n = me.mark(V.tensor_scalar(gden[:, :], gexp[:, :], 1.0, None, ALU.add))
            me.after(n)
            n = me.mark(V.reciprocal(gates[:, 0, :], gden[:, :]))
            me.after(n)
            me.mark(V.tensor_tensor(gates[:, 1, :], gexp[:, :], gates[:, 0, :], ALU.mult))
            n = me.mark(V.tensor_copy(running[:, :, 0, :], running[:, :, GB, :]))
            me.after(n)
            dve.wait_ge(s_pr_done, g)
            pr = ranks[:, :].rearrange("p (w j b e) -> p w j b e", w=2, j=2, b=GB)
            for b in range(GB):
                n = me.mark(V.tensor_tensor(running[:, :, b + 1, :], pr[:, 1, :, b, :], running[:, :, b, :], ALU.add))
                me.after(n)
            n = me.mark(V.tensor_tensor(place[:, :, :, :], pr[:, 0], running[:, :, 0:GB, :], ALU.add))
            me.after(n)
            n = me.mark(V.tensor_tensor(place[:, :, :, :], place[:, :, :, :], mask[:, :, :, :], ALU.mult))
            me.after(n)
            n = me.mark(V.tensor_reduce(loc[:, :, :], place[:, :, :, :], axis=AX, op=ALU.add))
            n = me.mark(V.tensor_scalar(slot[:, 0, :], choice[:, 0, :], float(CAP), None, ALU.mult))
            n = me.mark(V.tensor_scalar(slot[:, 1, :], choice[:, 1, :], float(CAP), float(CAP - 1), ALU.mult, ALU.add))
            me.after(n)
            n = me.mark(V.tensor_scalar(late[:, :, :], loc[:, :, :], float(CAP), BIG, ALU.is_ge, ALU.mult))
            n = me.mark(V.tensor_tensor(slot[:, 0, :], slot[:, 0, :], loc[:, 0, :], ALU.add))
            n = me.mark(V.tensor_tensor(slot[:, 1, :], slot[:, 1, :], loc[:, 1, :], ALU.subtract))
            me.after(n)
            n = me.mark(V.tensor_tensor(sloti[:, :, :], slot[:, :, :], late[:, :, :], ALU.add))
            me.after(n)
            n = me.mark(V.tensor_scalar(hl_i[:, 0], sloti[:, :, :], 7, None, ALU.arith_shift_right))
            n = me.mark(V.tensor_scalar(hl_i[:, 1], sloti[:, :, :], P - 1, None, ALU.bitwise_and))
            me.after(n)
            V.tensor_copy(hl[:, :, :, :], hl_i[:, :, :, :]).then_inc(s_slot_ready, 1)

        def iteration(g, has_prev, has_cur):
            jobs = jobs_of(has_prev, has_cur)
            for j in range(NP):
                u = 8 * g + j
                prev_unit = (has_cur and j > 0) or (has_prev and j == 0)
                if (has_prev and (has_cur or j < 2)) or (has_cur and j >= 2):
                    dve.wait_ge(s_at_hi, u - 1)
                    low(aT_l[:, (j - 2) % NP, :], av[j % 2][:, :], aT_h[:, (j - 2) % NP, :]).then_inc(s_at_split, 1)

                def values_out():
                    dve.wait_ge(s_v_ready, 8 * g + j + GB + 1)
                    if j == 4 or (j == 0 and has_prev):
                        dve.wait_ge(s_av_ready, u)
                    V.tensor_copy(v_sb[:, 1 if j < 4 else 0, j % 4, :], bank_of(("V", j), jobs)[:, :]).then_inc(s_v_done, 1)

                if has_cur and j == NP - 1:
                    for k in range(DK):
                        dve.wait_ge(s_f_hi, 2 * g + 3 + k)
                        low(xT_l[:, k, :], bank_of(("FA" if k == 0 else "FB", 0), jobs)[:, :], xT_h[:, k, :]).then_inc(
                            s_f_split, 1)
                if prev_unit and j == NP - 1:
                    dve.wait_ge(s_pt_ready, 2 * u)
                    V.tensor_copy(pT[:, 1, :], probT[1][:, :]).then_inc(s_pt_done1, 1)
                if has_cur and j % 4:
                    values_out()
                if prev_unit and j < NP - 1:
                    dve.wait_ge(s_pt_ready, 2 * u)
                    V.tensor_copy(pT[:, 1, :], probT[1][:, :]).then_inc(s_pt_done1, 1)
                if has_prev and j == 2:
                    dve.wait_ge(s_rstd2, g)
                    normalise(xn2, x1, mv2, rstd2, s_xn2_ready)
                if has_cur:
                    for hh in range(2):
                        dve.wait_ge(s_s_ready, 2 * u + 1 + hh)
                        V.tensor_reduce(negmax[:, j % 2, hh * GB:(hh + 1) * GB],
                                        score[hh][:, :].rearrange("p (i k) -> p i k", i=GB), axis=AX, op=ALU.max,
                                        negate=True).then_inc(s_negmax, 1)
                    if j % 4 == 0:
                        values_out()
                if has_prev and j == 2:
                    for k in range(DK):
                        dve.wait_ge(s_xt_ready, 2 * g - 1 + k)
                        V.tensor_copy(xn2T[:, k, :], bank_of((("XA", "XB")[k], 0), jobs)[:, :]).then_inc(s_xt_done, 1)
                if has_prev and j == 3:
                    dve.wait_ge(s_lg_ready, g)
                    V.tensor_copy(logits[:, :, :], bank_of(("LG", 0), jobs)[:, 0:GB * E].rearrange(
                        "p (b e) -> p b e", b=GB)).then_inc(s_lg_done, 1)
                if has_prev and j == 4:
                    dve.wait_ge(s_pr_ready, g)
                    V.tensor_copy(ranks[:, :], bank_of(("PR", 0), jobs)[:, 0:4 * GB * E]).then_inc(s_pr_done, 1)
                if has_prev and j == 7:
                    for n in range(2):
                        dve.wait_ge(s_tb_ready, 2 * g - 1 + n)
                        V.tensor_tensor(table[:, n], bank_of((f"T{n}", 0), jobs)[:, 0:2 * NHI].rearrange(
                            "p (w h) -> p w h", w=2), table[:, n], ALU.add).then_inc(s_tb_done, 1)
                if not has_prev and j == 7:
                    dve.wait_ge(s_v_done, NP + GB)
                    dve.wait_ge(s_f_split, 4)
                    dve.sem_inc(s_tb_done, 2)
                if has_cur:
                    for hh in range(2):
                        c = slice(hh * GB, (hh + 1) * GB)
                        dve.wait_ge(s_exp, 2 * u + 1 + hh)
                        n = me.mark(V.reciprocal(rsum[:, c], sums[:, j % 2, c]))
                        me.after(n)
                        V.tensor_tensor(probs[:, c, :], probs[:, c, :], rsum[:, c].unsqueeze(2).to_broadcast([P, GB, P]),
                                        ALU.mult).then_inc(s_p_ready, 1)
                if has_prev and j == 1:
                    dve.wait_ge(s_xr_ready, g)
                    if not isinstance(g, int) or g > 1:
                        dve.wait_ge(s_x1_out, 16 * g - 16)
                    for n in range(2):
                        dve.wait_ge(s_o_ready, 2 * g - 1 + n)
                        V.scalar_tensor_tensor(out=x1[:, 2 * n:2 * n + 2, :],
                                               in0=bank_of((f"O{n}", 0), jobs)[:, :].rearrange("p (b d) -> p b d", b=2),
                                               scalar=tanh_g[:, 0:1], in1=xr[:, 2 * n:2 * n + 2, :], op0=ALU.mult,
                                               op1=ALU.add).then_inc(s_o_done, 1)
                    dve.wait_ge(s_o_done, 2 * g)
                    stats(x1, stats2, mv2, s_stats2)
                if has_cur and j == 2:
                    dve.wait_ge(s_x_in, 16 * g + 32)
                    stats(xn, stats1, mv1, s_stats1)
                if has_prev and j == 3:
                    route_masks(g)
                if has_prev and j == 4:
                    route_slots(g)
                if has_cur and j == 5:
                    dve.wait_ge(s_rstd1, g + 2)
                    normalise(xn, xn, mv1, rstd1, s_xn_ready)

        iteration(0, False, True)
        start, per = me.n, 53
        with dve.Fori(1, NG) as g:
            me.enter((g - 1) * per + start)
            iteration(g, True, True)
            assert me.n == per, me.n
        me.enter(start + (NG - 1) * per)
        iteration(NG, True, False)


def experts(nc, ctx, sem, acc_dram, xn2_dram, fc1T, fc1b, fc2, fc2b, out, table, running, tanh_g):
    f32, f32r, i32, u32 = mybir.dt.float32, mybir.dt.float32r, mybir.dt.int32, mybir.dt.uint32
    ALU, ACT, AX = mybir.AluOpType, mybir.ActivationFunctionType, mybir.AxisListType.X

    def sb(name, shape, dt=f32):
        return ctx.enter_context(nc.sbuf_tensor(name, shape, dt))

    w1_raw, w2_raw = sb("w1_raw", [P, DK, H]), sb("w2_raw", [P, HK, D])
    w1_h = [sb(f"w1_h{n}", [P, DK, H], f32r) for n in range(2)]
    w1_l = [sb(f"w1_l{n}", [P, DK, H], f32r) for n in range(2)]
    w2_h = [sb(f"w2_h{n}", [P, HK, D], f32r) for n in range(2)]
    w2_l = [sb(f"w2_l{n}", [P, HK, D], f32r) for n in range(2)]
    b1 = [sb(f"b1_{n}", [P, HK]) for n in range(2)]
    b2 = [sb(f"b2_{n}", [P, D]) for n in range(2)]
    rows = [sb(f"rows_{n}", [P, GB, D]) for n in range(2)]
    rT_h, rT_l = sb("rT_h", [P, DK, TOK], f32r), sb("rT_l", [P, DK, TOK], f32r)
    hid = [sb(f"hid{n}", [P, TOK]) for n in range(2)]
    hid_h, hid_l = sb("hid_h", [P, HK, TOK], f32r), sb("hid_l", [P, HK, TOK], f32r)
    eo_raw = sb("eo_raw", [P, GB, D])
    eo = [sb(f"eo_{n}", [P, GB, D]) for n in range(2)]
    ident = sb("ident_b", [P, P])
    NCOL = NHI + EH
    rank, keep2, tokf, free = sb("rank", [P, E, EH]), sb("keep2", [P, E, EH]), sb("tokf", [P, NCOL]), sb("free", [P, NHI])
    spare = sb("spare", [P, NHI])
    gate = sb("gate", [P, NHI])
    index = sb("index", [P, NCOL], u32)
    index_e = [sb(f"index_e{n}", [P, EH], u32) for n in range(2)]
    gate_e = [sb(f"gate_e{n}", [P, EH]) for n in range(2)]

    def ps(name):
        return ctx.enter_context(nc.psum_tensor(name, [P, TOK], f32))

    up = [ps("up0"), ps("up1")]
    rT = [ps("rT0"), ps("rT1")]
    down = [ps(f"down{n}") for n in range(GB)]

    (
        s_consts, s_index, s_w_in, s_w_hi, s_w_lo, s_w_raw_free, s_b_in0, s_b_in1, s_gather0, s_gather1,
        s_rt_ready, s_rt_hi, s_rt_split, s_up_ready, s_hid, s_hid_hi, s_hid_split, s_down_ready, s_eo_raw,
        s_eo_raw2, s_eo_ready, s_scatter, s_gate_e, s_index_e, s_out, s_dve_self, s_pool_self, s_dve_gate,
        s_pool_gate, s_rows_free,
    ) = (sem("e_" + name) for name in (
        "consts", "index", "w_in", "w_hi", "w_lo", "w_raw_free", "b_in0", "b_in1", "gather0", "gather1",
        "rt_ready", "rt_hi", "rt_split", "up_ready", "hid", "hid_hi", "hid_split", "down_ready", "eo_raw",
        "eo_raw2", "eo_ready", "scatter", "gate_e", "index_e", "out", "dve_self", "pool_self", "dve_gate",
        "pool_gate", "rows_free",
    ))
    gathers = [s_gather0, s_gather1]
    biases = [s_b_in0, s_b_in1]

    block = ctx.enter_context(nc.Block())
    EB = 2
    TURNS = E // EB

    @block.sync
    def _(sp):
        def load(e, par):
            sp.dma_start(w1_raw[:, :, :], fc1T[bass.ds(e, 1), :, :].rearrange("o (k p) h -> p (o k) h", p=P)).then_inc(s_w_in, 16)
            sp.dma_start(w2_raw[:, :, :], fc2[bass.ds(e, 1), :, :].rearrange("o (k p) d -> p (o k) d", p=P)).then_inc(s_w_in, 16)

        def load_bias(e, par):
            sp.dma_start(b1[par][:, :], fc1b[bass.ds(e, 1), :, :].rearrange("o p m -> p (o m)")).then_inc(biases[par], 16)
            sp.dma_start(b2[par][:, :], fc2b[bass.ds(e, 1), 0, :].to_broadcast([P, D])).then_inc(biases[par], 16)

        def step(e, nxt, par, first=False):
            sp.wait_ge(s_w_lo, e + 1)
            load(nxt, 1 - par)
            if not first:
                sp.wait_ge(s_eo_raw2, 2 * e)
            load_bias(nxt, 1 - par)

        load(0, 0)
        load_bias(0, 0)
        step(0, 1, 0, True)
        step(1, 2, 1)
        with sp.Fori(1, TURNS - 1) as t:
            for i in range(EB):
                step(EB * t + i, EB * t + i + 1, i)
        step(E - 2, E - 1, 0)
        step(E - 1, E - 1, 1)
        sp.wait_ge(s_w_in, 32 * (E + 1))
        sp.wait_ge(biases[0], 32 * (E // 2 + 1))
        sp.wait_ge(biases[1], 32 * (E // 2))
        sp.wait_ge(s_scatter, 16 * NHI)
        flat_in = acc_dram[0:N, :].rearrange("(q r) d -> q (r d)", q=P)
        flat_out = out.rearrange("b s d -> (b s) d").rearrange("(q r) d -> q (r d)", q=P)
        sp.dma_start(flat_out, flat_in).then_inc(s_out, 16)
        sp.wait_ge(s_out, 16)

    @block.gpsimd
    def _(pool):
        me = Steps(pool, s_pool_self)
        me.mark(nc.gpsimd.memset(ident[:, :], 0.0))
        me.after()
        nc.gpsimd.affine_select(out=ident[:, :], in_=ident[:, :], compare_op=ALU.not_equal, fill=1.0, base=0,
                                pattern=[[-1, P]], channel_multiplier=1)
        nc.gpsimd.iota(rank[:, :, :], pattern=[[0, E], [P, EH]], base=0, channel_multiplier=1,
                       allow_small_or_imprecise_dtypes=True)
        me.mark(nc.gpsimd.iota(spare[:, :], pattern=[[0, NHI]], base=N + 1, channel_multiplier=1,
                               allow_small_or_imprecise_dtypes=True))
        nc.gpsimd.iota(tokf[:, NHI:NCOL], pattern=[[0, EH]], base=N, channel_multiplier=1,
                       allow_small_or_imprecise_dtypes=True)
        me.after()
        nc.gpsimd.memset(eo_raw[:, 0, 0:1], 0.0).then_inc(s_consts, 1)

        def columns(e, par):
            nc.gpsimd.tensor_copy(index_e[par][:, :], index[:, bass.ds(e * EH, EH)]).then_inc(s_index_e, 1)

        def gather(n, par, half):
            pass_gate(pool, s_pool_gate)
            for i in range(GB):
                pool.indirect_dma_start(
                    out=rows[half][:, i, :], out_offset=None, in_=xn2_dram[:, :],
                    in_offset=bass.IndirectOffsetOnAxis(ap=index_e[par][:, half * GB + i:half * GB + i + 1], axis=0),
                    bounds_check=N + PAD - 1, oob_is_err=False).then_inc(gathers[half], 16)

        def scatter(n, par, half):
            pool.wait_ge(s_eo_ready, n + 1)
            for i in range(GB):
                if not (isinstance(n, int) and n == 0 and i == 0):
                    pool.wait_ge(s_scatter, 16 * (GB * n + i))
                pass_gate(pool, s_pool_gate)
                pool.indirect_dma_start(
                    out=acc_dram[:, :], out_offset=bass.IndirectOffsetOnAxis(
                        ap=index_e[par][:, half * GB + i:half * GB + i + 1], axis=0),
                    in_=eo[half][:, i, :], in_offset=None, bounds_check=N + PAD - 1, oob_is_err=True,
                    compute_op=ALU.add).then_inc(s_scatter, 16)

        def split_low(e, par):
            pool.wait_ge(s_w_hi, 2 * e + 1)
            for k in range(DK):
                nc.gpsimd.tensor_tensor(w1_l[par][:, k, :], w1_raw[:, k, :], w1_h[par][:, k, :].bitcast(f32), ALU.subtract)
            pool.wait_ge(s_w_hi, 2 * e + 2)
            nc.gpsimd.tensor_tensor(w2_l[par][:, :, :], w2_raw[:, :, :], w2_h[par][:, :, :].bitcast(f32),
                                    ALU.subtract).then_inc(s_w_lo, 1)

        pool.wait_ge(s_index, 1)
        columns(0, 0)
        pool.wait_ge(s_index_e, 1)
        gather(0, 0, 0)
        gather(1, 0, 1)
        split_low(0, 0)

        def step(e, par):
            split_low(e + 1, 1 - par)
            if not (isinstance(e, int) and e == 0):
                pool.wait_ge(s_scatter, 16 * EH * e)
                pass_gate(pool, s_pool_gate)
            columns(e + 1, 1 - par)
            pool.wait_ge(s_index_e, e + 2)
            for half in range(2):
                n = 2 * e + half
                pool.wait_ge(s_rt_ready, 2 * n + 2)
                gather(n + 2, 1 - par, half)
                scatter(n, par, half)

        step(0, 0)
        step(1, 1)
        with pool.Fori(1, TURNS) as t:
            for i in range(EB):
                step(EB * t + i, i)
        for half in range(2):
            pool.wait_ge(gathers[half], 16 * GB * (E + 1))
        pool.wait_ge(s_scatter, 16 * NHI)

    @block.tensor
    def _(pe):
        mm = nc.tensor.matmul
        pe.wait_ge(s_consts, 1)

        def transpose_rows(n, half, first=False):
            e = n
            pe.wait_ge(gathers[half], n)
            for k in range(DK):
                for b in range(GB):
                    last = nc.tensor.transpose(rT[k][:, b * P:(b + 1) * P], rows[half][:, b, k * P:(k + 1) * P], ident[:, :])
                last.then_inc(s_rt_ready, 1)

        def group(n, e, par, half):
            for m in range(HK):
                if not (isinstance(n, int) and n == 0 and m < 2):
                    pe.wait_ge(s_hid, 8 * n + m - 1)
                if m == 0:
                    pe.wait_ge(s_rt_split, 2 * n + 2)
                    pe.wait_ge(s_w_lo, e + 1)
                c = slice(m * P, (m + 1) * P)
                for k in range(DK):
                    mm(up[m % 2][:, :], w1_h[par][:, k, c], rT_h[:, k, :], start=(k == 0), stop=False)
                    mm(up[m % 2][:, :], w1_h[par][:, k, c], rT_l[:, k, :], start=False, stop=False)
                    last = mm(up[m % 2][:, :], w1_l[par][:, k, c], rT_h[:, k, :], start=False, stop=(k == DK - 1))
                last.then_inc(s_up_ready, 1)
            transpose_rows(16 * GB * (e + 1) if half == 0 else 16 * GB * (e + 2), 1 - half)
            for k in range(HK):
                pe.wait_ge(s_hid_split, 8 * n + k + 1)
                for i in range(GB):
                    if k == 0 and not (isinstance(n, int) and n == 0):
                        pe.wait_ge(s_eo_raw, 4 * n - 3 + i)
                    t = slice(i * P, (i + 1) * P)
                    o = down[i][:, 0:D]
                    mm(o, hid_h[:, k, t], w2_h[par][:, k, :], start=(k == 0), stop=False)
                    mm(o, hid_h[:, k, t], w2_l[par][:, k, :], start=False, stop=False)
                    last = mm(o, hid_l[:, k, t], w2_h[par][:, k, :], start=False, stop=(k == HK - 1))
                    if k == HK - 1:
                        last.then_inc(s_down_ready, 1)

        transpose_rows(16 * GB, 0)
        for n in range(2 * EB):
            group(n, n // 2, n // 2, n % 2)
        with pe.Fori(1, TURNS) as t:
            for i in range(2 * EB):
                group(2 * EB * t + i, EB * t + i // 2, i // 2, i % 2)

    @block.scalar
    def _(act):
        def split_high(e, par):
            act.wait_ge(s_w_in, 32 * e + 32)
            nc.scalar.activation(w1_h[par][:, :, :], w1_raw[:, :, :], ACT.Copy).then_inc(s_w_hi, 1)
            nc.scalar.activation(w2_h[par][:, :, :], w2_raw[:, :, :], ACT.Copy).then_inc(s_w_hi, 1)

        def high_rows(n):
            for k in range(DK):
                act.wait_ge(s_rt_ready, 2 * n + k + 1)
                nc.scalar.activation(rT_h[:, k, :], rT[k][:, :], ACT.Copy).then_inc(s_rt_hi, 1)

        def group(n, e, par, half):
            if half == 0:
                act.wait_ge(biases[par], 16 * (e - par) + 32)
            for m in range(HK):
                act.wait_ge(s_up_ready, 8 * n + m + 1)
                if not (isinstance(n, int) and n == 0 and m < 2):
                    act.wait_ge(s_hid_split, 8 * n + m - 1)
                nc.scalar.activation(hid[m % 2][:, :], up[m % 2][:, :], ACT.Relu, bias=b1[par][:, m:m + 1]).then_inc(s_hid, 1)
            high_rows(n + 1)
            if half == 0:
                split_high(e + 1, 1 - par)
            if not (isinstance(n, int) and n < 2):
                act.wait_ge(s_scatter, 64 * n - 64)
            for i in range(GB):
                act.wait_ge(s_eo_raw, 4 * n + i + 1)
                last = nc.scalar.activation(eo[half][:, i, :], eo_raw[:, i, :], ACT.Copy,
                                            scale=gate_e[par][:, half * GB + i:half * GB + i + 1])
            last.then_inc(s_eo_ready, 1)

        split_high(0, 0)
        high_rows(0)
        for n in range(2 * EB):
            group(n, n // 2, n // 2, n % 2)
        with act.Fori(1, TURNS) as t:
            for i in range(2 * EB):
                group(2 * EB * t + i, EB * t + i // 2, i // 2, i % 2)

    @block.vector
    def _(dve):
        me = Steps(dve, s_dve_self)
        V = nc.vector
        dve.wait_ge(s_consts, 1)
        n = me.mark(V.tensor_tensor(keep2[:, :, :], rank[:, :, :],
                                    running[:, 0, GB, :].unsqueeze(2).to_broadcast([P, E, EH]), ALU.is_ge))
        me.after(n)
        k2 = keep2[:, :, :].rearrange("p e h -> p (e h)")
        n = me.mark(V.tensor_tensor(tokf[:, 0:NHI], table[:, 1, 0, :], k2, ALU.mult))
        n = me.mark(V.tensor_tensor(gate[:, :], table[:, 1, 1, :], k2, ALU.mult))
        me.after(n)
        n = me.mark(V.tensor_tensor(tokf[:, 0:NHI], tokf[:, 0:NHI], table[:, 0, 0, :], ALU.add))
        n = me.mark(V.tensor_tensor(gate[:, :], gate[:, :], table[:, 0, 1, :], ALU.add))
        me.after(n)
        n = me.mark(V.tensor_scalar(free[:, :], tokf[:, 0:NHI], 0.0, None, ALU.is_equal))
        n = me.mark(V.tensor_scalar(gate[:, :], gate[:, :], tanh_g[:, 1:2], None, ALU.mult))
        me.after(n)
        n = me.mark(V.tensor_tensor(free[:, :], free[:, :], spare[:, :], ALU.mult))
        me.after(n)
        n = me.mark(V.scalar_tensor_tensor(out=tokf[:, 0:NHI], in0=tokf[:, 0:NHI], scalar=-1.0, in1=free[:, :],
                                           op0=ALU.add, op1=ALU.add))
        me.after(n)
        V.tensor_copy(index[:, :], tokf[:, :]).then_inc(s_index, 1)

        def low_rows(n):
            for k in range(DK):
                dve.wait_ge(s_rt_hi, 2 * n + k + 1)
                V.tensor_tensor(rT_l[:, k, :], rT[k][:, :], rT_h[:, k, :].bitcast(f32), ALU.subtract).then_inc(s_rt_split, 1)

        def group(n, e, par, half):
            if half == 0:
                dve.wait_ge(biases[par], 16 * (e - par) + 32)
                V.tensor_copy(gate_e[par][:, :], gate[:, bass.ds(e * EH, EH)])
            for m in range(HK):
                dve.wait_ge(s_hid, 8 * n + m + 1)
                V.tensor_copy(hid_h[:, m, :], hid[m % 2][:, :]).then_inc(s_hid_hi, 1)
                dve.wait_ge(s_hid_hi, 8 * n + m + 1)
                V.tensor_tensor(hid_l[:, m, :], hid[m % 2][:, :], hid_h[:, m, :].bitcast(f32),
                                ALU.subtract).then_inc(s_hid_split, 1)
            low_rows(n + 1)
            for i in range(GB):
                dve.wait_ge(s_down_ready, 4 * n + i + 1)
                if not (isinstance(n, int) and n == 0):
                    dve.wait_ge(s_eo_ready, n)
                V.tensor_tensor(eo_raw[:, i, :], down[i][:, 0:D], b2[par][:, :], ALU.add).then_inc(s_eo_raw, 1)
            dve.wait_ge(s_eo_raw, 4 * n + 4)
            dve.sem_inc(s_eo_raw2, 1)

        low_rows(0)
        for n in range(2 * EB):
            group(n, n // 2, n // 2, n % 2)
        with dve.Fori(1, TURNS) as t:
            for i in range(2 * EB):
                group(2 * EB * t + i, EB * t + i // 2, i // 2, i % 2)


def kernel(**inputs):
    import numpy as _np
    import concourse.bacc as _bacc
    from concourse import mybir as _mybir
    from concourse.bass_utils import run_bass_kernel_spmd as _run

    a = {k: _np.asarray(v) for k, v in inputs.items()}
    arrays = {
        "x": a["x"],
        "ctxT": a["ctx_768"].reshape(N, DE).T,
        "g_x": a["g_xattn"],
        "g_f": a["g_ffn"],
        "wq": a["L0_xattn_Wq"], "wk": a["L0_xattn_Wk"], "wv": a["L0_xattn_Wv"], "wo": a["L0_xattn_Wo"],
        "bo": a["L0_xattn_bo"],
        "gateT": a["L0_ffn_gate_w"].T,
        "fc1T": a["L0_ffn_fc1_w"].transpose(0, 2, 1),
        "fc1b": a["L0_ffn_fc1_b"].reshape(E, HK, P).transpose(0, 2, 1),
        "fc2": a["L0_ffn_fc2_w"],
        "fc2b": a["L0_ffn_fc2_b"],
    }
    arrays = {f"{k}_dram": _np.ascontiguousarray(v) for k, v in arrays.items()}
    nc = _bacc.Bacc("TRN2", target_bir_lowering=False, num_devices=1)
    args = [nc.dram_tensor(k, v.shape, _mybir.dt.from_np(v.dtype), kind="ExternalInput").ap() for k, v in arrays.items()]
    out = nc.dram_tensor("out_dram", (B, S, D), _mybir.dt.float32, kind="ExternalOutput").ap()
    gated_block(nc, *args, out)
    r = _run(nc, [arrays], core_ids=[0])
    return r.results[0]["out_dram"]
```

```python
import concourse.bass as bass
from concourse import mybir
from contextlib import ExitStack

P = 128
B, S, D, DE = 32, 128, 256, 192
HEADS, DH = 16, 64
INNER = HEADS * DH
E, H = 8, 1024
N = B * S
CAP = 2 * ((N + E - 1) // E)
EPS = 1e-5
SCALE = 1.0 / 8.0

GB = 4
NG = B // GB
TOK = GB * S
NP = HEADS // 2
DK = D // P
HALF = INNER // 2
R2 = DE - P
HK = H // P
NHI = E * CAP // P
EH = CAP // P
NSG = E * CAP // TOK
PAD = P
BIG = 65536.0


def pass_gate(eng, sem):
    eng.sem_inc(sem, 1)


class Steps:

    def __init__(self, eng, sem):
        self.eng, self.sem, self.base, self.n = eng, sem, 0, 0

    def mark(self, ins):
        ins.then_inc(self.sem, 1)
        self.n += 1
        return self.n

    def after(self, n=None):
        self.eng.wait_ge(self.sem, self.base + (self.n if n is None else n))

    def enter(self, base):
        self.base, self.n = base, 0


MISC_PREV = {1: ["O0", "O1"], 2: ["XA", "XB"], 3: ["LG"], 4: ["PR"], 7: ["T0", "T1"]}


def jobs_of(has_prev, has_cur):
    out = []
    for j in range(NP):
        if has_cur:
            out += [("Q", j), ("K", j)] + [("FA", 0), ("FB", 0)] * (j == NP - 1) + [("V", j)]
        if has_prev:
            out += [(m, 0) for m in MISC_PREV.get(j, [])]
    return out


def gated_block(nc, x, ctxT, g_x, g_f, wq, wk, wv, wo, bo, gateT, fc1T, fc1b, fc2, fc2b, out):
    f32 = mybir.dt.float32

    xn2_dram = nc.dram_tensor("xn2_rows", [N + PAD, D], f32, kind="Internal").ap()
    x_v = x.rearrange("b p d -> p b d")
    out_v = out.rearrange("b p d -> p b d")
    out_rows = out.rearrange("b p d -> (b p) d")
    xn2_v = xn2_dram[0:N, :].rearrange("(b p) d -> p b d", p=P)

    with ExitStack() as keep:
        def sem(name):
            return keep.enter_context(nc.semaphore(name))

        table = keep.enter_context(nc.sbuf_tensor("table", [P, 2, 2, NHI], f32))
        running = keep.enter_context(nc.sbuf_tensor("running", [P, 2, GB + 1, E], f32))
        tanh_g = keep.enter_context(nc.sbuf_tensor("tanh_g", [P, 2], f32))
        ident = keep.enter_context(nc.sbuf_tensor("ident", [P, P], f32))
        w1_raw = keep.enter_context(nc.sbuf_tensor("w1_raw", [P, DK, H], f32))
        w2_raw = keep.enter_context(nc.sbuf_tensor("w2_raw", [P, HK, D], f32))
        w1_split = [keep.enter_context(nc.sbuf_tensor(f"w1_split{n}", [P, DK, H], mybir.dt.float32r)) for n in range(2)]
        w2_split = [keep.enter_context(nc.sbuf_tensor(f"w2_split{n}", [P, HK, D], mybir.dt.float32r)) for n in range(2)]
        shared = (table, running, tanh_g, ident, w1_raw, w2_raw, w1_split, w2_split)

        with ExitStack() as ctx:
            attention(nc, ctx, sem, x_v, out_v, xn2_v, xn2_dram, ctxT, g_x, g_f, wq, wk, wv, wo, bo, gateT, fc1T, fc2, shared)
        with ExitStack() as ctx:
            experts(nc, ctx, sem, out_rows, xn2_dram, fc1T, fc1b, fc2, fc2b, shared)


def load_expert(sp, fc1T, fc2, e, w1_raw, w2_raw, done_sem):
    sp.dma_start(w1_raw[:, :, :], fc1T[bass.ds(e, 1), :, :].rearrange("o (k p) h -> p (o k) h", p=P)).then_inc(done_sem, 16)
    sp.dma_start(w2_raw[:, :, :], fc2[bass.ds(e, 1), :, :].rearrange("o (k p) d -> p (o k) d", p=P)).then_inc(done_sem, 16)


def attention(nc, ctx, sem, x_v, out_v, xn2_v, xn2_dram, ctxT, g_x, g_f, wq, wk, wv, wo, bo, gateT, fc1T, fc2, shared):
    f32, f32r, i32, u32 = mybir.dt.float32, mybir.dt.float32r, mybir.dt.int32, mybir.dt.uint32
    ALU, ACT, AX = mybir.AluOpType, mybir.ActivationFunctionType, mybir.AxisListType.X

    def sb(name, shape, dt=f32):
        return ctx.enter_context(nc.sbuf_tensor(name, shape, dt))

    table, running, tanh_g, ident, w1_raw, w2_raw, w1_split, w2_split = shared
    (wq_h, wq_l), (wo_h, wo_l) = w1_split, w2_split
    wk_h, wk_l, wk_d = (sb(n, [P, INNER], f32r) for n in ("wk_h", "wk_l", "wk_d"))
    wk_e = sb("wk_e", [R2, INNER], f32r)
    wv_h, wv_l, wv_d = (sb(n, [P, INNER], f32r) for n in ("wv_h", "wv_l", "wv_d"))
    wv_e = sb("wv_e", [R2, INNER], f32r)
    v_sb = sb("v_sb", [P, 2, GB, HALF])
    xT_h, xT_l = sb("xT_h", [P, DK, TOK], f32r), sb("xT_l", [P, DK, TOK], f32r)
    cv_h, cv_l, cv_d = (sb(n, [P, TOK], f32r) for n in ("cv_h", "cv_l", "cv_d"))
    ck_h, ck_l, ck_d = (sb(n, [P, TOK], f32r) for n in ("ck_h", "ck_l", "ck_d"))
    c_raw = sb("c_raw", [P, 2, TOK])
    c_tmp = sb("c_tmp", [P, TOK], f32r)
    work = sb("work", [P, 2 * 1024])
    wv_raw = work
    probs = work[:, 0:1024].rearrange("p (s k) -> p s k", s=8)
    xn2T = work[:, 1024:2048].rearrange("p (k t) -> p k t", k=DK)
    onehot_lo = work[:, 1024:2048].rearrange("p (s k) -> p s k", s=8)
    rows = sb("rows", [P, 4, GB, D])
    xn, xr, x1, xn2 = (rows[:, n] for n in range(4))
    wk_raw = rows[:, 2:4].rearrange("p a b d -> p (a b d)")
    hi_vals = rows[:, 3].rearrange("p b (two c) -> p (b two) c", two=2)
    q_sb, k_sb = sb("q_sb", [P, TOK]), sb("k_sb", [P, TOK])
    pT = sb("pT", [P, 2, TOK])
    aT_h, aT_l = sb("aT_h", [P, NP, TOK], f32r), sb("aT_l", [P, NP, TOK], f32r)
    tri, ones, iota = (sb(n, [P, P]) for n in ("tri", "ones", "iota"))
    bias_o = sb("bias_o", [P, D])
    gate_sb = sb("gate_sb", [P, DK, E])
    zrow = sb("zrow", [P, D])
    stats1, mv1, rstd1 = sb("stats1", [P, GB, 6]), sb("mv1", [P, GB, 2]), sb("rstd1", [P, GB])
    stats2, mv2, rstd2 = sb("stats2", [P, GB, 6]), sb("mv2", [P, GB, 2]), sb("rstd2", [P, GB])
    var1, var2, mhalf = sb("var1", [P, GB]), sb("var2", [P, GB]), sb("mhalf", [P, GB])
    negmax = sb("negmax", [P, 2, 8])
    sums = sb("sums", [P, 2, 8])
    rsum = sb("rsum", [P, 8])
    logits, top, topi = sb("logits", [P, GB, E]), sb("top", [P, GB, E]), sb("topi", [P, GB, E], u32)
    choice = sb("choice", [P, 2, GB])
    mask = sb("mask", [P, 2, GB, E])
    gates, gdiff, gexp, gden = sb("gates", [P, 2, GB]), sb("gdiff", [P, GB]), sb("gexp", [P, GB]), sb("gden", [P, GB])
    place, loc, late, slot = sb("place", [P, 2, GB, E]), sb("loc", [P, 2, GB]), sb("late", [P, 2, GB]), sb("slot", [P, 2, GB])
    ranks = sb("ranks", [P, 2 * 2 * GB * E])
    sloti, hl_i = sb("sloti", [P, 2, GB], i32), sb("hl_i", [P, 2, 2, GB], i32)
    hl = sb("hl", [P, 2, 2, GB])
    token = sb("token", [P, GB])
    lower_half = sb("lower_half", [P, 1])

    def ps(name):
        return ctx.enter_context(nc.psum_tensor(name, [P, TOK], f32))

    proj = [ps("proj0"), ps("proj1")]
    score = [ps("score0"), ps("score1")]
    probT = [ps("probT0"), ps("probT1")]
    av = [ps("av0"), ps("av1")]

    (
        s_consts, s_wv_in, s_wk_in, s_wq_in, s_wo_in, s_c_in, s_x_in, s_xr_in, s_small_in, s_zeros_out, s_w_hi,
        s_w_lo, s_tanh, s_bias_o, s_zrow, s_q_ready, s_k_ready, s_v_ready, s_s_ready, s_pt_ready,
        s_av_ready, s_o_ready, s_xt_ready, s_lg_ready, s_pr_ready, s_tb_ready, s_f_ready, s_at_hi,
        s_f_hi, s_q_done, s_k_done, s_v_done, s_pt_done0, s_pt_done1, s_at_split, s_f_split, s_negmax,
        s_exp, s_p_ready, s_o_done, s_xt_done, s_lg_done, s_pr_done, s_tb_done, s_stats1,
        s_rstd1, s_xn_ready, s_stats2, s_rstd2, s_xn2_ready, s_mask_ready, s_gdiff, s_gexp,
        s_slot_ready, s_onehot, s_cv_ready, s_ck_ready, s_xr_ready, s_x1_out, s_xn2_out, s_wo_lo,
        s_dve_self, s_pool_self, s_dve_gate, s_pool_gate, s_e0_in, s_e0_hi, s_e0_lo,
    ) = (sem("a_" + name) for name in (
        "consts", "wv_in", "wk_in", "wq_in", "wo_in", "c_in", "x_in", "xr_in", "small_in", "zeros_out", "w_hi",
        "w_lo", "tanh", "bias_o", "zrow", "q_ready", "k_ready", "v_ready", "s_ready", "pt_ready",
        "av_ready", "o_ready", "xt_ready", "lg_ready", "pr_ready", "tb_ready", "f_ready", "at_hi",
        "f_hi", "q_done", "k_done", "v_done", "pt_done0", "pt_done1", "at_split", "f_split", "negmax",
        "exp", "p_ready", "o_done", "xt_done", "lg_done", "pr_done", "tb_done", "stats1",
        "rstd1", "xn_ready", "stats2", "rstd2", "xn2_ready", "mask_ready", "gdiff", "gexp",
        "slot_ready", "onehot", "cv_ready", "ck_ready", "xr_ready", "x1_out", "xn2_out", "wo_lo",
        "dve_self", "pool_self", "dve_gate", "pool_gate", "e0_in", "e0_hi", "e0_lo",
    ))

    def done(job, g):
        kind, j = job
        return {
            "Q": (s_q_done, 8 * g + j + 1), "K": (s_k_done, 8 * g + j + 1), "V": (s_v_done, 8 * g + j + GB + 1),
            "O0": (s_o_done, 2 * g - 1), "O1": (s_o_done, 2 * g), "XA": (s_xt_done, 2 * g - 1), "XB": (s_xt_done, 2 * g),
            "LG": (s_lg_done, g), "PR": (s_pr_done, g), "T0": (s_tb_done, 2 * g + 1), "T1": (s_tb_done, 2 * g + 2),
            "FA": (s_f_split, 2 * g + 3), "FB": (s_f_split, 2 * g + 4),
        }[kind]

    def bank_of(job, jobs):
        return proj[jobs.index(job) % 2]

    def onehots(engine):
        for j in range(2):
            for b in range(GB):
                n = j * GB + b
                engine.tensor_scalar(onehot_lo[:, n, :], iota[:, :], hl[:, 1, j, b:b + 1], None, ALU.is_equal)
                engine.tensor_scalar(hi_vals[:, n, 0:NHI], iota[:, 0:NHI], hl[:, 0, j, b:b + 1],
                                     token[:, b:b + 1], ALU.is_equal, ALU.mult)
                last = engine.tensor_scalar(hi_vals[:, n, NHI:2 * NHI], iota[:, 0:NHI], hl[:, 0, j, b:b + 1],
                                            gates[:, j, b:b + 1], ALU.is_equal, ALU.mult)
        return last

    block = ctx.enter_context(nc.Block())

    @block.sync
    def _(sp):
        def load_x(g, dst, done_sem):
            sp.dma_start(rows[:, dst], x_v[:, bass.ds(g * GB, GB), :]).then_inc(done_sem, 16)

        def load_ctx(g):
            cols = bass.ds(g * TOK, TOK)
            sp.dma_start(c_raw[:, 0, :], ctxT[0:P, cols]).then_inc(s_c_in, 16)
            sp.dma_start(c_raw[0:R2, 1, :], ctxT[P:DE, cols]).then_inc(s_c_in, 16)
            sp.dma_start(c_raw[R2:P, 1, :], ctxT[P:DE, cols]).then_inc(s_c_in, 16)

        load_x(0, 0, s_x_in)
        load_ctx(0)

        def load_kv(w, dst, done_sem):
            sp.dma_start(dst[:, 0:INNER], w[0:P, :]).then_inc(done_sem, 16)
            sp.dma_start(dst[0:R2, INNER:2 * INNER], w[P:DE, :]).then_inc(done_sem, 16)
            sp.dma_start(dst[R2:P, INNER:2 * INNER], w[P:DE, :]).then_inc(done_sem, 16)

        load_kv(wv, wv_raw, s_wv_in)
        sp.dma_start(w1_raw[:, :, :], wq.rearrange("(k p) n -> p k n", p=P)).then_inc(s_wq_in, 16)
        load_kv(wk, wk_raw, s_wk_in)
        for k, (src, n) in enumerate(((g_x, 0), (g_f, 1))):
            sp.dma_start(tanh_g[:, n:n + 1], src.rearrange("(o n) -> o n", o=1).to_broadcast([P, 1])).then_inc(s_small_in, 16)
        sp.dma_start(bias_o[:, :], bo.rearrange("(o n) -> o n", o=1).to_broadcast([P, D])).then_inc(s_small_in, 16)
        sp.dma_start(gate_sb[:, :, :], gateT.rearrange("(k p) e -> p k e", p=P)).then_inc(s_small_in, 16)
        sp.dma_start(w2_raw[:, :, :], wo.rearrange("(j p) n -> p j n", p=P)).then_inc(s_wo_in, 16)
        sp.wait_ge(s_zrow, 1)
        sp.dma_start(xn2_dram[N:N + PAD, :], zrow[:, :]).then_inc(s_zeros_out, 16)

        def iteration(g, nxt, has_prev, has_cur):
            if has_cur:
                sp.wait_ge(s_f_ready, 2 * g + 2)
                load_x(nxt, 0, s_x_in)
                sp.wait_ge(s_cv_ready, g + 1)
                load_ctx(nxt)
            if has_prev:
                if not isinstance(g, int) or g > 1:
                    sp.wait_ge(s_o_done, 2 * g - 2)
                load_x(g - 1, 1, s_xr_in)
                sp.wait_ge(s_stats2, g)
                sp.dma_start(out_v[:, bass.ds((g - 1) * GB, GB), :], x1).then_inc(s_x1_out, 16)
                sp.wait_ge(s_xn2_ready, g)
                sp.dma_start(xn2_v[:, bass.ds((g - 1) * GB, GB), :], xn2).then_inc(s_xn2_out, 16)

        iteration(0, 1, False, True)
        sp.wait_ge(s_w_lo, 2)
        sp.wait_ge(s_wo_lo, 1)
        load_expert(sp, fc1T, fc2, 0, w1_raw, w2_raw, s_e0_in)
        iteration(1, 2, True, True)
        with sp.Fori(2, NG - 1) as g:
            iteration(g, g + 1, True, True)
        iteration(NG - 1, NG - 1, True, True)
        iteration(NG, None, True, False)
        sp.wait_ge(s_x1_out, 16 * NG)
        sp.wait_ge(s_xn2_out, 16 * NG)
        sp.wait_ge(s_zeros_out, 16)
        sp.wait_ge(s_x_in, 16 * (NG + 1))
        sp.wait_ge(s_c_in, 48 * (NG + 1))

    @block.gpsimd
    def _(pool):
        me = Steps(pool, s_pool_self)
        me.mark(nc.gpsimd.memset(ident[:, :], 0.0))
        me.mark(nc.gpsimd.memset(tri[:, :], 1.0))
        nc.gpsimd.memset(ones[:, :], 1.0)
        me.mark(nc.gpsimd.memset(lower_half[:, :], 0.0))
        nc.gpsimd.memset(mhalf[:, :], -0.5)
        nc.gpsimd.memset(running[:, :, :, :], 0.0)
        nc.gpsimd.memset(table[:, :, :, :], 0.0)
        nc.gpsimd.memset(zrow[:, :], 0.0).then_inc(s_zrow, 1)
        me.after()
        nc.gpsimd.affine_select(out=ident[:, :], in_=ident[:, :], compare_op=ALU.not_equal, fill=1.0, base=0,
                                pattern=[[-1, P]], channel_multiplier=1)
        nc.gpsimd.affine_select(out=tri[:, :], in_=tri[:, :], compare_op=ALU.is_gt, fill=0.0, base=0,
                                pattern=[[1, P]], channel_multiplier=-1)
        nc.gpsimd.affine_select(out=lower_half[:, :], in_=lower_half[:, :], compare_op=ALU.is_ge, fill=1.0, base=R2 - 1,
                                pattern=[[0, 1]], channel_multiplier=-1)
        nc.gpsimd.iota(iota[:, :], pattern=[[1, P]], base=0, channel_multiplier=0, allow_small_or_imprecise_dtypes=True)
        me.mark(nc.gpsimd.iota(token[:, :], pattern=[[P, GB]], base=1, channel_multiplier=1,
                               allow_small_or_imprecise_dtypes=True))
        me.after()
        nc.gpsimd.tensor_scalar(token[:, :], token[:, :], 0.0, None, ALU.add).then_inc(s_consts, 1)

        def copy(out_, in_):
            return nc.gpsimd.tensor_scalar(out_, in_, 1.0, 0.0, ALU.mult, ALU.add)

        def rstd(var_mv, var, r, ready, value, out_sem):
            pool.wait_ge(ready, value)
            pass_gate(pool, s_pool_gate)
            me.mark(nc.gpsimd.tensor_scalar(var[:, :], var_mv[:, :, 1], EPS, None, ALU.add))
            me.after()
            nc.gpsimd.tensor_tensor(r[:, :], var[:, :], mhalf[:, :], ALU.pow).then_inc(out_sem, 1)

        def split_cv(n):
            pool.wait_ge(s_c_in, 48 * (n + 1))
            pass_gate(pool, s_pool_gate)
            copy(cv_h[:, :], c_raw[:, 0, :])
            me.mark(copy(c_tmp[:, :], c_raw[:, 1, :]))
            me.after()
            nc.gpsimd.tensor_tensor(cv_l[:, :], c_raw[:, 0, :], cv_h[:, :].bitcast(f32), ALU.subtract)
            me.mark(nc.gpsimd.tensor_scalar(c_tmp[:, :], c_tmp[:, :].bitcast(f32), lower_half[:, 0:1], 0.0, ALU.mult, ALU.add))
            me.after()
            nc.gpsimd.tensor_tensor(cv_d[:, :], c_raw[:, 1, :], c_tmp[:, :].bitcast(f32),
                                    ALU.subtract).then_inc(s_cv_ready, 1)

        def copy_ck():
            pass_gate(pool, s_pool_gate)
            copy(ck_h[:, :], cv_h[:, :].bitcast(f32))
            copy(ck_l[:, :], cv_l[:, :].bitcast(f32))
            copy(ck_d[:, :], cv_d[:, :].bitcast(f32)).then_inc(s_ck_ready, 1)

        rstd(mv1, var1, rstd1, s_stats1, 1, s_rstd1)
        split_cv(0)
        pool.wait_ge(s_cv_ready, 1)
        copy_ck()
        pool.wait_ge(s_w_hi, 4)
        nc.gpsimd.tensor_tensor(wo_l[:, :, :], w2_raw[:, :, :], wo_h[:, :, :].bitcast(f32), ALU.subtract).then_inc(s_wo_lo, 1)

        def iteration(g, has_prev, has_cur):
            if has_prev:
                pool.wait_ge(s_xr_in, 16 * g)
                pool.wait_ge(s_bias_o, 1)
                for b in range(GB):
                    last = nc.gpsimd.tensor_tensor(xr[:, b, :], xr[:, b, :], bias_o[:, :], ALU.add)
                last.then_inc(s_xr_ready, 1)
                rstd(mv2, var2, rstd2, s_stats2, g, s_rstd2)
            if has_cur:
                rstd(mv1, var1, rstd1, s_stats1, g + 2, s_rstd1)
                pool.wait_ge(s_v_ready, 8 * g + 8)
                split_cv(g + 1)
            if has_prev and has_cur:
                pool.wait_ge(s_slot_ready, g)
                pool.wait_ge(s_xn2_out, 16 * g)
                pass_gate(pool, s_pool_gate)
                last = onehots(nc.gpsimd)
                me.mark(last)
                me.after()
                pass_gate(pool, s_pool_gate)
                nc.gpsimd.tensor_scalar(token[:, :], token[:, :], float(TOK), None, ALU.add).then_inc(s_onehot, 1)
            if not has_cur:
                for n, (raw, h, l) in enumerate(((w1_raw, wq_h, wq_l), (w2_raw, wo_h, wo_l))):
                    pool.wait_ge(s_e0_hi, n + 1)
                    nc.gpsimd.tensor_tensor(l[:, :, :], raw[:, :, :], h[:, :, :].bitcast(f32), ALU.subtract).then_inc(s_e0_lo, 1)
            if has_cur:
                pool.wait_ge(s_k_ready, 8 * g + 8)
                pool.wait_ge(s_cv_ready, g + 2)
                copy_ck()

        pool.wait_ge(s_consts, 1)
        iteration(0, False, True)
        start = me.n
        per = 5
        with pool.Fori(1, NG) as g:
            me.enter((g - 1) * per + start)
            iteration(g, True, True)
            assert me.n == per, me.n
        me.enter(start + (NG - 1) * per)
        iteration(NG, True, False)

    @block.tensor
    def _(pe):
        mm = nc.tensor.matmul
        pe.wait_ge(s_consts, 1)

        def take_bank(job, jobs, g):
            n = jobs.index(job)
            if n >= 2:
                pe.wait_ge(*done(jobs[n - 2], g))
            elif isinstance(g, int) and g == 0:
                pe.wait_ge(s_v_done, GB - 1 + n)
            else:
                pe.wait_ge(s_tb_done, 2 * g - 1 + n)
            return proj[n % 2]

        def values(bank, b, half):
            cols, keys = slice(half * HALF, (half + 1) * HALF), slice(b * P, (b + 1) * P)
            mm(bank[:, :], cv_h[:, keys], wv_h[:, cols], start=True, stop=False)
            mm(bank[:, :], cv_h[:, keys], wv_l[:, cols], start=False, stop=False)
            mm(bank[:, :], cv_l[:, keys], wv_h[:, cols], start=False, stop=False)
            mm(bank[:, :], cv_d[:, keys], wv_d[:, cols], start=False, stop=False)
            mm(bank[:, :], cv_d[0:R2, keys], wv_e[:, cols], start=False, stop=True).then_inc(s_v_ready, 1)

        def front(bank, k):
            for b in range(GB):
                last = nc.tensor.transpose(bank[:, b * P:(b + 1) * P], xn[:, b, k * P:(k + 1) * P], ident[:, :])
            last.then_inc(s_f_ready, 1)

        def transpose_probs(u):
            for hh in range(2):
                pe.wait_ge(s_p_ready, 2 * u + hh + 1)
                if not isinstance(u, int) or u > 0:
                    pe.wait_ge((s_pt_done0, s_pt_done1)[hh], u)
                for b in range(GB):
                    last = nc.tensor.transpose(probT[hh][:, b * P:(b + 1) * P], probs[:, hh * GB + b, :], ident[:, :])
                last.then_inc(s_pt_ready, 1)

        def weigh_values(u, j, v_needed):
            pe.wait_ge(s_v_done, v_needed)
            if not isinstance(u, int) or u > 1:
                pe.wait_ge(s_at_split, u - 1)
            pe.wait_ge(s_pt_done0, u + 1)
            pe.wait_ge(s_pt_done1, u + 1)
            for b in range(GB):
                for hh in range(2):
                    cols = slice((j % 4) * P + hh * DH, (j % 4) * P + (hh + 1) * DH)
                    last = mm(av[j % 2][hh * DH:(hh + 1) * DH, b * P:(b + 1) * P], v_sb[:, j // 4, b, cols],
                              pT[:, hh, b * P:(b + 1) * P], start=True, stop=True)
            last.then_inc(s_av_ready, 1)

        def scores(u):
            pe.wait_ge(s_q_done, u + 1)
            pe.wait_ge(s_k_done, u + 1)
            if not isinstance(u, int) or u > 0:
                pe.wait_ge(s_exp, 2 * u)
            for b in range(GB):
                for hh in range(2):
                    r, t = slice(hh * DH, (hh + 1) * DH), slice(b * P, (b + 1) * P)
                    last = mm(score[hh][:, t], q_sb[r, t], k_sb[r, t], start=True, stop=True)
                    if b == GB - 1:
                        last.then_inc(s_s_ready, 1)

        def project_out(bank, g, b0):
            pe.wait_ge(s_at_split, 8 * g)
            pe.wait_ge(s_wo_lo, 1)
            for i in range(2):
                o, t = bank[:, i * D:(i + 1) * D], slice((b0 + i) * P, (b0 + i + 1) * P)
                for j in range(NP):
                    mm(o, aT_h[:, j, t], wo_h[:, j, :], start=(j == 0), stop=False)
                    mm(o, aT_h[:, j, t], wo_l[:, j, :], start=False, stop=False)
                    last = mm(o, aT_l[:, j, t], wo_h[:, j, :], start=False, stop=(j == NP - 1))
            last.then_inc(s_o_ready, 1)

        def misc(kind, bank, g):
            if kind in ("O0", "O1"):
                project_out(bank, g, 0 if kind == "O0" else 2)
            elif kind in ("XA", "XB"):
                pe.wait_ge(s_xn2_ready, g)
                k = 0 if kind == "XA" else 1
                for b in range(GB):
                    last = nc.tensor.transpose(bank[:, b * P:(b + 1) * P], xn2[:, b, k * P:(k + 1) * P], ident[:, :])
                last.then_inc(s_xt_ready, 1)
            elif kind == "LG":
                pe.wait_ge(s_xt_done, 2 * g)
                for b in range(GB):
                    for k in range(DK):
                        last = mm(bank[:, b * E:(b + 1) * E], xn2T[:, k, b * P:(b + 1) * P], gate_sb[:, k, :],
                                  start=(k == 0), stop=(k == DK - 1))
                last.then_inc(s_lg_ready, 1)
            elif kind == "PR":
                pe.wait_ge(s_mask_ready, g)
                flat = mask[:, :, :, :].rearrange("p j b e -> p (j b e)")
                mm(bank[:, 0:64], tri[:, :], flat, start=True, stop=True)
                mm(bank[:, 64:128], ones[:, :], flat, start=True, stop=True).then_inc(s_pr_ready, 1)
            elif kind in ("T0", "T1"):
                pe.wait_ge(s_onehot, g)
                j = int(kind[1])
                for b in range(GB):
                    last = mm(bank[:, 0:2 * NHI], onehot_lo[:, j * GB + b, :], hi_vals[:, j * GB + b, :],
                              start=(b == 0), stop=(b == GB - 1))
                last.then_inc(s_tb_ready, 1)
            else:
                if kind == "FA":
                    pe.wait_ge(s_xn_ready, g + 2)
                front(bank, 0 if kind == "FA" else 1)

        pe.wait_ge(s_xn_ready, 1)
        for k in range(DK):
            front(proj[k], k)
        pe.wait_ge(s_w_lo, 1)
        pe.wait_ge(s_cv_ready, 1)
        for b in range(GB):
            if b < 2:
                pe.wait_ge(s_f_split, b + 1)
            else:
                pe.wait_ge(s_v_done, b - 1)
            values(proj[b % 2], b, 0)

        def iteration(g, has_prev, has_cur):
            jobs = jobs_of(has_prev, has_cur)
            for j in range(NP):
                u = 8 * g + j
                if has_cur:
                    bank = take_bank(("Q", j), jobs, g)
                    if j == 0:
                        pe.wait_ge(s_f_split, 2 * g + 2)
                        pe.wait_ge(s_w_lo, 2)
                    c = slice(j * P, (j + 1) * P)
                    for k in range(DK):
                        mm(bank[:, :], wq_h[:, k, c], xT_h[:, k, :], start=(k == 0), stop=False)
                        mm(bank[:, :], wq_h[:, k, c], xT_l[:, k, :], start=False, stop=False)
                        last = mm(bank[:, :], wq_l[:, k, c], xT_h[:, k, :], start=False, stop=(k == DK - 1))
                    last.then_inc(s_q_ready, 1)
                if has_cur:
                    bank = take_bank(("K", j), jobs, g)
                    if j == 0:
                        pe.wait_ge(s_ck_ready, g + 1)
                        pe.wait_ge(s_w_lo, 3)
                    mm(bank[:, :], wk_h[:, c], ck_h[:, :], start=True, stop=False)
                    mm(bank[:, :], wk_h[:, c], ck_l[:, :], start=False, stop=False)
                    mm(bank[:, :], wk_l[:, c], ck_h[:, :], start=False, stop=False)
                    mm(bank[:, :], wk_d[:, c], ck_d[:, :], start=False, stop=False)
                    mm(bank[:, :], wk_e[:, c], ck_d[0:R2, :], start=False, stop=True).then_inc(s_k_ready, 1)
                    if j == NP - 1:
                        misc("FA", take_bank(("FA", 0), jobs, g), g)
                        misc("FB", take_bank(("FB", 0), jobs, g), g)
                        transpose_probs(u - 1)
                    bank = take_bank(("V", j), jobs, g)
                    if j == 4:
                        pe.wait_ge(s_cv_ready, g + 2)
                    values(bank, j % 4, 1 if j < 4 else 0)
                prev_unit = (has_cur and j > 0) or (has_prev and j == 0)
                if prev_unit and j < NP - 1:
                    transpose_probs(u - 1)
                if has_cur:
                    scores(u)
                if prev_unit:
                    jp = (j - 1) % NP
                    v_needed = 8 * g + (8 if 4 <= jp and j else 4) if j else 8 * g
                    weigh_values(u - 1, jp, v_needed)
                for kind in MISC_PREV.get(j, []) if has_prev else []:
                    misc(kind, take_bank((kind, 0), jobs, g), g)

        iteration(0, False, True)
        with pe.Fori(1, NG) as g:
            iteration(g, True, True)
        iteration(NG, True, False)

    @block.scalar
    def _(act):
        def high(out_, in_, scale=1.0):
            return nc.scalar.activation(out_, in_, ACT.Copy, scale=scale)

        act.wait_ge(s_wv_in, 48)
        high(wv_h[:, :], wv_raw[:, 0:INNER])
        high(wv_d[:, :], wv_raw[:, INNER:2 * INNER]).then_inc(s_w_hi, 1)
        for k in range(DK):
            act.wait_ge(s_f_ready, k + 1)
            high(xT_h[:, k, :], proj[k][:, :]).then_inc(s_f_hi, 1)
        act.wait_ge(s_wq_in, 16)
        high(wq_h[:, :, :], w1_raw[:, :, :], SCALE).then_inc(s_w_hi, 1)
        act.wait_ge(s_wk_in, 48)
        high(wk_h[:, :], wk_raw[:, 0:INNER])
        high(wk_d[:, :], wk_raw[:, INNER:2 * INNER]).then_inc(s_w_hi, 1)
        act.wait_ge(s_small_in, 64)
        nc.scalar.activation(tanh_g[:, :], tanh_g[:, :], ACT.Tanh).then_inc(s_tanh, 1)
        act.wait_ge(s_wo_in, 16)
        high(wo_h[:, :, :], w2_raw[:, :, :]).then_inc(s_w_hi, 1)

        def iteration(g, has_prev, has_cur):
            jobs = jobs_of(has_prev, has_cur)
            for j in range(NP):
                u = 8 * g + j
                if has_cur:
                    act.wait_ge(s_q_ready, u + 1)
                    high(q_sb[:, :], bank_of(("Q", j), jobs)[:, :]).then_inc(s_q_done, 1)
                if (has_prev and (has_cur or j < 2)) or (has_cur and j >= 2):
                    act.wait_ge(s_av_ready, u - 1)
                    high(aT_h[:, (j - 2) % NP, :], av[j % 2][:, :]).then_inc(s_at_hi, 1)
                if has_cur:
                    act.wait_ge(s_k_ready, u + 1)
                    high(k_sb[:, :], bank_of(("K", j), jobs)[:, :]).then_inc(s_k_done, 1)
                if has_cur and j == NP - 1:
                    for k in range(DK):
                        act.wait_ge(s_f_ready, 2 * g + 3 + k)
                        high(xT_h[:, k, :], bank_of(("FA" if k == 0 else "FB", 0), jobs)[:, :]).then_inc(s_f_hi, 1)
                if has_prev and j == 4:
                    act.wait_ge(s_gdiff, g)
                    nc.scalar.activation(gexp[:, :], gdiff[:, :], ACT.Exp).then_inc(s_gexp, 1)
                prev_unit = (has_cur and j > 0) or (has_prev and j == 0)
                if prev_unit:
                    act.wait_ge(s_pt_ready, 2 * u - 1)
                    high(pT[:, 0, :], probT[0][:, :]).then_inc(s_pt_done0, 1)
                if has_cur:
                    for hh in range(2):
                        act.wait_ge(s_negmax, 2 * u + 1 + hh)
                        for b in range(GB):
                            c = hh * GB + b
                            last = nc.scalar.activation(probs[:, c, :], score[hh][:, b * P:(b + 1) * P], ACT.Exp,
                                                        bias=negmax[:, j % 2, c:c + 1], accum_out=sums[:, j % 2, c:c + 1])
                        last.then_inc(s_exp, 1)
                if not has_cur and j == 1:
                    act.wait_ge(s_e0_in, 32)
                    high(wq_h[:, :, :], w1_raw[:, :, :]).then_inc(s_e0_hi, 1)
                    act.wait_ge(s_o_ready, 2 * g)
                    high(wo_h[:, :, :], w2_raw[:, :, :]).then_inc(s_e0_hi, 1)

        iteration(0, False, True)
        with act.Fori(1, NG) as g:
            iteration(g, True, True)
        iteration(NG, True, False)

    @block.vector
    def _(dve):
        me = Steps(dve, s_dve_self)
        V = nc.vector

        def low(out_, full, high_):
            return V.tensor_tensor(out_, full, high_.bitcast(f32), ALU.subtract)

        def row_stats(src, st, batches):
            for b in batches:
                last = me.mark(V.bn_stats(st[:, b, :], src[:, b, :]))
            return last

        def stats(src, st, mv, out_sem):
            whole_stats(row_stats(src, st, range(GB)), st, mv, out_sem)

        def whole_stats(n, st, mv, out_sem):
            me.after(n)
            pass_gate(dve, s_dve_gate)
            for b in range(GB):
                last = V.bn_aggr(mv[:, b, :], st[:, b, :])
            last.then_inc(out_sem, 1)

        def normalise(dst, src, mv, r, out_sem):
            for b in range(GB):
                last = V.tensor_scalar(dst[:, b, :], src[:, b, :], mv[:, b, 0:1], r[:, b:b + 1], ALU.subtract, ALU.mult)
            last.then_inc(out_sem, 1)

        dve.wait_ge(s_x_in, 16)
        stats(xn, stats1, mv1, s_stats1)
        dve.wait_ge(s_rstd1, 1)
        normalise(xn, xn, mv1, rstd1, s_xn_ready)

        def low_kv(raw, l, h, d, e):
            low(l[:, :], raw[:, 0:INNER], h[:, :])
            low(e[:, :], raw[0:R2, INNER:2 * INNER], d[0:R2, :]).then_inc(s_w_lo, 1)

        def first_values(b):
            dve.wait_ge(s_v_ready, b + 1)
            V.tensor_copy(v_sb[:, 0, b, :], proj[b % 2][:, :]).then_inc(s_v_done, 1)

        dve.wait_ge(s_w_hi, 1)
        low_kv(wv_raw, wv_l, wv_h, wv_d, wv_e)
        for k in range(DK):
            dve.wait_ge(s_f_hi, k + 1)
            low(xT_l[:, k, :], proj[k][:, :], xT_h[:, k, :]).then_inc(s_f_split, 1)
        dve.wait_ge(s_w_hi, 2)
        V.scalar_tensor_tensor(out=wq_l[:, :, :], in0=w1_raw[:, :, :], scalar=SCALE,
                               in1=wq_h[:, :, :].bitcast(f32), op0=ALU.mult, op1=ALU.subtract).then_inc(s_w_lo, 1)
        first_values(0)
        first_values(1)
        dve.wait_ge(s_w_hi, 3)
        low_kv(wk_raw, wk_l, wk_h, wk_d, wk_e)
        first_values(2)
        first_values(3)
        dve.wait_ge(s_tanh, 1)
        V.tensor_scalar(bias_o[:, :], bias_o[:, :], tanh_g[:, 0:1], None, ALU.mult).then_inc(s_bias_o, 1)

        def route_masks(g):
            dve.wait_ge(s_lg_done, g)
            pass_gate(dve, s_dve_gate)
            for b in range(GB):
                n = me.mark(V.max(top[:, b, :], logits[:, b, :]))
            me.after(n)
            n = me.mark(V.tensor_tensor(gdiff[:, :], top[:, :, 1], top[:, :, 0], ALU.subtract))
            for b in range(GB):
                n = me.mark(V.max_index(topi[:, b, :], top[:, b, :], logits[:, b, :]))
            me.after(n)
            n = me.mark(V.tensor_copy(choice[:, :, :], topi[:, :, 0:2].rearrange("p b j -> p j b")))
            me.after(n)
            dve.sem_inc(s_gdiff, 1)
            V.tensor_tensor(mask[:, :, :, :].rearrange("p j b e -> p (j b) e"),
                            iota[:, 0:E].unsqueeze(1).to_broadcast([P, 2 * GB, E]),
                            choice[:, :, :].rearrange("p j b -> p (j b)").unsqueeze(2).to_broadcast([P, 2 * GB, E]),
                            ALU.is_equal).then_inc(s_mask_ready, 1)

        def route_slots(g):
            dve.wait_ge(s_gexp, g)
            n = me.mark(V.tensor_scalar(gden[:, :], gexp[:, :], 1.0, None, ALU.add))
            me.after(n)
            n = me.mark(V.reciprocal(gates[:, 0, :], gden[:, :]))
            me.after(n)
            me.mark(V.tensor_tensor(gates[:, 1, :], gexp[:, :], gates[:, 0, :], ALU.mult))
            n = me.mark(V.tensor_copy(running[:, :, 0, :], running[:, :, GB, :]))
            me.after(n)
            dve.wait_ge(s_pr_done, g)
            pr = ranks[:, :].rearrange("p (w j b e) -> p w j b e", w=2, j=2, b=GB)
            for b in range(GB):
                n = me.mark(V.tensor_tensor(running[:, :, b + 1, :], pr[:, 1, :, b, :], running[:, :, b, :], ALU.add))
                me.after(n)
            n = me.mark(V.tensor_tensor(place[:, :, :, :], pr[:, 0], running[:, :, 0:GB, :], ALU.add))
            me.after(n)
            n = me.mark(V.tensor_tensor(place[:, :, :, :], place[:, :, :, :], mask[:, :, :, :], ALU.mult))
            me.after(n)
            n = me.mark(V.tensor_reduce(loc[:, :, :], place[:, :, :, :], axis=AX, op=ALU.add))
            n = me.mark(V.tensor_scalar(slot[:, 0, :], choice[:, 0, :], float(CAP), None, ALU.mult))
            n = me.mark(V.tensor_scalar(slot[:, 1, :], choice[:, 1, :], float(CAP), float(CAP - 1), ALU.mult, ALU.add))
            me.after(n)
            n = me.mark(V.tensor_scalar(late[:, :, :], loc[:, :, :], float(CAP), BIG, ALU.is_ge, ALU.mult))
            n = me.mark(V.tensor_tensor(slot[:, 0, :], slot[:, 0, :], loc[:, 0, :], ALU.add))
            n = me.mark(V.tensor_tensor(slot[:, 1, :], slot[:, 1, :], loc[:, 1, :], ALU.subtract))
            me.after(n)
            n = me.mark(V.tensor_tensor(sloti[:, :, :], slot[:, :, :], late[:, :, :], ALU.add))
            me.after(n)
            n = me.mark(V.tensor_scalar(hl_i[:, 0], sloti[:, :, :], 7, None, ALU.arith_shift_right))
            n = me.mark(V.tensor_scalar(hl_i[:, 1], sloti[:, :, :], P - 1, None, ALU.bitwise_and))
            me.after(n)
            V.tensor_copy(hl[:, :, :, :], hl_i[:, :, :, :]).then_inc(s_slot_ready, 1)

        def iteration(g, has_prev, has_cur):
            jobs = jobs_of(has_prev, has_cur)
            for j in range(NP):
                u = 8 * g + j
                prev_unit = (has_cur and j > 0) or (has_prev and j == 0)
                if (has_prev and (has_cur or j < 2)) or (has_cur and j >= 2):
                    dve.wait_ge(s_at_hi, u - 1)
                    low(aT_l[:, (j - 2) % NP, :], av[j % 2][:, :], aT_h[:, (j - 2) % NP, :]).then_inc(s_at_split, 1)

                def values_out():
                    dve.wait_ge(s_v_ready, 8 * g + j + GB + 1)
                    if j == 4 or (j == 0 and has_prev):
                        dve.wait_ge(s_av_ready, u)
                    V.tensor_copy(v_sb[:, 1 if j < 4 else 0, j % 4, :], bank_of(("V", j), jobs)[:, :]).then_inc(s_v_done, 1)

                if has_cur and j == NP - 1:
                    for k in range(DK):
                        dve.wait_ge(s_f_hi, 2 * g + 3 + k)
                        low(xT_l[:, k, :], bank_of(("FA" if k == 0 else "FB", 0), jobs)[:, :], xT_h[:, k, :]).then_inc(
                            s_f_split, 1)
                if prev_unit and j == NP - 1:
                    dve.wait_ge(s_pt_ready, 2 * u)
                    V.tensor_copy(pT[:, 1, :], probT[1][:, :]).then_inc(s_pt_done1, 1)
                if has_cur and j % 4:
                    values_out()
                if prev_unit and j < NP - 1:
                    dve.wait_ge(s_pt_ready, 2 * u)
                    V.tensor_copy(pT[:, 1, :], probT[1][:, :]).then_inc(s_pt_done1, 1)
                if has_prev and j == 2:
                    dve.wait_ge(s_rstd2, g)
                    normalise(xn2, x1, mv2, rstd2, s_xn2_ready)
                if has_cur:
                    for hh in range(2):
                        dve.wait_ge(s_s_ready, 2 * u + 1 + hh)
                        V.tensor_reduce(negmax[:, j % 2, hh * GB:(hh + 1) * GB],
                                        score[hh][:, :].rearrange("p (i k) -> p i k", i=GB), axis=AX, op=ALU.max,
                                        negate=True).then_inc(s_negmax, 1)
                    if j % 4 == 0:
                        values_out()
                if has_prev and j == 2:
                    for k in range(DK):
                        dve.wait_ge(s_xt_ready, 2 * g - 1 + k)
                        V.tensor_copy(xn2T[:, k, :], bank_of((("XA", "XB")[k], 0), jobs)[:, :]).then_inc(s_xt_done, 1)
                if has_prev and j == 3:
                    dve.wait_ge(s_lg_ready, g)
                    V.tensor_copy(logits[:, :, :], bank_of(("LG", 0), jobs)[:, 0:GB * E].rearrange(
                        "p (b e) -> p b e", b=GB)).then_inc(s_lg_done, 1)
                if has_prev and j == 4:
                    dve.wait_ge(s_pr_ready, g)
                    V.tensor_copy(ranks[:, :], bank_of(("PR", 0), jobs)[:, 0:4 * GB * E]).then_inc(s_pr_done, 1)
                if has_prev and j == 7:
                    for n in range(2):
                        dve.wait_ge(s_tb_ready, 2 * g - 1 + n)
                        V.tensor_tensor(table[:, n], bank_of((f"T{n}", 0), jobs)[:, 0:2 * NHI].rearrange(
                            "p (w h) -> p w h", w=2), table[:, n], ALU.add).then_inc(s_tb_done, 1)
                if not has_prev and j == 7:
                    dve.wait_ge(s_v_done, NP + GB)
                    dve.wait_ge(s_f_split, 4)
                    dve.sem_inc(s_tb_done, 2)
                if has_cur:
                    for hh in range(2):
                        c = slice(hh * GB, (hh + 1) * GB)
                        dve.wait_ge(s_exp, 2 * u + 1 + hh)
                        n = me.mark(V.reciprocal(rsum[:, c], sums[:, j % 2, c]))
                        me.after(n)
                        V.tensor_tensor(probs[:, c, :], probs[:, c, :], rsum[:, c].unsqueeze(2).to_broadcast([P, GB, P]),
                                        ALU.mult).then_inc(s_p_ready, 1)
                if has_prev and j == 1:
                    dve.wait_ge(s_xr_ready, g)
                    if not isinstance(g, int) or g > 1:
                        dve.wait_ge(s_x1_out, 16 * g - 16)
                    for n in range(2):
                        dve.wait_ge(s_o_ready, 2 * g - 1 + n)
                        V.scalar_tensor_tensor(out=x1[:, 2 * n:2 * n + 2, :],
                                               in0=bank_of((f"O{n}", 0), jobs)[:, :].rearrange("p (b d) -> p b d", b=2),
                                               scalar=tanh_g[:, 0:1], in1=xr[:, 2 * n:2 * n + 2, :], op0=ALU.mult,
                                               op1=ALU.add).then_inc(s_o_done, 1)
                        dve.wait_ge(s_o_done, 2 * g - 1 + n)
                        last = row_stats(x1, stats2, (2 * n, 2 * n + 1))
                    whole_stats(last, stats2, mv2, s_stats2)
                if has_cur and j == 2:
                    dve.wait_ge(s_x_in, 16 * g + 32)
                    stats(xn, stats1, mv1, s_stats1)
                if has_prev and j == 3:
                    route_masks(g)
                if has_prev and j == 4:
                    route_slots(g)
                if not has_cur and j == 4:
                    dve.wait_ge(s_slot_ready, g)
                    dve.wait_ge(s_xn2_out, 16 * g)
                    pass_gate(dve, s_dve_gate)
                    onehots(V).then_inc(s_onehot, 1)
                if has_cur and j == 5:
                    dve.wait_ge(s_rstd1, g + 2)
                    normalise(xn, xn, mv1, rstd1, s_xn_ready)

        iteration(0, False, True)
        start, per = me.n, 53
        with dve.Fori(1, NG) as g:
            me.enter((g - 1) * per + start)
            iteration(g, True, True)
            assert me.n == per, me.n
        me.enter(start + (NG - 1) * per)
        iteration(NG, True, False)


def experts(nc, ctx, sem, out_rows, xn2_dram, fc1T, fc1b, fc2, fc2b, shared):
    f32, f32r, i32, u32 = mybir.dt.float32, mybir.dt.float32r, mybir.dt.int32, mybir.dt.uint32
    ALU, ACT, AX = mybir.AluOpType, mybir.ActivationFunctionType, mybir.AxisListType.X

    def sb(name, shape, dt=f32):
        return ctx.enter_context(nc.sbuf_tensor(name, shape, dt))

    table, running, tanh_g, ident, w1_raw, w2_raw, w1_split, w2_split = shared
    w1_h, w1_l = [w1_split[0], sb("w1_h1", [P, DK, H], f32r)], [w1_split[1], sb("w1_l1", [P, DK, H], f32r)]
    w2_h, w2_l = [w2_split[0], sb("w2_h1", [P, HK, D], f32r)], [w2_split[1], sb("w2_l1", [P, HK, D], f32r)]
    b1 = [sb(f"b1_{n}", [P, HK]) for n in range(2)]
    b2 = [sb(f"b2_{n}", [P, D]) for n in range(2)]
    rows = [sb(f"rows_{n}", [P, GB, D]) for n in range(2)]
    rT_h, rT_l = sb("rT_h", [P, DK, TOK], f32r), sb("rT_l", [P, DK, TOK], f32r)
    hid = [sb(f"hid{n}", [P, TOK]) for n in range(2)]
    hid_h, hid_l = sb("hid_h", [P, HK, TOK], f32r), sb("hid_l", [P, HK, TOK], f32r)
    eo_raw = sb("eo_raw", [P, GB, D])
    eo = [sb(f"eo_{n}", [P, GB, D]) for n in range(2)]
    NCOL = NHI + EH
    rank, keep2, tokf, free = sb("rank", [P, E, EH]), sb("keep2", [P, E, EH]), sb("tokf", [P, NCOL]), sb("free", [P, NHI])
    spare = sb("spare", [P, NHI])
    gate = sb("gate", [P, NHI])
    index = sb("index", [P, NCOL], u32)
    index_e = [sb(f"index_e{n}", [P, EH], u32) for n in range(2)]
    gate_e = [sb(f"gate_e{n}", [P, EH]) for n in range(2)]

    def ps(name):
        return ctx.enter_context(nc.psum_tensor(name, [P, TOK], f32))

    up = [ps("up0"), ps("up1")]
    rT = [ps("rT0"), ps("rT1")]
    down = [ps(f"down{n}") for n in range(GB)]

    (
        s_consts, s_index, s_w_in, s_w_hi, s_w_lo, s_w_raw_free, s_b_in0, s_b_in1, s_gather0, s_gather1,
        s_rt_ready, s_rt_hi, s_rt_split, s_up_ready, s_hid, s_hid_hi, s_hid_split, s_down_ready, s_eo_raw,
        s_eo_raw2, s_eo_ready, s_scatter, s_gate_e, s_index_e, s_out, s_dve_self, s_pool_self, s_dve_gate,
        s_pool_gate, s_rows_free,
    ) = (sem("e_" + name) for name in (
        "consts", "index", "w_in", "w_hi", "w_lo", "w_raw_free", "b_in0", "b_in1", "gather0", "gather1",
        "rt_ready", "rt_hi", "rt_split", "up_ready", "hid", "hid_hi", "hid_split", "down_ready", "eo_raw",
        "eo_raw2", "eo_ready", "scatter", "gate_e", "index_e", "out", "dve_self", "pool_self", "dve_gate",
        "pool_gate", "rows_free",
    ))
    gathers = [s_gather0, s_gather1]
    biases = [s_b_in0, s_b_in1]

    block = ctx.enter_context(nc.Block())
    EB = 2
    TURNS = E // EB

    @block.sync
    def _(sp):
        def load_bias(e, par):
            sp.dma_start(b1[par][:, :], fc1b[bass.ds(e, 1), :, :].rearrange("o p m -> p (o m)")).then_inc(biases[par], 16)
            sp.dma_start(b2[par][:, :], fc2b[bass.ds(e, 1), 0, :].to_broadcast([P, D])).then_inc(biases[par], 16)

        def step(e, nxt, par, first=False):
            if not first:
                sp.wait_ge(s_w_lo, e)
            load_expert(sp, fc1T, fc2, nxt, w1_raw, w2_raw, s_w_in)
            if not first:
                sp.wait_ge(s_eo_raw2, 2 * e)
            load_bias(nxt, 1 - par)

        load_bias(0, 0)
        step(0, 1, 0, True)
        step(1, 2, 1)
        with sp.Fori(1, TURNS - 1) as t:
            for i in range(EB):
                step(EB * t + i, EB * t + i + 1, i)
        step(E - 2, E - 1, 0)
        step(E - 1, E - 1, 1)
        sp.wait_ge(s_w_in, 32 * E)
        sp.wait_ge(biases[0], 32 * (E // 2 + 1))
        sp.wait_ge(biases[1], 32 * (E // 2))
        sp.wait_ge(s_scatter, 16 * NHI)

    @block.gpsimd
    def _(pool):
        me = Steps(pool, s_pool_self)
        nc.gpsimd.iota(rank[:, :, :], pattern=[[0, E], [P, EH]], base=0, channel_multiplier=1,
                       allow_small_or_imprecise_dtypes=True)
        me.mark(nc.gpsimd.iota(spare[:, :], pattern=[[0, NHI]], base=N + 1, channel_multiplier=1,
                               allow_small_or_imprecise_dtypes=True))
        nc.gpsimd.iota(tokf[:, NHI:NCOL], pattern=[[0, EH]], base=N, channel_multiplier=1,
                       allow_small_or_imprecise_dtypes=True)
        me.after()
        nc.gpsimd.memset(eo_raw[:, 0, 0:1], 0.0).then_inc(s_consts, 1)

        def columns(e, par):
            nc.gpsimd.tensor_copy(index_e[par][:, :], index[:, bass.ds(e * EH, EH)]).then_inc(s_index_e, 1)

        def gather(n, par, half):
            pass_gate(pool, s_pool_gate)
            for i in range(GB):
                pool.indirect_dma_start(
                    out=rows[half][:, i, :], out_offset=None, in_=xn2_dram[:, :],
                    in_offset=bass.IndirectOffsetOnAxis(ap=index_e[par][:, half * GB + i:half * GB + i + 1], axis=0),
                    bounds_check=N + PAD - 1, oob_is_err=False).then_inc(gathers[half], 16)

        def scatter(n, par, half):
            if half == 0 and not (isinstance(n, int) and n == 0):
                pool.wait_ge(s_scatter, 16 * GB * n)
            for i in range(GB):
                pool.wait_ge(s_eo_ready, GB * n + i + 1)
                pass_gate(pool, s_pool_gate)
                pool.indirect_dma_start(
                    out=out_rows[:, :], out_offset=bass.IndirectOffsetOnAxis(
                        ap=index_e[par][:, half * GB + i:half * GB + i + 1], axis=0),
                    in_=eo[half][:, i, :], in_offset=None, bounds_check=N - 1, oob_is_err=False,
                    compute_op=ALU.add).then_inc(s_scatter, 16)

        def split_low(e, par):
            pool.wait_ge(s_w_hi, 2 * e - 1)
            for k in range(DK):
                nc.gpsimd.tensor_tensor(w1_l[par][:, k, :], w1_raw[:, k, :], w1_h[par][:, k, :].bitcast(f32), ALU.subtract)
            pool.wait_ge(s_w_hi, 2 * e)
            nc.gpsimd.tensor_tensor(w2_l[par][:, :, :], w2_raw[:, :, :], w2_h[par][:, :, :].bitcast(f32),
                                    ALU.subtract).then_inc(s_w_lo, 1)

        pool.wait_ge(s_index, 1)
        columns(0, 0)
        pool.wait_ge(s_index_e, 1)
        gather(0, 0, 0)
        gather(1, 0, 1)

        def step(e, par):
            split_low(e + 1, 1 - par)
            if not (isinstance(e, int) and e == 0):
                pool.wait_ge(s_scatter, 16 * EH * e)
                pass_gate(pool, s_pool_gate)
            columns(e + 1, 1 - par)
            pool.wait_ge(s_index_e, e + 2)
            for half in range(2):
                n = 2 * e + half
                pool.wait_ge(s_rt_ready, 2 * n + 2)
                gather(n + 2, 1 - par, half)
                scatter(n, par, half)

        step(0, 0)
        step(1, 1)
        with pool.Fori(1, TURNS) as t:
            for i in range(EB):
                step(EB * t + i, i)
        for half in range(2):
            pool.wait_ge(gathers[half], 16 * GB * (E + 1))
        pool.wait_ge(s_scatter, 16 * NHI)

    @block.tensor
    def _(pe):
        mm = nc.tensor.matmul
        pe.wait_ge(s_consts, 1)

        def transpose_rows(n, half):
            pe.wait_ge(gathers[half], n)
            for k in range(DK):
                for b in range(GB):
                    last = nc.tensor.transpose(rT[k][:, b * P:(b + 1) * P], rows[half][:, b, k * P:(k + 1) * P], ident[:, :])
                last.then_inc(s_rt_ready, 1)

        def group(n, e, par, half):
            for m in range(HK):
                if not (isinstance(n, int) and n == 0 and m < 2):
                    pe.wait_ge(s_hid, 8 * n + m - 1)
                if m == 0:
                    pe.wait_ge(s_rt_split, 2 * n + 2)
                    if not (isinstance(e, int) and e == 0):
                        pe.wait_ge(s_w_lo, e)
                c = slice(m * P, (m + 1) * P)
                for k in range(DK):
                    mm(up[m % 2][:, :], w1_h[par][:, k, c], rT_h[:, k, :], start=(k == 0), stop=False)
                    mm(up[m % 2][:, :], w1_h[par][:, k, c], rT_l[:, k, :], start=False, stop=False)
                    last = mm(up[m % 2][:, :], w1_l[par][:, k, c], rT_h[:, k, :], start=False, stop=(k == DK - 1))
                last.then_inc(s_up_ready, 1)
            transpose_rows(16 * GB * (e + 1) if half == 0 else 16 * GB * (e + 2), 1 - half)
            for k in range(HK):
                pe.wait_ge(s_hid_split, 8 * n + k + 1)
                for i in range(GB):
                    if k == 0 and not (isinstance(n, int) and n == 0):
                        pe.wait_ge(s_eo_raw, 4 * n - 3 + i)
                    t = slice(i * P, (i + 1) * P)
                    o = down[i][:, 0:D]
                    mm(o, hid_h[:, k, t], w2_h[par][:, k, :], start=(k == 0), stop=False)
                    mm(o, hid_h[:, k, t], w2_l[par][:, k, :], start=False, stop=False)
                    last = mm(o, hid_l[:, k, t], w2_h[par][:, k, :], start=False, stop=(k == HK - 1))
                    if k == HK - 1:
                        last.then_inc(s_down_ready, 1)

        transpose_rows(16 * GB, 0)
        for n in range(2 * EB):
            group(n, n // 2, n // 2, n % 2)
        with pe.Fori(1, TURNS) as t:
            for i in range(2 * EB):
                group(2 * EB * t + i, EB * t + i // 2, i // 2, i % 2)

    @block.scalar
    def _(act):
        def split_high(e, par):
            act.wait_ge(s_w_in, 32 * e)
            nc.scalar.activation(w1_h[par][:, :, :], w1_raw[:, :, :], ACT.Copy).then_inc(s_w_hi, 1)
            nc.scalar.activation(w2_h[par][:, :, :], w2_raw[:, :, :], ACT.Copy).then_inc(s_w_hi, 1)

        def high_rows(n):
            for k in range(DK):
                act.wait_ge(s_rt_ready, 2 * n + k + 1)
                nc.scalar.activation(rT_h[:, k, :], rT[k][:, :], ACT.Copy).then_inc(s_rt_hi, 1)

        def group(n, e, par, half):
            if half == 0:
                act.wait_ge(biases[par], 16 * (e - par) + 32)
            for m in range(HK):
                act.wait_ge(s_up_ready, 8 * n + m + 1)
                if not (isinstance(n, int) and n == 0 and m < 2):
                    act.wait_ge(s_hid_split, 8 * n + m - 1)
                nc.scalar.activation(hid[m % 2][:, :], up[m % 2][:, :], ACT.Relu, bias=b1[par][:, m:m + 1]).then_inc(s_hid, 1)
            high_rows(n + 1)
            if half == 0:
                split_high(e + 1, 1 - par)
            if not (isinstance(n, int) and n < 2):
                act.wait_ge(s_scatter, 64 * n - 64)
            for i in range(GB):
                act.wait_ge(s_eo_raw, 4 * n + i + 1)
                nc.scalar.activation(eo[half][:, i, :], eo_raw[:, i, :], ACT.Copy,
                                     scale=gate_e[par][:, half * GB + i:half * GB + i + 1]).then_inc(s_eo_ready, 1)

        high_rows(0)
        for n in range(2 * EB):
            group(n, n // 2, n // 2, n % 2)
        with act.Fori(1, TURNS) as t:
            for i in range(2 * EB):
                group(2 * EB * t + i, EB * t + i // 2, i // 2, i % 2)

    @block.vector
    def _(dve):
        me = Steps(dve, s_dve_self)
        V = nc.vector
        dve.wait_ge(s_consts, 1)
        n = me.mark(V.tensor_tensor(keep2[:, :, :], rank[:, :, :],
                                    running[:, 0, GB, :].unsqueeze(2).to_broadcast([P, E, EH]), ALU.is_ge))
        me.after(n)
        k2 = keep2[:, :, :].rearrange("p e h -> p (e h)")
        n = me.mark(V.tensor_tensor(tokf[:, 0:NHI], table[:, 1, 0, :], k2, ALU.mult))
        n = me.mark(V.tensor_tensor(gate[:, :], table[:, 1, 1, :], k2, ALU.mult))
        me.after(n)
        n = me.mark(V.tensor_tensor(tokf[:, 0:NHI], tokf[:, 0:NHI], table[:, 0, 0, :], ALU.add))
        n = me.mark(V.tensor_tensor(gate[:, :], gate[:, :], table[:, 0, 1, :], ALU.add))
        me.after(n)
        n = me.mark(V.tensor_scalar(free[:, :], tokf[:, 0:NHI], 0.0, None, ALU.is_equal))
        n = me.mark(V.tensor_scalar(gate[:, :], gate[:, :], tanh_g[:, 1:2], None, ALU.mult))
        me.after(n)
        n = me.mark(V.tensor_tensor(free[:, :], free[:, :], spare[:, :], ALU.mult))
        me.after(n)
        n = me.mark(V.scalar_tensor_tensor(out=tokf[:, 0:NHI], in0=tokf[:, 0:NHI], scalar=-1.0, in1=free[:, :],
                                           op0=ALU.add, op1=ALU.add))
        me.after(n)
        V.tensor_copy(index[:, :], tokf[:, :]).then_inc(s_index, 1)

        def low_rows(n):
            for k in range(DK):
                dve.wait_ge(s_rt_hi, 2 * n + k + 1)
                V.tensor_tensor(rT_l[:, k, :], rT[k][:, :], rT_h[:, k, :].bitcast(f32), ALU.subtract).then_inc(s_rt_split, 1)

        def group(n, e, par, half):
            if half == 0:
                dve.wait_ge(biases[par], 16 * (e - par) + 32)
                V.tensor_copy(gate_e[par][:, :], gate[:, bass.ds(e * EH, EH)])
            for m in range(HK):
                dve.wait_ge(s_hid, 8 * n + m + 1)
                V.tensor_copy(hid_h[:, m, :], hid[m % 2][:, :]).then_inc(s_hid_hi, 1)
                dve.wait_ge(s_hid_hi, 8 * n + m + 1)
                V.tensor_tensor(hid_l[:, m, :], hid[m % 2][:, :], hid_h[:, m, :].bitcast(f32),
                                ALU.subtract).then_inc(s_hid_split, 1)
            low_rows(n + 1)
            for i in range(GB):
                dve.wait_ge(s_down_ready, 4 * n + i + 1)
                if not (isinstance(n, int) and n == 0):
                    dve.wait_ge(s_eo_ready, GB * n - GB + i + 1)
                V.tensor_tensor(eo_raw[:, i, :], down[i][:, 0:D], b2[par][:, :], ALU.add).then_inc(s_eo_raw, 1)
            dve.wait_ge(s_eo_raw, 4 * n + 4)
            dve.sem_inc(s_eo_raw2, 1)

        low_rows(0)
        for n in range(2 * EB):
            group(n, n // 2, n // 2, n % 2)
        with dve.Fori(1, TURNS) as t:
            for i in range(2 * EB):
                group(2 * EB * t + i, EB * t + i // 2, i // 2, i % 2)


def kernel(**inputs):
    import numpy as _np
    import concourse.bacc as _bacc
    from concourse import mybir as _mybir
    from concourse.bass_utils import run_bass_kernel_spmd as _run

    a = {k: _np.asarray(v) for k, v in inputs.items()}
    arrays = {
        "x": a["x"],
        "ctxT": a["ctx_768"].reshape(N, DE).T,
        "g_x": a["g_xattn"],
        "g_f": a["g_ffn"],
        "wq": a["L0_xattn_Wq"], "wk": a["L0_xattn_Wk"], "wv": a["L0_xattn_Wv"], "wo": a["L0_xattn_Wo"],
        "bo": a["L0_xattn_bo"],
        "gateT": a["L0_ffn_gate_w"].T,
        "fc1T": a["L0_ffn_fc1_w"].transpose(0, 2, 1),
        "fc1b": a["L0_ffn_fc1_b"].reshape(E, HK, P).transpose(0, 2, 1),
        "fc2": a["L0_ffn_fc2_w"],
        "fc2b": a["L0_ffn_fc2_b"],
    }
    arrays = {f"{k}_dram": _np.ascontiguousarray(v) for k, v in arrays.items()}
    nc = _bacc.Bacc("TRN2", target_bir_lowering=False, num_devices=1)
    args = [nc.dram_tensor(k, v.shape, _mybir.dt.from_np(v.dtype), kind="ExternalInput").ap() for k, v in arrays.items()]
    out = nc.dram_tensor("out_dram", (B, S, D), _mybir.dt.float32, kind="ExternalOutput").ap()
    gated_block(nc, *args, out)
    r = _run(nc, [arrays], core_ids=[0])
    return r.results[0]["out_dram"]
```

```python
import concourse.bass as bass
from concourse import mybir
from contextlib import ExitStack

P = 128
B, S, D, DE = 32, 128, 256, 192
HEADS, DH = 16, 64
INNER = HEADS * DH
E, H = 8, 1024
N = B * S
CAP = 2 * ((N + E - 1) // E)
EPS = 1e-5
SCALE = 1.0 / 8.0

GB = 4
NG = B // GB
TOK = GB * S
NP = HEADS // 2
DK = D // P
HALF = INNER // 2
R2 = DE - P
HK = H // P
NHI = E * CAP // P
EH = CAP // P
PAD = 1
BIG = 65536.0
V_AHEAD = 2


def pass_gate(eng, sem):
    eng.sem_inc(sem, 1)


class Steps:

    def __init__(self, eng, sem):
        self.eng, self.sem, self.base, self.n = eng, sem, 0, 0

    def mark(self, ins):
        ins.then_inc(self.sem, 1)
        self.n += 1
        return self.n

    def after(self, n=None):
        self.eng.wait_ge(self.sem, self.base + (self.n if n is None else n))

    def enter(self, base):
        self.base, self.n = base, 0


MISC_PREV = {1: ["O0", "O1"], 2: ["XA", "XB"], 3: ["LG"], 4: ["PR"], 7: ["T0", "T1"]}


def jobs_of(has_prev, has_next):
    out = []
    for j in range(NP):
        out += [("Q", j), ("K", j)]
        if has_next or j < NP - V_AHEAD:
            out += [("V", j)]
        if has_next and j == NP - 1:
            out += [("FA", 0), ("FB", 0)]
        if has_prev:
            out += [(m, 0) for m in MISC_PREV.get(j, [])]
    return out


def gated_block(nc, x, ctxT, g_x, g_f, wq, wk, wv, wo, bo, gateT, fc1T, fc1b, fc2, fc2b, out):
    f32 = mybir.dt.float32

    xn2_dram = nc.dram_tensor("xn2_rows", [N + PAD, D], f32, kind="Internal").ap()
    x_v = x.rearrange("b p d -> p b d")
    out_v = out.rearrange("b p d -> p b d")
    out_rows = out.rearrange("b p d -> (b p) d")
    xn2_v = xn2_dram[0:N, :].rearrange("(b p) d -> p b d", p=P)

    with ExitStack() as keep:
        def sem(name):
            return keep.enter_context(nc.semaphore(name))

        table = keep.enter_context(nc.sbuf_tensor("table", [P, 2, 2, NHI], f32))
        running = keep.enter_context(nc.sbuf_tensor("running", [P, 2, GB + 1, E], f32))
        tanh_g = keep.enter_context(nc.sbuf_tensor("tanh_g", [P, 2], f32))
        ident = keep.enter_context(nc.sbuf_tensor("ident", [P, P], f32))
        w1_raw = keep.enter_context(nc.sbuf_tensor("w1_raw", [P, DK, H], f32))
        w2_raw = keep.enter_context(nc.sbuf_tensor("w2_raw", [P, HK, D], f32))
        w1_split = [keep.enter_context(nc.sbuf_tensor(f"w1_split{n}", [P, DK, H], mybir.dt.float32r)) for n in range(2)]
        w2_split = [keep.enter_context(nc.sbuf_tensor(f"w2_split{n}", [P, HK, D], mybir.dt.float32r)) for n in range(2)]
        keep2 = keep.enter_context(nc.sbuf_tensor("keep2", [P, E, EH], f32))
        shared = (keep2, table, running, tanh_g, ident, w1_raw, w2_raw, w1_split, w2_split)

        with ExitStack() as ctx:
            attention(nc, ctx, sem, x_v, out_v, xn2_v, xn2_dram, ctxT, g_x, g_f, wq, wk, wv, wo, bo, gateT, fc1T, fc2, shared)
        with ExitStack() as ctx:
            experts(nc, ctx, sem, out_rows, xn2_dram, fc1T, fc1b, fc2, fc2b, shared)


def keep_warm(nc, bank, lhsT, rhs, count):
    for _ in range(count):
        nc.tensor.matmul(bank[:, 0:rhs.shape[-1]], lhsT, rhs, start=True, stop=True)


def load_expert(sp, fc1T, fc2, e, w1_raw, w2_raw, done_sem):
    sp.dma_start(w1_raw[:, :, :], fc1T[bass.ds(e, 1), :, :].rearrange("o (k p) h -> p (o k) h", p=P)).then_inc(done_sem, 16)
    sp.dma_start(w2_raw[:, :, :], fc2[bass.ds(e, 1), :, :].rearrange("o (k p) d -> p (o k) d", p=P)).then_inc(done_sem, 16)


def attention(nc, ctx, sem, x_v, out_v, xn2_v, xn2_dram, ctxT, g_x, g_f, wq, wk, wv, wo, bo, gateT, fc1T, fc2, shared):
    f32, f32r, i32, u32 = mybir.dt.float32, mybir.dt.float32r, mybir.dt.int32, mybir.dt.uint32
    ALU, ACT, AX = mybir.AluOpType, mybir.ActivationFunctionType, mybir.AxisListType.X

    def sb(name, shape, dt=f32):
        return ctx.enter_context(nc.sbuf_tensor(name, shape, dt))

    keep2, table, running, tanh_g, ident, w1_raw, w2_raw, w1_split, w2_split = shared
    (wq_h, wq_l), (wo_h, wo_l) = w1_split, w2_split
    wk_h, wk_l, wk_d = (sb(n, [P, INNER], f32r) for n in ("wk_h", "wk_l", "wk_d"))
    wk_e = sb("wk_e", [R2, INNER], f32r)
    wv_h, wv_l, wv_d = (sb(n, [P, INNER], f32r) for n in ("wv_h", "wv_l", "wv_d"))
    wv_e = sb("wv_e", [R2, INNER], f32r)
    v_sb = sb("v_sb", [P, 2, GB, HALF])
    xT_h, xT_l = sb("xT_h", [P, DK, TOK], f32r), sb("xT_l", [P, DK, TOK], f32r)
    cv_h, cv_l, cv_d = (sb(n, [P, TOK], f32r) for n in ("cv_h", "cv_l", "cv_d"))
    ck_h, ck_l, ck_d = (sb(n, [P, TOK], f32r) for n in ("ck_h", "ck_l", "ck_d"))
    c_raw = sb("c_raw", [P, 2, TOK])
    c_tmp = sb("c_tmp", [P, TOK], f32r)
    work = sb("work", [P, 2 * 1024])
    probs = [work[:, 0:1024].rearrange("p (s k) -> p s k", s=8), sb("probs_odd", [P, 2 * GB, P])]
    xn2T = work[:, 1024:2048].rearrange("p (k t) -> p k t", k=DK)
    onehot_lo = work[:, 1024:2048].rearrange("p (s k) -> p s k", s=8)
    rows = sb("rows", [P, 4, GB, D])
    xn, xr, x1, xn2 = (rows[:, n] for n in range(4))
    flat_rows = rows.rearrange("p a b d -> p a (b d)")
    wv_raw, wk_raw = [work[:, 0:INNER], flat_rows[:, 1]], [flat_rows[:, 2], flat_rows[:, 3]]
    hi_vals = rows[:, 3].rearrange("p b (two c) -> p (b two) c", two=2)
    q_sb, k_sb = sb("q_sb", [P, TOK]), sb("k_sb", [P, TOK])
    pT = sb("pT", [P, 2, 2, TOK])
    aT_h, aT_l = sb("aT_h", [P, NP, TOK], f32r), sb("aT_l", [P, NP, TOK], f32r)
    tri, ones, iota = (sb(n, [P, P]) for n in ("tri", "ones", "iota"))
    bias_o = sb("bias_o", [P, D])
    gate_sb = sb("gate_sb", [P, DK, E])
    zrow = sb("zrow", [PAD, D])
    stats1, mv1, rstd1 = sb("stats1", [P, GB, 6]), sb("mv1", [P, GB, 2]), sb("rstd1", [P, GB])
    stats2, mv2, rstd2 = sb("stats2", [P, GB, 6]), sb("mv2", [P, GB, 2]), sb("rstd2", [P, GB])
    var1, var2, mhalf = sb("var1", [P, GB]), sb("var2", [P, GB]), sb("mhalf", [P, GB])
    negmax = sb("negmax", [P, 2, 8])
    sums = sb("sums", [P, 2, 8])
    rsum = sb("rsum", [P, 8])
    logits, top, topi = sb("logits", [P, GB, E]), sb("top", [P, GB, E]), sb("topi", [P, GB, E], u32)
    choice = sb("choice", [P, 2, GB])
    mask = sb("mask", [P, 2, GB, E])
    gates, gdiff, gexp, gden = sb("gates", [P, 2, GB]), sb("gdiff", [P, GB]), sb("gexp", [P, GB]), sb("gden", [P, GB])
    place, loc, late, slot = sb("place", [P, 2, GB, E]), sb("loc", [P, 2, GB]), sb("late", [P, 2, GB]), sb("slot", [P, 2, GB])
    ranks = sb("ranks", [P, 2 * 2 * GB * E])
    sloti, hl_i = sb("sloti", [P, 2, GB], i32), sb("hl_i", [P, 2, 2, GB], i32)
    hl = sb("hl", [P, 2, 2, GB])
    token = sb("token", [P, GB])
    rank = sb("rank", [P, E, EH])
    lower_half = sb("lower_half", [P, 1])

    def ps(name):
        return ctx.enter_context(nc.psum_tensor(name, [P, TOK], f32))

    proj = [ps("proj0"), ps("proj1")]
    score = [ps("score0"), ps("score1")]
    probT = [ps("probT0"), ps("probT1")]
    av = [ps("av0"), ps("av1")]

    (
        s_consts, s_wo_in, s_c_in, s_x_in, s_xr_in, s_small_in, s_zeros_out, s_w_hi,
        s_w_lo, s_tanh, s_bias_o, s_zrow, s_q_ready, s_k_ready, s_v_ready, s_s_ready, s_pt_ready,
        s_av_ready, s_o_ready, s_xt_ready, s_lg_ready, s_pr_ready, s_tb_ready, s_f_ready, s_at_hi,
        s_f_hi, s_q_done, s_k_done, s_v_done, s_pt_done0, s_pt_done1, s_at_split, s_f_split, s_negmax,
        s_exp, s_p_ready, s_o_done, s_xa_done, s_xb_done, s_lg_done, s_pr_done, s_tb_done, s_stats1,
        s_rstd1, s_xn_ready, s_stats2, s_rstd2, s_xn2_ready, s_mask_ready, s_gdiff, s_gexp,
        s_slot_ready, s_onehot0, s_onehot1, s_onehot_last, s_token, s_cv_ready, s_ck_ready, s_xr_ready, s_x1_out, s_xn2_out, s_w_rest,
        s_dve_self, s_pool_self, s_dve_gate, s_pool_gate, s_e0_in, s_c0_hi, s_e0_hi, s_e0_lo,
    ) = (sem("a_" + name) for name in (
        "consts", "wo_in", "c_in", "x_in", "xr_in", "small_in", "zeros_out", "w_hi",
        "w_lo", "tanh", "bias_o", "zrow", "q_ready", "k_ready", "v_ready", "s_ready", "pt_ready",
        "av_ready", "o_ready", "xt_ready", "lg_ready", "pr_ready", "tb_ready", "f_ready", "at_hi",
        "f_hi", "q_done", "k_done", "v_done", "pt_done0", "pt_done1", "at_split", "f_split", "negmax",
        "exp", "p_ready", "o_done", "xa_done", "xb_done", "lg_done", "pr_done", "tb_done", "stats1",
        "rstd1", "xn_ready", "stats2", "rstd2", "xn2_ready", "mask_ready", "gdiff", "gexp",
        "slot_ready", "onehot0", "onehot1", "onehot_last", "token", "cv_ready", "ck_ready", "xr_ready", "x1_out", "xn2_out", "w_rest",
        "dve_self", "pool_self", "dve_gate", "pool_gate", "e0_in", "c0_hi", "e0_hi", "e0_lo",
    ))

    s_wv_in, s_wq_in, s_wk_in = ([sem(f"a_{n}_in{half}") for half in range(2)] for n in ("wv", "wq", "wk"))

    def done(job, g):
        kind, j = job
        return {
            "Q": (s_q_done, 8 * g + j + 1), "K": (s_k_done, 8 * g + j + 1), "V": (s_v_done, 8 * g + j + V_AHEAD + 1),
            "O0": (s_o_done, 2 * g - 1), "O1": (s_o_done, 2 * g), "XA": (s_xa_done, g), "XB": (s_xb_done, g),
            "LG": (s_lg_done, g), "PR": (s_pr_done, g), "T0": (s_tb_done, 2 * g + 1), "T1": (s_tb_done, 2 * g + 2),
            "FA": (s_f_split, 2 * g + 3), "FB": (s_f_split, 2 * g + 4),
        }[kind]

    def bank_of(job, jobs):
        return proj[jobs.index(job) % 2]

    def onehots(engine, j, batches=range(GB)):
        for b in batches:
            n = j * GB + b
            engine.tensor_scalar(onehot_lo[:, n, :], iota[:, :], hl[:, 1, j, b:b + 1], None, ALU.is_equal)
            engine.tensor_scalar(hi_vals[:, n, 0:NHI], iota[:, 0:NHI], hl[:, 0, j, b:b + 1],
                                 token[:, b:b + 1], ALU.is_equal, ALU.mult)
            last = engine.tensor_scalar(hi_vals[:, n, NHI:2 * NHI], iota[:, 0:NHI], hl[:, 0, j, b:b + 1],
                                        gates[:, j, b:b + 1], ALU.is_equal, ALU.mult)
        return last

    block = ctx.enter_context(nc.Block())

    @block.sync
    def _(sp):
        def load_x(g, dst, done_sem):
            sp.dma_start(rows[:, dst], x_v[:, bass.ds(g * GB, GB), :]).then_inc(done_sem, 16)

        def load_ctx(g):
            cols = bass.ds(g * TOK, TOK)
            sp.dma_start(c_raw[:, 0, :], ctxT[0:P, cols]).then_inc(s_c_in, 16)
            sp.dma_start(c_raw[0:R2, 1, :], ctxT[P:DE, cols]).then_inc(s_c_in, 16)
            sp.dma_start(c_raw[R2:P, 1, :], ctxT[P:DE, cols]).then_inc(s_c_in, 16)

        load_x(0, 0, s_x_in)
        load_ctx(0)

        def load_kv(w, dst, half, done_sem):
            cols = slice(half * HALF, (half + 1) * HALF)
            sp.dma_start(dst[:, 0:HALF], w[0:P, cols]).then_inc(done_sem, 16)
            sp.dma_start(dst[0:R2, HALF:INNER], w[P:DE, cols]).then_inc(done_sem, 16)
            sp.dma_start(dst[R2:P, HALF:INNER], w[P:DE, cols]).then_inc(done_sem, 16)

        for half in range(2):
            cols = slice(half * HALF, (half + 1) * HALF)
            load_kv(wv, wv_raw[half], half, s_wv_in[half])
            sp.dma_start(w1_raw[:, :, cols], wq[:, cols].rearrange("(k p) n -> p k n", p=P)).then_inc(s_wq_in[half], 16)
            load_kv(wk, wk_raw[half], half, s_wk_in[half])
        for k, (src, n) in enumerate(((g_x, 0), (g_f, 1))):
            sp.dma_start(tanh_g[:, n:n + 1], src.rearrange("(o n) -> o n", o=1).to_broadcast([P, 1])).then_inc(s_small_in, 16)
        sp.dma_start(bias_o[:, :], bo.rearrange("(o n) -> o n", o=1).to_broadcast([P, D])).then_inc(s_small_in, 16)
        sp.dma_start(gate_sb[:, :, :], gateT.rearrange("(k p) e -> p k e", p=P)).then_inc(s_small_in, 16)
        sp.dma_start(w2_raw[:, :, :], wo.rearrange("(j p) n -> p j n", p=P)).then_inc(s_wo_in, 16)
        sp.wait_ge(s_zrow, 1)
        sp.dma_start(xn2_dram[N:N + PAD, :], zrow[:, :]).then_inc(s_zeros_out, 16)

        def iteration(g, nxt, has_prev):
            if nxt is not None:
                sp.wait_ge(s_f_ready, 2 * g + 2)
                load_x(nxt, 0, s_x_in)
                sp.wait_ge(s_cv_ready, g + 1)
                load_ctx(nxt)
            if has_prev:
                if not isinstance(g, int) or g > 1:
                    sp.wait_ge(s_o_done, 2 * g - 2)
                load_x(g - 1, 1, s_xr_in)
                store(g - 1, g)

        def store(g, whole):
            sp.wait_ge(s_stats2, whole)
            sp.dma_start(out_v[:, bass.ds(g * GB, GB), :], x1).then_inc(s_x1_out, 16)
            sp.wait_ge(s_xn2_ready, whole)
            sp.dma_start(xn2_v[:, bass.ds(g * GB, GB), :], xn2).then_inc(s_xn2_out, 16)

        iteration(0, 1, False)
        sp.wait_ge(s_w_lo, 2)
        sp.wait_ge(s_w_rest, 4)
        load_expert(sp, fc1T, fc2, 0, w1_raw, w2_raw, s_e0_in)
        iteration(1, 2, True)
        with sp.Fori(2, NG - 1) as g:
            iteration(g, g + 1, True)
        iteration(NG - 1, None, True)
        sp.wait_ge(s_o_done, 2 * NG - 2)
        load_x(NG - 1, 1, s_xr_in)
        store(NG - 1, NG + 1)
        sp.wait_ge(s_x1_out, 16 * NG)
        sp.wait_ge(s_xn2_out, 16 * NG)
        sp.wait_ge(s_zeros_out, 16)
        sp.wait_ge(s_x_in, 16 * NG)
        sp.wait_ge(s_c_in, 48 * NG)

    @block.gpsimd
    def _(pool):
        me = Steps(pool, s_pool_self)
        me.mark(nc.gpsimd.memset(ident[:, :], 0.0))
        me.mark(nc.gpsimd.memset(tri[:, :], 1.0))
        nc.gpsimd.memset(ones[:, :], 1.0)
        me.mark(nc.gpsimd.memset(lower_half[:, :], 0.0))
        nc.gpsimd.memset(mhalf[:, :], -0.5)
        nc.gpsimd.memset(running[:, :, :, :], 0.0)
        me.mark(nc.gpsimd.memset(table[:, :, :, :], 0.0))
        nc.gpsimd.memset(zrow[:, :], 0.0).then_inc(s_zrow, 1)
        me.after()
        nc.gpsimd.affine_select(out=ident[:, :], in_=ident[:, :], compare_op=ALU.not_equal, fill=1.0, base=0,
                                pattern=[[-1, P]], channel_multiplier=1)
        nc.gpsimd.affine_select(out=tri[:, :], in_=tri[:, :], compare_op=ALU.is_gt, fill=0.0, base=0,
                                pattern=[[1, P]], channel_multiplier=-1)
        nc.gpsimd.affine_select(out=lower_half[:, :], in_=lower_half[:, :], compare_op=ALU.is_ge, fill=1.0, base=R2 - 1,
                                pattern=[[0, 1]], channel_multiplier=-1)
        nc.gpsimd.iota(iota[:, :], pattern=[[1, P]], base=0, channel_multiplier=0, allow_small_or_imprecise_dtypes=True)
        nc.gpsimd.iota(rank[:, :, :], pattern=[[0, E], [P, EH]], base=0, channel_multiplier=1,
                       allow_small_or_imprecise_dtypes=True)
        nc.gpsimd.memset(table[:, 0, 0, :], float(N))
        me.mark(nc.gpsimd.iota(token[:, :], pattern=[[P, GB]], base=-N, channel_multiplier=1,
                               allow_small_or_imprecise_dtypes=True))
        me.after()
        pool.sem_inc(s_token, 1)
        pool.sem_inc(s_consts, 1)

        def copy(out_, in_):
            return nc.gpsimd.tensor_scalar(out_, in_, 1.0, 0.0, ALU.mult, ALU.add)

        def rstd(var_mv, var, r, ready, value, out_sem, b=slice(0, GB)):
            pool.wait_ge(ready, value)
            pass_gate(pool, s_pool_gate)
            me.mark(nc.gpsimd.tensor_scalar(var[:, b], var_mv[:, b, 1], EPS, None, ALU.add))
            me.after()
            nc.gpsimd.tensor_tensor(r[:, b], var[:, b], mhalf[:, b], ALU.pow).then_inc(out_sem, 1)

        def split_cv(n):
            pool.wait_ge(s_c_in, 48 * (n + 1))
            pass_gate(pool, s_pool_gate)
            if isinstance(n, int) and n == 0:
                pool.wait_ge(s_c0_hi, 1)
            else:
                copy(cv_h[:, :], c_raw[:, 0, :])
                me.mark(copy(c_tmp[:, :], c_raw[:, 1, :]))
                me.after()
            nc.gpsimd.tensor_tensor(cv_l[:, :], c_raw[:, 0, :], cv_h[:, :].bitcast(f32), ALU.subtract)
            me.mark(nc.gpsimd.tensor_scalar(c_tmp[:, :], c_tmp[:, :].bitcast(f32), lower_half[:, 0:1], 0.0, ALU.mult, ALU.add))
            me.after()
            nc.gpsimd.tensor_tensor(cv_d[:, :], c_raw[:, 1, :], c_tmp[:, :].bitcast(f32),
                                    ALU.subtract).then_inc(s_cv_ready, 1)

        def copy_ck():
            pass_gate(pool, s_pool_gate)
            copy(ck_h[:, :], cv_h[:, :].bitcast(f32))
            copy(ck_l[:, :], cv_l[:, :].bitcast(f32))
            copy(ck_d[:, :], cv_d[:, :].bitcast(f32)).then_inc(s_ck_ready, 1)

        rstd(mv1, var1, rstd1, s_stats1, 1, s_rstd1)
        split_cv(0)
        pool.wait_ge(s_cv_ready, 1)
        copy_ck()

        def split(pieces):
            for h, l, full, r in pieces:
                me.mark(copy(h, full))
            me.after()
            for h, l, full, r in pieces:
                last = nc.gpsimd.tensor_tensor(l, full[0:r], h[0:r].bitcast(f32), ALU.subtract)
            last.then_inc(s_w_rest, 1)

        cols = slice(HALF, INNER)
        pool.wait_ge(s_wv_in[1], 48)
        split([(wv_h[:, cols], wv_l[:, cols], wv_raw[1][:, 0:HALF], P), (wv_d[:, cols], wv_e[:, cols], wv_raw[1][:, HALF:INNER], R2)])
        pool.wait_ge(s_wq_in[1], 16)
        split([(wq_h[:, k, cols], wq_l[:, k, cols], w1_raw[:, k, cols], P) for k in range(DK)])
        pool.wait_ge(s_wk_in[1], 48)
        split([(wk_h[:, cols], wk_l[:, cols], wk_raw[1][:, 0:HALF], P), (wk_d[:, cols], wk_e[:, cols], wk_raw[1][:, HALF:INNER], R2)])
        pool.wait_ge(s_wo_in, 16)
        split([(wo_h[:, j, :], wo_l[:, j, :], w2_raw[:, j, :], P) for j in range(NP)])

        def add_bias(g):
            pool.wait_ge(s_xr_in, 16 * g)
            pool.wait_ge(s_bias_o, 1)
            for b in range(GB):
                last = nc.gpsimd.tensor_tensor(xr[:, b, :], xr[:, b, :], bias_o[:, :], ALU.add)
            last.then_inc(s_xr_ready, 1)

        def iteration(g, has_prev, has_next):
            if has_prev:
                add_bias(g)
                rstd(mv2, var2, rstd2, s_stats2, g, s_rstd2)
            if has_next:
                rstd(mv1, var1, rstd1, s_stats1, g + 2, s_rstd1)
                pool.wait_ge(s_v_ready, 8 * g + 8)
                split_cv(g + 1)
            if has_prev:
                pool.wait_ge(s_slot_ready, g)
                pool.wait_ge(s_xn2_out, 16 * g)
                pool.wait_ge(s_token, g)
                pass_gate(pool, s_pool_gate)
                onehots(nc.gpsimd, 0).then_inc(s_onehot0, 1)
                if has_next:
                    onehots(nc.gpsimd, 1, (0, 1, 2)).then_inc(s_onehot1, 1)
                pool.wait_ge(s_onehot0, g)
                pool.wait_ge(s_onehot1, g)
                pool.wait_ge(s_onehot_last, g)
                pass_gate(pool, s_pool_gate)
                nc.gpsimd.tensor_scalar(token[:, :], token[:, :], float(TOK), None, ALU.add).then_inc(s_token, 1)
            if has_next:
                pool.wait_ge(s_k_ready, 8 * g + 8)
                pool.wait_ge(s_cv_ready, g + 2)
                copy_ck()

        def finish():
            add_bias(NG)
            pool.wait_ge(s_e0_hi, 1)
            nc.gpsimd.tensor_tensor(wq_l[:, :, :], w1_raw[:, :, :], wq_h[:, :, :].bitcast(f32), ALU.subtract).then_inc(s_e0_lo, 1)
            for half in range(2):
                rstd(mv2, var2, rstd2, s_stats2, NG + half, s_rstd2, slice(2 * half, 2 * half + 2))
            pool.wait_ge(s_e0_hi, 2)
            nc.gpsimd.tensor_tensor(wo_l[:, :, :], w2_raw[:, :, :], wo_h[:, :, :].bitcast(f32), ALU.subtract).then_inc(s_e0_lo, 1)
            pool.wait_ge(s_slot_ready, NG)
            pool.wait_ge(s_xn2_out, 16 * NG)
            onehots(nc.gpsimd, 1, (2, 3)).then_inc(s_onehot_last, 1)

        pool.wait_ge(s_consts, 1)
        iteration(0, False, True)
        start = me.n
        per = 4
        with pool.Fori(1, NG - 1) as g:
            me.enter((g - 1) * per + start)
            iteration(g, True, True)
            assert me.n == per, me.n
        me.enter(start + (NG - 2) * per)
        iteration(NG - 1, True, False)
        finish()

    @block.tensor
    def _(pe):
        mm = nc.tensor.matmul
        pe.wait_ge(s_consts, 1)

        def take_bank(job, jobs, g):
            n = jobs.index(job)
            if n >= 2:
                pe.wait_ge(*done(jobs[n - 2], g))
            elif isinstance(g, int) and g == 0:
                pe.wait_ge(s_v_done, 1 + n)
            else:
                pe.wait_ge(s_tb_done, 2 * g - 1 + n)
            return proj[n % 2]

        def values(bank, b, half):
            cols, keys = slice(half * HALF, (half + 1) * HALF), slice(b * P, (b + 1) * P)
            mm(bank[:, :], cv_h[:, keys], wv_h[:, cols], start=True, stop=False)
            mm(bank[:, :], cv_h[:, keys], wv_l[:, cols], start=False, stop=False)
            mm(bank[:, :], cv_l[:, keys], wv_h[:, cols], start=False, stop=False)
            mm(bank[:, :], cv_d[:, keys], wv_d[:, cols], start=False, stop=False)
            mm(bank[:, :], cv_d[0:R2, keys], wv_e[:, cols], start=False, stop=True).then_inc(s_v_ready, 1)

        def front(bank, k):
            for b in range(GB):
                last = nc.tensor.transpose(bank[:, b * P:(b + 1) * P], xn[:, b, k * P:(k + 1) * P], ident[:, :])
            last.then_inc(s_f_ready, 1)

        def transpose_probs(u, j):
            for hh in range(2):
                pe.wait_ge(s_p_ready, 2 * u + hh + 1)
                if not isinstance(u, int) or u > 0:
                    pe.wait_ge((s_pt_done0, s_pt_done1)[hh], u)
                for b in range(GB):
                    last = nc.tensor.transpose(probT[hh][:, b * P:(b + 1) * P], probs[j % 2][:, hh * GB + b, :], ident[:, :])
                last.then_inc(s_pt_ready, 1)

        def weigh_values(u, j, v_needed):
            pe.wait_ge(s_v_done, v_needed)
            if not isinstance(u, int) or u > 1:
                pe.wait_ge(s_at_split, u - 1)
            pe.wait_ge(s_pt_done0, u + 1)
            pe.wait_ge(s_pt_done1, u + 1)
            for b in range(GB):
                for hh in range(2):
                    cols = slice((j % 4) * P + hh * DH, (j % 4) * P + (hh + 1) * DH)
                    last = mm(av[j % 2][hh * DH:(hh + 1) * DH, b * P:(b + 1) * P], v_sb[:, j // 4, b, cols],
                              pT[:, j % 2, hh, b * P:(b + 1) * P], start=True, stop=True)
            last.then_inc(s_av_ready, 1)

        def scores(u):
            pe.wait_ge(s_q_done, u + 1)
            pe.wait_ge(s_k_done, u + 1)
            if not isinstance(u, int) or u > 0:
                pe.wait_ge(s_exp, 2 * u)
            for b in range(GB):
                for hh in range(2):
                    r, t = slice(hh * DH, (hh + 1) * DH), slice(b * P, (b + 1) * P)
                    last = mm(score[hh][:, t], q_sb[r, t], k_sb[r, t], start=True, stop=True)
                    if b == GB - 1:
                        last.then_inc(s_s_ready, 1)

        def project_out(bank, g, b0):
            pe.wait_ge(s_w_rest, 4)
            pe.wait_ge(s_at_split, 8 * g - 1)
            for i in range(2):
                o, t = bank[:, i * D:(i + 1) * D], slice((b0 + i) * P, (b0 + i + 1) * P)
                for j in range(NP):
                    if i == 0 and j == NP - 1:
                        pe.wait_ge(s_at_split, 8 * g)
                    mm(o, aT_h[:, j, t], wo_h[:, j, :], start=(j == 0), stop=False)
                    mm(o, aT_h[:, j, t], wo_l[:, j, :], start=False, stop=False)
                    last = mm(o, aT_l[:, j, t], wo_h[:, j, :], start=False, stop=(j == NP - 1))
            last.then_inc(s_o_ready, 1)

        def misc(kind, bank, g):
            if kind in ("O0", "O1"):
                project_out(bank, g, 0 if kind == "O0" else 2)
            elif kind in ("XA", "XB"):
                pe.wait_ge(s_xn2_ready, g)
                k = 0 if kind == "XA" else 1
                for b in range(GB):
                    last = nc.tensor.transpose(bank[:, b * P:(b + 1) * P], xn2[:, b, k * P:(k + 1) * P], ident[:, :])
                last.then_inc(s_xt_ready, 1)
            elif kind == "LG":
                pe.wait_ge(s_xa_done, g)
                pe.wait_ge(s_xb_done, g)
                for b in range(GB):
                    for k in range(DK):
                        last = mm(bank[:, b * E:(b + 1) * E], xn2T[:, k, b * P:(b + 1) * P], gate_sb[:, k, :],
                                  start=(k == 0), stop=(k == DK - 1))
                last.then_inc(s_lg_ready, 1)
            elif kind == "PR":
                pe.wait_ge(s_mask_ready, g)
                flat = mask[:, :, :, :].rearrange("p j b e -> p (j b e)")
                mm(bank[:, 0:64], tri[:, :], flat, start=True, stop=True)
                mm(bank[:, 64:128], ones[:, :], flat, start=True, stop=True).then_inc(s_pr_ready, 1)
            elif kind in ("T0", "T1"):
                j = int(kind[1])
                pe.wait_ge((s_onehot0, s_onehot1)[j], g)
                if j == 1:
                    pe.wait_ge(s_onehot_last, g)
                for b in range(GB):
                    last = mm(bank[:, 0:2 * NHI], onehot_lo[:, j * GB + b, :], hi_vals[:, j * GB + b, :],
                              start=(b == 0), stop=(b == GB - 1))
                last.then_inc(s_tb_ready, 1)
            else:
                if kind == "FA":
                    pe.wait_ge(s_xn_ready, g + 2)
                front(bank, 0 if kind == "FA" else 1)

        keep_warm(nc, av[1], ident[:, :], ident[:, :], 16)
        pe.wait_ge(s_xn_ready, 1)
        for k in range(DK):
            front(proj[k], k)
        pe.wait_ge(s_w_lo, 1)
        pe.wait_ge(s_cv_ready, 1)
        for b in range(V_AHEAD):
            pe.wait_ge(s_f_split, b + 1)
            values(proj[b % 2], b, 0)

        def iteration(g, has_prev, has_next):
            jobs = jobs_of(has_prev, has_next)
            for j in range(NP):
                u = 8 * g + j
                bank = take_bank(("Q", j), jobs, g)
                if j == 0:
                    pe.wait_ge(s_f_split, 2 * g + 2)
                    pe.wait_ge(s_w_lo, 2)
                if j == NP // 2:
                    pe.wait_ge(s_w_rest, 3)
                c = slice(j * P, (j + 1) * P)
                for k in range(DK):
                    mm(bank[:, :], wq_h[:, k, c], xT_h[:, k, :], start=(k == 0), stop=False)
                    mm(bank[:, :], wq_h[:, k, c], xT_l[:, k, :], start=False, stop=False)
                    last = mm(bank[:, :], wq_l[:, k, c], xT_h[:, k, :], start=False, stop=(k == DK - 1))
                last.then_inc(s_q_ready, 1)
                bank = take_bank(("K", j), jobs, g)
                if j == 0:
                    pe.wait_ge(s_ck_ready, g + 1)
                    pe.wait_ge(s_w_lo, 3)
                mm(bank[:, :], wk_h[:, c], ck_h[:, :], start=True, stop=False)
                mm(bank[:, :], wk_h[:, c], ck_l[:, :], start=False, stop=False)
                mm(bank[:, :], wk_l[:, c], ck_h[:, :], start=False, stop=False)
                mm(bank[:, :], wk_d[:, c], ck_d[:, :], start=False, stop=False)
                mm(bank[:, :], wk_e[:, c], ck_d[0:R2, :], start=False, stop=True).then_inc(s_k_ready, 1)
                if ("V", j) in jobs:
                    bank = take_bank(("V", j), jobs, g)
                    n = (j + V_AHEAD) % NP
                    if n == 0:
                        pe.wait_ge(s_cv_ready, g + 2)
                    if n == GB:
                        pe.wait_ge(s_w_rest, 1)
                    values(bank, n % GB, n // GB)
                scores(u)
                if has_next and j == NP - 1:
                    misc("FA", take_bank(("FA", 0), jobs, g), g)
                    misc("FB", take_bank(("FB", 0), jobs, g), g)
                if has_prev or j > 0:
                    transpose_probs(u - 1, (j - 1) % NP)
                todo = MISC_PREV.get(j, []) if has_prev else []
                if todo == ["XA", "XB"]:
                    misc("XA", take_bank(("XA", 0), jobs, g), g)
                    todo = ["XB"]
                if has_prev or j > 1:
                    jp = (j - 2) % NP
                    v_needed = 8 * g + (0 if j < 2 else 4 if jp < 4 else 8)
                    weigh_values(u - 2, jp, v_needed)
                for kind in todo:
                    misc(kind, take_bank((kind, 0), jobs, g), g)

        def wait_warm(count):
            keep_warm(nc, av[1], wk_h[:, 0:P], wk_h[:, 0:TOK], count)

        def finish():
            u = 8 * NG
            transpose_probs(u - 1, NP - 1)
            weigh_values(u - 2, NP - 2, u)
            weigh_values(u - 1, NP - 1, u)
            for half in range(2):
                pe.wait_ge(s_tb_done, 2 * NG - 1 + half)
                project_out(proj[half], NG, 2 * half)
            for half in range(2):
                pe.wait_ge(s_xn2_ready, NG + half)
                pe.wait_ge(s_exp, 16 * NG)
                for k in range(DK):
                    for b in range(2):
                        last = nc.tensor.transpose(score[half][:, (2 * k + b) * P:(2 * k + b + 1) * P],
                                                   xn2[:, 2 * half + b, k * P:(k + 1) * P], ident[:, :])
                last.then_inc(s_xt_ready, 1)
                if half == 0:
                    pe.wait_ge(s_at_split, 8 * NG)
                wait_warm(3)
                pe.wait_ge(s_xa_done, NG + half)
                pe.wait_ge((s_pt_done0, s_pt_done1)[half], 8 * NG)
                for b in range(2):
                    for k in range(DK):
                        last = mm(probT[half][:, b * E:(b + 1) * E], xn2T[:, k, (2 * half + b) * P:(2 * half + b + 1) * P],
                                  gate_sb[:, k, :], start=(k == 0), stop=(k == DK - 1))
                last.then_inc(s_lg_ready, 1)
                wait_warm(6)
            misc("PR", av[0], NG)
            wait_warm(24)
            for half in range(2):
                pe.wait_ge(s_o_done, 2 * NG - 1 + half)
                misc(f"T{half}", proj[half], NG)

        iteration(0, False, True)
        with pe.Fori(1, NG - 1) as g:
            iteration(g, True, True)
        iteration(NG - 1, True, False)
        finish()

    @block.scalar
    def _(act):
        def high(out_, in_, scale=1.0):
            return nc.scalar.activation(out_, in_, ACT.Copy, scale=scale)

        act.wait_ge(s_c_in, 48)
        high(cv_h[:, :], c_raw[:, 0, :])
        high(c_tmp[:, :], c_raw[:, 1, :]).then_inc(s_c0_hi, 1)
        act.wait_ge(s_wv_in[0], 48)
        high(wv_h[:, 0:HALF], wv_raw[0][:, 0:HALF])
        high(wv_d[:, 0:HALF], wv_raw[0][:, HALF:INNER]).then_inc(s_w_hi, 1)
        for k in range(DK):
            act.wait_ge(s_f_ready, k + 1)
            high(xT_h[:, k, :], proj[k][:, :]).then_inc(s_f_hi, 1)
        act.wait_ge(s_wq_in[0], 16)
        high(wq_h[:, :, 0:HALF], w1_raw[:, :, 0:HALF]).then_inc(s_w_hi, 1)
        act.wait_ge(s_wk_in[0], 48)
        high(wk_h[:, 0:HALF], wk_raw[0][:, 0:HALF])
        high(wk_d[:, 0:HALF], wk_raw[0][:, HALF:INNER]).then_inc(s_w_hi, 1)
        act.wait_ge(s_small_in, 64)
        nc.scalar.activation(tanh_g[:, :], tanh_g[:, :], ACT.Tanh).then_inc(s_tanh, 1)

        def attention_high(u, j):
            act.wait_ge(s_av_ready, u + 1)
            high(aT_h[:, j % NP, :], av[j % 2][:, :]).then_inc(s_at_hi, 1)

        def iteration(g, has_prev, has_next):
            jobs = jobs_of(has_prev, has_next)
            for j in range(NP):
                u = 8 * g + j
                act.wait_ge(s_q_ready, u + 1)
                high(q_sb[:, :], bank_of(("Q", j), jobs)[:, :], SCALE).then_inc(s_q_done, 1)
                act.wait_ge(s_k_ready, u + 1)
                high(k_sb[:, :], bank_of(("K", j), jobs)[:, :]).then_inc(s_k_done, 1)
                if j > 2 or (has_prev and j < 2):
                    attention_high(u - 3, j - 3)
                if has_next and j == NP - 1:
                    for k in range(DK):
                        act.wait_ge(s_f_ready, 2 * g + 3 + k)
                        high(xT_h[:, k, :], bank_of(("FA" if k == 0 else "FB", 0), jobs)[:, :]).then_inc(s_f_hi, 1)
                if has_prev and j == 4:
                    act.wait_ge(s_gdiff, g)
                    nc.scalar.activation(gexp[:, :], gdiff[:, :], ACT.Exp).then_inc(s_gexp, 1)
                for hh in range(2):
                    act.wait_ge(s_negmax, 2 * u + 1 + hh)
                    for b in range(GB):
                        c = hh * GB + b
                        last = nc.scalar.activation(probs[j % 2][:, c, :], score[hh][:, b * P:(b + 1) * P], ACT.Exp,
                                                    bias=negmax[:, j % 2, c:c + 1], accum_out=sums[:, j % 2, c:c + 1])
                    last.then_inc(s_exp, 1)
                    if hh == 0 and has_prev and j == 2:
                        act.wait_ge(s_xt_ready, 2 * g - 1)
                        high(xn2T[:, 0, :], bank_of(("XA", 0), jobs)[:, :]).then_inc(s_xa_done, 1)
                    if hh == 0 and has_prev and j == 1:
                        attention_high(u - 2, j - 2)

        def finish():
            for n in range(3, 0, -1):
                attention_high(8 * NG - n, -n)
            act.wait_ge(s_e0_in, 32)
            high(wq_h[:, :, :], w1_raw[:, :, :]).then_inc(s_e0_hi, 1)
            for half in range(2):
                act.wait_ge(s_xt_ready, 2 * (NG - 1) + 1 + half)
                high(xn2T[:, :, half * 2 * P:(half + 1) * 2 * P],
                     score[half][:, :].rearrange("p (k t) -> p k t", k=DK)).then_inc(s_xa_done, 1)
                if half == 0:
                    act.wait_ge(s_o_ready, 2 * NG)
                    high(wo_h[:, :, :], w2_raw[:, :, :]).then_inc(s_e0_hi, 1)
            act.wait_ge(s_gdiff, NG)
            nc.scalar.activation(gexp[:, :], gdiff[:, :], ACT.Exp).then_inc(s_gexp, 1)

        iteration(0, False, True)
        with act.Fori(1, NG - 1) as g:
            iteration(g, True, True)
        iteration(NG - 1, True, False)
        finish()

    @block.vector
    def _(dve):
        me = Steps(dve, s_dve_self)
        V = nc.vector

        def low(out_, full, high_):
            return V.tensor_tensor(out_, full, high_.bitcast(f32), ALU.subtract)

        def row_stats(src, st, batches):
            for b in batches:
                last = me.mark(V.bn_stats(st[:, b, :], src[:, b, :]))
            return last

        def stats(src, st, mv, out_sem):
            whole_stats(row_stats(src, st, range(GB)), st, mv, out_sem)

        def whole_stats(n, st, mv, out_sem, batches=range(GB)):
            me.after(n)
            pass_gate(dve, s_dve_gate)
            for b in batches:
                last = V.bn_aggr(mv[:, b, :], st[:, b, :])
            last.then_inc(out_sem, 1)

        def normalise(dst, src, mv, r, out_sem, batches=range(GB)):
            for b in batches:
                last = V.tensor_scalar(dst[:, b, :], src[:, b, :], mv[:, b, 0:1], r[:, b:b + 1], ALU.subtract, ALU.mult)
            last.then_inc(out_sem, 1)

        dve.wait_ge(s_x_in, 16)
        stats(xn, stats1, mv1, s_stats1)
        dve.wait_ge(s_rstd1, 1)
        normalise(xn, xn, mv1, rstd1, s_xn_ready)

        def low_kv(raw, l, h, d, e):
            low(l[:, 0:HALF], raw[:, 0:HALF], h[:, 0:HALF])
            low(e[:, 0:HALF], raw[0:R2, HALF:INNER], d[0:R2, 0:HALF]).then_inc(s_w_lo, 1)

        def first_values(b):
            dve.wait_ge(s_v_ready, b + 1)
            V.tensor_copy(v_sb[:, 0, b, :], proj[b % 2][:, :]).then_inc(s_v_done, 1)

        dve.wait_ge(s_w_hi, 1)
        low_kv(wv_raw[0], wv_l, wv_h, wv_d, wv_e)
        for k in range(DK):
            dve.wait_ge(s_f_hi, k + 1)
            low(xT_l[:, k, :], proj[k][:, :], xT_h[:, k, :]).then_inc(s_f_split, 1)
        dve.wait_ge(s_w_hi, 2)
        low(wq_l[:, :, 0:HALF], w1_raw[:, :, 0:HALF], wq_h[:, :, 0:HALF]).then_inc(s_w_lo, 1)
        first_values(0)
        dve.wait_ge(s_w_hi, 3)
        low_kv(wk_raw[0], wk_l, wk_h, wk_d, wk_e)
        first_values(1)
        dve.wait_ge(s_tanh, 1)
        V.tensor_scalar(bias_o[:, :], bias_o[:, :], tanh_g[:, 0:1], None, ALU.mult).then_inc(s_bias_o, 1)

        def route_masks(g):
            pass_gate(dve, s_dve_gate)
            for b in range(GB):
                n = me.mark(V.max(top[:, b, :], logits[:, b, :]))
            me.after(n)
            n = me.mark(V.tensor_tensor(gdiff[:, :], top[:, :, 1], top[:, :, 0], ALU.subtract))
            for b in range(GB):
                n = me.mark(V.max_index(topi[:, b, :], top[:, b, :], logits[:, b, :]))
            me.after(n)
            n = me.mark(V.tensor_copy(choice[:, :, :], topi[:, :, 0:2].rearrange("p b j -> p j b")))
            me.after(n)
            dve.sem_inc(s_gdiff, 1)
            V.tensor_tensor(mask[:, :, :, :].rearrange("p j b e -> p (j b) e"),
                            iota[:, 0:E].unsqueeze(1).to_broadcast([P, 2 * GB, E]),
                            choice[:, :, :].rearrange("p j b -> p (j b)").unsqueeze(2).to_broadcast([P, 2 * GB, E]),
                            ALU.is_equal).then_inc(s_mask_ready, 1)

        def route_counts(g):
            dve.wait_ge(s_gexp, g)
            n = me.mark(V.tensor_scalar(gden[:, :], gexp[:, :], 1.0, None, ALU.add))
            me.after(n)
            n = me.mark(V.reciprocal(gates[:, 0, :], gden[:, :]))
            me.after(n)
            me.mark(V.tensor_tensor(gates[:, 1, :], gexp[:, :], gates[:, 0, :], ALU.mult))
            n = me.mark(V.tensor_copy(running[:, :, 0, :], running[:, :, GB, :]))
            me.after(n)
            dve.wait_ge(s_pr_done, g)
            pr = ranks[:, :].rearrange("p (w j b e) -> p w j b e", w=2, j=2, b=GB)
            for b in range(GB):
                n = me.mark(V.tensor_tensor(running[:, :, b + 1, :], pr[:, 1, :, b, :], running[:, :, b, :], ALU.add))
                me.after(n)

        def route_slots():
            pr = ranks[:, :].rearrange("p (w j b e) -> p w j b e", w=2, j=2, b=GB)
            n = me.mark(V.tensor_tensor(place[:, :, :, :], pr[:, 0], running[:, :, 0:GB, :], ALU.add))
            me.after(n)
            n = me.mark(V.tensor_tensor(place[:, :, :, :], place[:, :, :, :], mask[:, :, :, :], ALU.mult))
            me.after(n)
            n = me.mark(V.tensor_reduce(loc[:, :, :], place[:, :, :, :], axis=AX, op=ALU.add))
            n = me.mark(V.tensor_scalar(slot[:, 0, :], choice[:, 0, :], float(CAP), None, ALU.mult))
            n = me.mark(V.tensor_scalar(slot[:, 1, :], choice[:, 1, :], float(CAP), float(CAP - 1), ALU.mult, ALU.add))
            me.after(n)
            n = me.mark(V.tensor_scalar(late[:, :, :], loc[:, :, :], float(CAP), BIG, ALU.is_ge, ALU.mult))
            n = me.mark(V.tensor_tensor(slot[:, 0, :], slot[:, 0, :], loc[:, 0, :], ALU.add))
            n = me.mark(V.tensor_tensor(slot[:, 1, :], slot[:, 1, :], loc[:, 1, :], ALU.subtract))
            me.after(n)
            n = me.mark(V.tensor_tensor(sloti[:, :, :], slot[:, :, :], late[:, :, :], ALU.add))
            me.after(n)
            n = me.mark(V.tensor_scalar(hl_i[:, 0], sloti[:, :, :], 7, None, ALU.arith_shift_right))
            n = me.mark(V.tensor_scalar(hl_i[:, 1], sloti[:, :, :], P - 1, None, ALU.bitwise_and))
            me.after(n)
            V.tensor_copy(hl[:, :, :, :], hl_i[:, :, :, :]).then_inc(s_slot_ready, 1)

        def small_out(g, j, jobs):
            if j == 3:
                dve.wait_ge(s_lg_ready, g)
                V.tensor_copy(logits[:, :, :], bank_of(("LG", 0), jobs)[:, 0:GB * E].rearrange(
                    "p (b e) -> p b e", b=GB)).then_inc(s_lg_done, 1)
            if j == 4:
                dve.wait_ge(s_pr_ready, g)
                V.tensor_copy(ranks[:, :], bank_of(("PR", 0), jobs)[:, 0:4 * GB * E]).then_inc(s_pr_done, 1)

        def attention_low(u, j):
            dve.wait_ge(s_at_hi, u + 1)
            low(aT_l[:, j % NP, :], av[j % 2][:, :], aT_h[:, j % NP, :]).then_inc(s_at_split, 1)

        def probs_out(u, j):
            for hh, pt_done in enumerate((s_pt_done0, s_pt_done1)):
                dve.wait_ge(s_pt_ready, 2 * u + 1 + hh)
                V.tensor_copy(pT[:, j % 2, hh, :], probT[hh][:, :]).then_inc(pt_done, 1)

        def residual_start(g):
            dve.wait_ge(s_xr_ready, g)
            if not isinstance(g, int) or g > 1:
                dve.wait_ge(s_x1_out, 16 * g - 16)

        def residual(g, bank, n):
            dve.wait_ge(s_o_ready, 2 * g - 1 + n)
            V.scalar_tensor_tensor(out=x1[:, 2 * n:2 * n + 2, :], in0=bank[:, :].rearrange("p (b d) -> p b d", b=2),
                                   scalar=tanh_g[:, 0:1], in1=xr[:, 2 * n:2 * n + 2, :], op0=ALU.mult,
                                   op1=ALU.add).then_inc(s_o_done, 1)
            dve.wait_ge(s_o_done, 2 * g - 1 + n)
            return row_stats(x1, stats2, (2 * n, 2 * n + 1))

        def iteration(g, has_prev, has_next):
            jobs = jobs_of(has_prev, has_next)
            for j in range(NP):
                u = 8 * g + j
                if ("V", j) in jobs:
                    n = (j + V_AHEAD) % NP
                    dve.wait_ge(s_v_ready, u + V_AHEAD + 1)
                    if n == 0 or (n == GB and has_prev):
                        dve.wait_ge(s_av_ready, u - 2)
                    V.tensor_copy(v_sb[:, n // GB, n % GB, :], bank_of(("V", j), jobs)[:, :]).then_inc(s_v_done, 1)
                if j > 2 or (has_prev and j < 2):
                    attention_low(u - 3, j - 3)
                if has_prev and j == 2:
                    dve.wait_ge(s_rstd2, g)
                    normalise(xn2, x1, mv2, rstd2, s_xn2_ready)
                for hh in range(2):
                    dve.wait_ge(s_s_ready, 2 * u + 1 + hh)
                    V.tensor_reduce(negmax[:, j % 2, hh * GB:(hh + 1) * GB],
                                    score[hh][:, :].rearrange("p (i k) -> p i k", i=GB), axis=AX, op=ALU.max,
                                    negate=True).then_inc(s_negmax, 1)
                if has_next and j == NP - 1:
                    for k in range(DK):
                        dve.wait_ge(s_f_hi, 2 * g + 3 + k)
                        low(xT_l[:, k, :], bank_of(("FA" if k == 0 else "FB", 0), jobs)[:, :], xT_h[:, k, :]).then_inc(
                            s_f_split, 1)
                if has_prev or j > 0:
                    probs_out(u - 1, j - 1)
                if has_prev and j == 5:
                    route_slots()
                if has_prev and j == 2:
                    dve.wait_ge(s_xt_ready, 2 * g)
                    V.tensor_copy(xn2T[:, 1, :], bank_of(("XB", 0), jobs)[:, :]).then_inc(s_xb_done, 1)
                if has_prev and j == 7:
                    for n in range(2):
                        dve.wait_ge(s_tb_ready, 2 * g - 1 + n)
                        V.tensor_tensor(table[:, n], bank_of((f"T{n}", 0), jobs)[:, 0:2 * NHI].rearrange(
                            "p (w h) -> p w h", w=2), table[:, n], ALU.add).then_inc(s_tb_done, 1)
                if not has_prev and j == 7:
                    dve.wait_ge(s_v_done, NP + V_AHEAD)
                    dve.wait_ge(s_f_split, 4)
                    dve.sem_inc(s_tb_done, 2)
                for hh in range(2):
                    c = slice(hh * GB, (hh + 1) * GB)
                    dve.wait_ge(s_exp, 2 * u + 1 + hh)
                    n = me.mark(V.reciprocal(rsum[:, c], sums[:, j % 2, c]))
                    me.after(n)
                    V.tensor_tensor(probs[j % 2][:, c, :], probs[j % 2][:, c, :],
                                    rsum[:, c].unsqueeze(2).to_broadcast([P, GB, P]), ALU.mult).then_inc(s_p_ready, 1)
                    if hh == 0 and has_prev and j == 1:
                        attention_low(u - 2, j - 2)
                    if hh == 0 and has_prev:
                        small_out(g, j, jobs)
                if has_prev and j == 1:
                    residual_start(g)
                    for n in range(2):
                        last = residual(g, bank_of((f"O{n}", 0), jobs), n)
                    whole_stats(last, stats2, mv2, s_stats2)
                if has_next and j == 2:
                    dve.wait_ge(s_x_in, 16 * g + 32)
                    stats(xn, stats1, mv1, s_stats1)
                if has_prev and j == 3:
                    dve.wait_ge(s_lg_done, g)
                    route_masks(g)
                if has_prev and j == 4:
                    route_counts(g)
                if has_prev and j == 6:
                    dve.wait_ge(s_slot_ready, g)
                    dve.wait_ge(s_xn2_out, 16 * g)
                    dve.wait_ge(s_token, g)
                    pass_gate(dve, s_dve_gate)
                    if not has_next:
                        onehots(V, 1, (0, 1, 2)).then_inc(s_onehot1, 1)
                    onehots(V, 1, (3,)).then_inc(s_onehot_last, 1)
                if has_next and j == 6:
                    dve.wait_ge(s_rstd1, g + 2)
                    normalise(xn, xn, mv1, rstd1, s_xn_ready)

        def finish():
            attention_low(8 * NG - 3, -3)
            probs_out(8 * NG - 1, -1)
            for n in (2, 1):
                attention_low(8 * NG - n, -n)
            residual_start(NG)
            last = residual(NG, proj[0], 0)
            whole_stats(last, stats2, mv2, s_stats2, (0, 1))
            dve.wait_ge(s_rstd2, NG)
            normalise(xn2, x1, mv2, rstd2, s_xn2_ready, (0, 1))
            last = residual(NG, proj[1], 1)
            whole_stats(last, stats2, mv2, s_stats2, (2, 3))
            dve.wait_ge(s_rstd2, NG + 1)
            normalise(xn2, x1, mv2, rstd2, s_xn2_ready, (2, 3))
            for half in range(2):
                dve.wait_ge(s_lg_ready, NG + half)
                V.tensor_copy(logits[:, 2 * half:2 * half + 2, :],
                              probT[half][:, 0:2 * E].rearrange("p (b e) -> p b e", b=2)).then_inc(s_lg_done, 1)
            dve.wait_ge(s_lg_done, NG + 1)
            route_masks(NG)
            dve.wait_ge(s_pr_ready, NG)
            V.tensor_copy(ranks[:, :], av[0][:, 0:4 * GB * E]).then_inc(s_pr_done, 1)
            route_counts(NG)
            route_slots()
            dve.wait_ge(s_slot_ready, NG)
            dve.wait_ge(s_xn2_out, 16 * NG)
            dve.wait_ge(s_token, NG)
            onehots(V, 0).then_inc(s_onehot0, 1)
            onehots(V, 1, (0, 1)).then_inc(s_onehot1, 1)
            V.tensor_tensor(keep2[:, :, :], rank[:, :, :],
                            running[:, 0, GB, :].unsqueeze(2).to_broadcast([P, E, EH]), ALU.is_ge)
            for n in range(2):
                dve.wait_ge(s_tb_ready, 2 * NG - 1 + n)
                V.tensor_tensor(table[:, n], proj[n][:, 0:2 * NHI].rearrange("p (w h) -> p w h", w=2), table[:, n],
                                ALU.add).then_inc(s_tb_done, 1)

        iteration(0, False, True)
        start, per = me.n, 53
        with dve.Fori(1, NG - 1) as g:
            me.enter((g - 1) * per + start)
            iteration(g, True, True)
            assert me.n == per, me.n
        me.enter(start + (NG - 2) * per)
        iteration(NG - 1, True, False)
        finish()


def experts(nc, ctx, sem, out_rows, xn2_dram, fc1T, fc1b, fc2, fc2b, shared):
    f32, f32r, i32, u32 = mybir.dt.float32, mybir.dt.float32r, mybir.dt.int32, mybir.dt.uint32
    ALU, ACT, AX = mybir.AluOpType, mybir.ActivationFunctionType, mybir.AxisListType.X

    def sb(name, shape, dt=f32):
        return ctx.enter_context(nc.sbuf_tensor(name, shape, dt))

    keep2, table, running, tanh_g, ident, w1_raw, w2_raw, w1_split, w2_split = shared
    w1_h, w1_l = [w1_split[0], sb("w1_h1", [P, DK, H], f32r)], [w1_split[1], sb("w1_l1", [P, DK, H], f32r)]
    w2_h, w2_l = [w2_split[0], sb("w2_h1", [P, HK, D], f32r)], [w2_split[1], sb("w2_l1", [P, HK, D], f32r)]
    b1 = [sb(f"b1_{n}", [P, HK]) for n in range(2)]
    b2 = [sb(f"b2_{n}", [P, D]) for n in range(2)]
    rows = [sb(f"rows_{n}", [P, GB, D]) for n in range(2)]
    rT_h, rT_l = sb("rT_h", [P, DK, TOK], f32r), sb("rT_l", [P, DK, TOK], f32r)
    hid = [sb(f"hid{n}", [P, TOK]) for n in range(2)]
    hid_h, hid_l = sb("hid_h", [P, HK, TOK], f32r), sb("hid_l", [P, HK, TOK], f32r)
    eo_raw = sb("eo_raw", [P, GB, D])
    eo = [sb(f"eo_{n}", [P, GB, D]) for n in range(2)]
    NCOL = NHI + EH
    gate = sb("gate", [P, NHI])
    index = sb("index", [P, NCOL], u32)
    index_e = [sb(f"index_e{n}", [P, EH], u32) for n in range(2)]
    gate_e = [sb(f"gate_e{n}", [P, EH]) for n in range(2)]

    def ps(name):
        return ctx.enter_context(nc.psum_tensor(name, [P, TOK], f32))

    up = [ps("up0"), ps("up1")]
    rT = [ps("rT0"), ps("rT1")]
    down = [ps(f"down{n}") for n in range(GB)]

    (
        s_index, s_w_in, s_w_hi, s_w_lo, s_b_in0, s_b_in1, s_gather0, s_gather1,
        s_rt_ready, s_rt_hi, s_rt_split, s_up_ready, s_hid, s_hid_hi, s_hid_split, s_down_ready, s_eo_raw,
        s_eo_raw2, s_eo_ready, s_scatter0, s_scatter1, s_index_e, s_index_pad, s_dve_self, s_pool_gate,
    ) = (sem("e_" + name) for name in (
        "index", "w_in", "w_hi", "w_lo", "b_in0", "b_in1", "gather0", "gather1",
        "rt_ready", "rt_hi", "rt_split", "up_ready", "hid", "hid_hi", "hid_split", "down_ready", "eo_raw",
        "eo_raw2", "eo_ready", "scatter0", "scatter1", "index_e", "index_pad", "dve_self", "pool_gate",
    ))
    gathers = [s_gather0, s_gather1]
    scatters = [s_scatter0, s_scatter1]
    biases = [s_b_in0, s_b_in1]

    block = ctx.enter_context(nc.Block())
    EB = 2
    TURNS = E // EB

    @block.sync
    def _(sp):
        def load_bias(e, par):
            sp.dma_start(b1[par][:, :], fc1b[bass.ds(e, 1), :, :].rearrange("o p m -> p (o m)")).then_inc(biases[par], 16)
            sp.dma_start(b2[par][:, :], fc2b[bass.ds(e, 1), 0, :].to_broadcast([P, D])).then_inc(biases[par], 16)

        def step(e, nxt, par, first=False):
            if not first:
                sp.wait_ge(s_w_lo, e)
            for half in range(2):
                sp.wait_ge(gathers[half], 16 * GB * (e + 1))
            load_expert(sp, fc1T, fc2, nxt, w1_raw, w2_raw, s_w_in)
            if not first:
                sp.wait_ge(s_eo_raw2, 2 * e)
            load_bias(nxt, 1 - par)

        load_bias(0, 0)
        step(0, 1, 0, True)
        step(1, 2, 1)
        with sp.Fori(1, TURNS - 1) as t:
            for i in range(EB):
                step(EB * t + i, EB * t + i + 1, i)
        step(E - 2, E - 1, 0)
        step(E - 1, E - 1, 1)
        sp.wait_ge(s_w_in, 32 * E)
        sp.wait_ge(biases[0], 32 * (E // 2 + 1))
        sp.wait_ge(biases[1], 32 * (E // 2))
        for half in range(2):
            sp.wait_ge(scatters[half], 16 * GB * E)

    @block.gpsimd
    def _(pool):
        def columns(e, par):
            nc.gpsimd.tensor_copy(index_e[par][:, :], index[:, bass.ds(e * EH, EH)]).then_inc(s_index_e, 1)

        def gather(columns_, half):
            pass_gate(pool, s_pool_gate)
            for i in range(GB):
                pool.indirect_dma_start(
                    out=rows[half][:, i, :], out_offset=None, in_=xn2_dram[:, :],
                    in_offset=bass.IndirectOffsetOnAxis(ap=columns_[:, half * GB + i:half * GB + i + 1], axis=0),
                    bounds_check=N + PAD - 1, oob_is_err=False).then_inc(gathers[half], 16)

        def scatter(n, e, par, half):
            if half == 0 and not (isinstance(e, int) and e == 0):
                for done in scatters:
                    pool.wait_ge(done, 16 * GB * e)
            for i in range(GB):
                pool.wait_ge(s_eo_ready, GB * n + i + 1)
                pass_gate(pool, s_pool_gate)
                pool.indirect_dma_start(
                    out=out_rows[:, :], out_offset=bass.IndirectOffsetOnAxis(
                        ap=index_e[par][:, half * GB + i:half * GB + i + 1], axis=0),
                    in_=eo[half][:, i, :], in_offset=None, bounds_check=N - 1, oob_is_err=False,
                    compute_op=ALU.add).then_inc(scatters[half], 16)

        def split_low(e, par):
            pool.wait_ge(s_w_hi, 2 * e - 1)
            for k in range(DK):
                nc.gpsimd.tensor_tensor(w1_l[par][:, k, :], w1_raw[:, k, :], w1_h[par][:, k, :].bitcast(f32), ALU.subtract)
            pool.wait_ge(s_w_hi, 2 * e)
            nc.gpsimd.tensor_tensor(w2_l[par][:, :, :], w2_raw[:, :, :], w2_h[par][:, :, :].bitcast(f32),
                                    ALU.subtract).then_inc(s_w_lo, 1)

        nc.gpsimd.memset(index[:, NHI:NCOL], N).then_inc(s_index_pad, 1)
        pool.wait_ge(s_index, 1)
        gather(index, 0)
        gather(index, 1)
        pool.wait_ge(s_index_pad, 1)
        columns(0, 0)

        def step(e, par):
            split_low(e + 1, 1 - par)
            if not (isinstance(e, int) and e == 0):
                for done in scatters:
                    pool.wait_ge(done, 16 * GB * e)
                pass_gate(pool, s_pool_gate)
            columns(e + 1, 1 - par)
            pool.wait_ge(s_index_e, e + 2)
            for half in range(2):
                n = 2 * e + half
                pool.wait_ge(s_rt_ready, 2 * n + 2)
                gather(index_e[1 - par], half)
                scatter(n, e, par, half)

        step(0, 0)
        step(1, 1)
        with pool.Fori(1, TURNS) as t:
            for i in range(EB):
                step(EB * t + i, i)
        for half in range(2):
            pool.wait_ge(gathers[half], 16 * GB * (E + 1))
        for done in scatters:
            pool.wait_ge(done, 16 * GB * E)

    @block.tensor
    def _(pe):
        mm = nc.tensor.matmul

        def transpose_rows(gathered, half):
            pe.wait_ge(gathers[half], gathered)
            for k in range(DK):
                for b in range(GB):
                    last = nc.tensor.transpose(rT[k][:, b * P:(b + 1) * P], rows[half][:, b, k * P:(k + 1) * P], ident[:, :])
                last.then_inc(s_rt_ready, 1)

        def group(n, e, par, half):
            for m in range(HK):
                if not (isinstance(n, int) and n == 0 and m < 2):
                    pe.wait_ge(s_hid, 8 * n + m - 1)
                if m == 0:
                    pe.wait_ge(s_rt_split, 2 * n + 2)
                    if not (isinstance(e, int) and e == 0):
                        pe.wait_ge(s_w_lo, e)
                c = slice(m * P, (m + 1) * P)
                for k in range(DK):
                    mm(up[m % 2][:, :], w1_h[par][:, k, c], rT_h[:, k, :], start=(k == 0), stop=False)
                    mm(up[m % 2][:, :], w1_h[par][:, k, c], rT_l[:, k, :], start=False, stop=False)
                    last = mm(up[m % 2][:, :], w1_l[par][:, k, c], rT_h[:, k, :], start=False, stop=(k == DK - 1))
                last.then_inc(s_up_ready, 1)
            transpose_rows(16 * GB * (e + 1) if half == 0 else 16 * GB * (e + 2), 1 - half)
            for k, i in [(k, i) for tiles in ((0, 1), (2,), (3,)) for k in range(HK) for i in tiles]:
                if i == 0:
                    pe.wait_ge(s_hid_split, 8 * n + k + 1)
                if k == 0 and not (isinstance(n, int) and n == 0):
                    pe.wait_ge(s_eo_raw, 4 * n - 3 + i)
                t = slice(i * P, (i + 1) * P)
                o = down[i][:, 0:D]
                mm(o, hid_h[:, k, t], w2_h[par][:, k, :], start=(k == 0), stop=False)
                mm(o, hid_h[:, k, t], w2_l[par][:, k, :], start=False, stop=False)
                last = mm(o, hid_l[:, k, t], w2_h[par][:, k, :], start=False, stop=(k == HK - 1))
                if k == HK - 1:
                    last.then_inc(s_down_ready, 1)

        def wait_warm(count):
            keep_warm(nc, down[0], w1_h[0][:, 0, 0:P], w1_h[0][:, 0, 0:TOK], count)

        wait_warm(26)
        transpose_rows(16 * GB, 0)
        wait_warm(6)
        for n in range(2 * EB):
            group(n, n // 2, n // 2, n % 2)
        with pe.Fori(1, TURNS) as t:
            for i in range(2 * EB):
                group(2 * EB * t + i, EB * t + i // 2, i // 2, i % 2)

    @block.scalar
    def _(act):
        def split_high(e, par):
            act.wait_ge(s_w_in, 32 * e)
            nc.scalar.activation(w1_h[par][:, :, :], w1_raw[:, :, :], ACT.Copy).then_inc(s_w_hi, 1)
            nc.scalar.activation(w2_h[par][:, :, :], w2_raw[:, :, :], ACT.Copy).then_inc(s_w_hi, 1)

        def high_rows(n):
            for k in range(DK):
                act.wait_ge(s_rt_ready, 2 * n + k + 1)
                nc.scalar.activation(rT_h[:, k, :], rT[k][:, :], ACT.Copy).then_inc(s_rt_hi, 1)

        def group(n, e, par, half):
            if half == 0:
                act.wait_ge(biases[par], 16 * (e - par) + 32)
            for m in range(HK):
                act.wait_ge(s_up_ready, 8 * n + m + 1)
                if not (isinstance(n, int) and n == 0 and m < 2):
                    act.wait_ge(s_hid_split, 8 * n + m - 1)
                nc.scalar.activation(hid[m % 2][:, :], up[m % 2][:, :], ACT.Relu, bias=b1[par][:, m:m + 1]).then_inc(s_hid, 1)
            high_rows(n + 1)
            if half == 0:
                split_high(e + 1, 1 - par)
            if not (isinstance(n, int) and n < 2):
                act.wait_ge(scatters[half], 16 * GB * e)
            for i in range(GB):
                act.wait_ge(s_eo_raw, 4 * n + i + 1)
                nc.scalar.activation(eo[half][:, i, :], eo_raw[:, i, :], ACT.Copy,
                                     scale=gate_e[par][:, half * GB + i:half * GB + i + 1]).then_inc(s_eo_ready, 1)

        high_rows(0)
        for n in range(2 * EB):
            group(n, n // 2, n // 2, n % 2)
        with act.Fori(1, TURNS) as t:
            for i in range(2 * EB):
                group(2 * EB * t + i, EB * t + i // 2, i // 2, i % 2)

    @block.vector
    def _(dve):
        me = Steps(dve, s_dve_self)
        V = nc.vector
        k2 = keep2[:, :, :].rearrange("p e h -> p (e h)")
        n = me.mark(V.tensor_tensor(table[:, 1], table[:, 1], k2.unsqueeze(1).to_broadcast([P, 2, NHI]), ALU.mult))
        me.after(n)
        V.tensor_tensor(index[:, 0:NHI], table[:, 1, 0, :], table[:, 0, 0, :], ALU.add).then_inc(s_index, 1)
        n = me.mark(V.tensor_tensor(gate[:, :], table[:, 1, 1, :], table[:, 0, 1, :], ALU.add))
        me.after(n)
        n = me.mark(V.tensor_scalar(gate[:, :], gate[:, :], tanh_g[:, 1:2], None, ALU.mult))
        me.after(n)

        def low_rows(n):
            for k in range(DK):
                dve.wait_ge(s_rt_hi, 2 * n + k + 1)
                V.tensor_tensor(rT_l[:, k, :], rT[k][:, :], rT_h[:, k, :].bitcast(f32), ALU.subtract).then_inc(s_rt_split, 1)

        def group(n, e, par, half):
            if half == 0:
                dve.wait_ge(biases[par], 16 * (e - par) + 32)
                V.tensor_copy(gate_e[par][:, :], gate[:, bass.ds(e * EH, EH)])
            for m in range(HK):
                dve.wait_ge(s_hid, 8 * n + m + 1)
                V.tensor_copy(hid_h[:, m, :], hid[m % 2][:, :]).then_inc(s_hid_hi, 1)
                dve.wait_ge(s_hid_hi, 8 * n + m + 1)
                V.tensor_tensor(hid_l[:, m, :], hid[m % 2][:, :], hid_h[:, m, :].bitcast(f32),
                                ALU.subtract).then_inc(s_hid_split, 1)
            low_rows(n + 1)
            for i in range(GB):
                dve.wait_ge(s_down_ready, 4 * n + i + 1)
                if not (isinstance(n, int) and n == 0):
                    dve.wait_ge(s_eo_ready, GB * n - GB + i + 1)
                V.tensor_tensor(eo_raw[:, i, :], down[i][:, 0:D], b2[par][:, :], ALU.add).then_inc(s_eo_raw, 1)
            dve.wait_ge(s_eo_raw, 4 * n + 4)
            dve.sem_inc(s_eo_raw2, 1)

        low_rows(0)
        for n in range(2 * EB):
            group(n, n // 2, n // 2, n % 2)
        with dve.Fori(1, TURNS) as t:
            for i in range(2 * EB):
                group(2 * EB * t + i, EB * t + i // 2, i // 2, i % 2)


def kernel(**inputs):
    import numpy as _np
    import concourse.bacc as _bacc
    from concourse import mybir as _mybir
    from concourse.bass_utils import run_bass_kernel_spmd as _run

    a = {k: _np.asarray(v) for k, v in inputs.items()}
    arrays = {
        "x": a["x"],
        "ctxT": a["ctx_768"].reshape(N, DE).T,
        "g_x": a["g_xattn"],
        "g_f": a["g_ffn"],
        "wq": a["L0_xattn_Wq"], "wk": a["L0_xattn_Wk"], "wv": a["L0_xattn_Wv"], "wo": a["L0_xattn_Wo"],
        "bo": a["L0_xattn_bo"],
        "gateT": a["L0_ffn_gate_w"].T,
        "fc1T": a["L0_ffn_fc1_w"].transpose(0, 2, 1),
        "fc1b": a["L0_ffn_fc1_b"].reshape(E, HK, P).transpose(0, 2, 1),
        "fc2": a["L0_ffn_fc2_w"],
        "fc2b": a["L0_ffn_fc2_b"],
    }
    arrays = {f"{k}_dram": _np.ascontiguousarray(v) for k, v in arrays.items()}
    nc = _bacc.Bacc("TRN2", target_bir_lowering=False, num_devices=1)
    args = [nc.dram_tensor(k, v.shape, _mybir.dt.from_np(v.dtype), kind="ExternalInput").ap() for k, v in arrays.items()]
    out = nc.dram_tensor("out_dram", (B, S, D), _mybir.dt.float32, kind="ExternalOutput").ap()
    gated_block(nc, *args, out)
    r = _run(nc, [arrays], core_ids=[0])
    return r.results[0]["out_dram"]
```
